# Optimizing a Trainium2 kernel written in Bass

```python
import numpy as np
import jax
import jax.numpy as jnp

def _softmax(x, axis=-1):
    return jax.nn.softmax(x, axis=axis)

def _gelu(x):
    return jax.nn.gelu(x, approximate=True)

def _silu(x):
    return jax.nn.silu(x)

def _sigmoid(x):
    return jax.nn.sigmoid(x)

def _layernorm(x, axis=-1, eps=1e-05):
    m = jnp.mean(x, axis=axis, keepdims=True)
    v = jnp.var(x, axis=axis, keepdims=True)
    return (x - m) / jnp.sqrt(v + eps)

def _scatter_add(tgt, idx, src, axis=0):
    return tgt.at[idx].add(src)

def _segment_sum(src, seg, n):
    return jax.ops.segment_sum(src, seg, n)
kernel_name = 'mk_gnn_resnorm_d4_gnn_r32_e7ddc2'

def setup_inputs(seed: int=0):
    np.random.seed(seed)
    _w = jnp.asarray

    def _rec_inputs():
        import jax
        import jax.numpy as jnp
        _gk = jax.random.key(seed)
        x = -0.0001006 + 1 * jax.random.normal(jax.random.fold_in(_gk, 1), (3125, 96), jnp.float32)
        src = jax.random.randint(jax.random.fold_in(_gk, 2), (50000,), 0, 3125, jnp.int32)
        dst = jnp.minimum((3125 * jax.random.uniform(jax.random.fold_in(_gk, 3), (50000,)) ** 2.0).astype(jnp.int32), 99999)
        _o = jnp.argsort(dst, stable=True)
        src = src[_o]
        dst = dst[_o]
        edge_attr_32 = 0.000196303 + 1.00016 * jax.random.normal(jax.random.fold_in(_gk, 12), (50000, 32), jnp.float32)
        edge_weight = jax.random.uniform(jax.random.fold_in(_gk, 14), (50000,), jnp.float32, 0.0, 0.999998)
        return (x, src, dst, edge_attr_32, edge_weight)
    x, src, dst, edge_attr_32, edge_weight = _rec_inputs()

    def _L0_gnn_setup():
        import jax, jax.numpy as jnp
        import numpy as np
        K = 16
        ALPHA = 0.1
        key = jax.random.key(seed)
        k1, k2 = jax.random.split(key)
        N, E, D = (50000, 25000, 96)
        x = jax.random.normal(k1, (N, D), dtype=jnp.float32)
        edge_index = jax.random.randint(k2, (2, E), 0, N, dtype=jnp.int64)
        return {'x': x, 'edge_index': edge_index}
    _L0_gnn_all = _L0_gnn_setup()
    _L0_gnn_in = {k: v for k, v in _L0_gnn_all.items() if k in ()}
    del _L0_gnn_all

    def _L1_gnn_setup():
        import jax, jax.numpy as jnp
        import numpy as np
        N_NODES = 50000
        N_EDGES = 25000
        D = 96
        DEPTH = 2
        key = jax.random.key(seed)
        ks = jax.random.split(key, 8)
        scale = 1.0 / np.sqrt(D)
        x = jax.random.normal(ks[0], (N_NODES, D), dtype=jnp.float32)
        W0 = jax.random.normal(ks[1], (DEPTH, D, D), dtype=jnp.float32) * scale
        b0 = jnp.zeros((DEPTH, D), dtype=jnp.float32)
        W1 = jax.random.normal(ks[2], (DEPTH, D, D), dtype=jnp.float32) * scale
        b1 = jnp.zeros((DEPTH, D), dtype=jnp.float32)
        W2 = jax.random.normal(ks[3], (DEPTH, 2 * D, D), dtype=jnp.float32) * (1.0 / np.sqrt(2 * D))
        b2 = jnp.zeros((DEPTH, D), dtype=jnp.float32)
        edge_src = jax.random.randint(ks[4], (N_EDGES,), 0, N_NODES, dtype=jnp.int64 if jax.config.jax_enable_x64 else jnp.int32)
        edge_dst = jnp.sort(jax.random.randint(ks[5], (N_EDGES,), 0, N_NODES, dtype=jnp.int64 if jax.config.jax_enable_x64 else jnp.int32))
        return {'x': x, 'W0': W0, 'b0': b0, 'W1': W1, 'b1': b1, 'W2': W2, 'b2': b2, 'edge_src': edge_src, 'edge_dst': edge_dst}
    _L1_gnn_all = _L1_gnn_setup()
    _L1_gnn_in = {k: v for k, v in _L1_gnn_all.items() if k in ('W0', 'b0', 'W1', 'b1', 'W2', 'b2')}
    del _L1_gnn_all

    def _L2_gnn_setup():
        import jax, jax.numpy as jnp
        import numpy as np
        N_NODES = 50000
        N_EDGES = 25000
        D_FEAT = 96
        key = jax.random.key(seed)
        k1, k2, k3 = jax.random.split(key, 3)
        X = jax.random.normal(k1, (N_NODES, D_FEAT), dtype=jnp.float32)
        edge_index = jax.random.randint(k2, (2, N_EDGES), 0, N_NODES, dtype=jnp.int64)
        edge_weight = jax.random.uniform(k3, (N_EDGES,), dtype=jnp.float32)
        return {'X': X, 'edge_index': edge_index, 'edge_weight': edge_weight}
    _L2_gnn_all = _L2_gnn_setup()
    _L2_gnn_in = {k: v for k, v in _L2_gnn_all.items() if k in ()}
    del _L2_gnn_all

    def _L3_gnn_setup():
        import jax, jax.numpy as jnp
        import numpy as np
        N, E = (50000, 25000)
        DIN = DOUT = 96
        DE = 32

        def _egnn_conv(x, src, dst, edge_attr, W_msg, W_edge, W_root, b):
            msg = x[src] @ W_msg + edge_attr @ W_edge
            agg = jax.ops.segment_max(msg, dst, num_segments=x.shape[0])
            agg = jnp.where(jnp.isneginf(agg), 0.0, agg)
            return agg + x @ W_root + b
        key = jax.random.key(seed)
        ks = jax.random.split(key, 10)
        rn = lambda k, sh, sc: jax.random.normal(k, sh, jnp.float32) * sc
        return {'X': rn(ks[0], (N, DIN), 1.0), 'edge_index': jax.random.randint(ks[1], (2, E), 0, N, jnp.int32), 'edge_attr': rn(ks[2], (E, DE), 1.0), 'W1_msg': rn(ks[3], (DIN, DOUT), DIN ** (-0.5)), 'W1_edge': rn(ks[4], (DE, DOUT), DE ** (-0.5)), 'W1_root': rn(ks[5], (DIN, DOUT), DIN ** (-0.5)), 'b1': jnp.zeros((DOUT,), jnp.float32), 'W2_msg': rn(ks[6], (DOUT, DOUT), DOUT ** (-0.5)), 'W2_edge': rn(ks[7], (DE, DOUT), DE ** (-0.5)), 'W2_root': rn(ks[8], (DOUT, DOUT), DOUT ** (-0.5)), 'b2': jnp.zeros((DOUT,), jnp.float32)}
    _L3_gnn_all = _L3_gnn_setup()
    _L3_gnn_in = {k: v for k, v in _L3_gnn_all.items() if k in ('W1_msg', 'W1_edge', 'W1_root', 'b1', 'W2_msg', 'W2_edge', 'W2_root', 'b2')}
    del _L3_gnn_all
    return {'x': x, 'src': src, 'dst': dst, 'edge_attr_32': edge_attr_32, 'edge_weight': edge_weight, 'L1_gnn_W0': _L1_gnn_in['W0'], 'L1_gnn_b0': _L1_gnn_in['b0'], 'L1_gnn_W1': _L1_gnn_in['W1'], 'L1_gnn_b1': _L1_gnn_in['b1'], 'L1_gnn_W2': _L1_gnn_in['W2'], 'L1_gnn_b2': _L1_gnn_in['b2'], 'L3_gnn_W1_msg': _L3_gnn_in['W1_msg'], 'L3_gnn_W1_edge': _L3_gnn_in['W1_edge'], 'L3_gnn_W1_root': _L3_gnn_in['W1_root'], 'L3_gnn_b1': _L3_gnn_in['b1'], 'L3_gnn_W2_msg': _L3_gnn_in['W2_msg'], 'L3_gnn_W2_edge': _L3_gnn_in['W2_edge'], 'L3_gnn_W2_root': _L3_gnn_in['W2_root'], 'L3_gnn_b2': _L3_gnn_in['b2']}

def reference(x, src, dst, edge_attr_32, edge_weight, L1_gnn_W0, L1_gnn_b0, L1_gnn_W1, L1_gnn_b1, L1_gnn_W2, L1_gnn_b2, L3_gnn_W1_msg, L3_gnn_W1_edge, L3_gnn_W1_root, L3_gnn_b1, L3_gnn_W2_msg, L3_gnn_W2_edge, L3_gnn_W2_root, L3_gnn_b2):
    import jax
    import jax.numpy as jnp

    def _L0_gnn_ref(x, edge_index):
        import jax, jax.numpy as jnp
        import numpy as np
        K = 16
        ALPHA = 0.1
        N = x.shape[0]
        loop = jnp.arange(N, dtype=edge_index.dtype)
        row = jnp.concatenate([edge_index[0], loop])
        col = jnp.concatenate([edge_index[1], loop])
        deg = jax.ops.segment_sum(jnp.ones_like(col, dtype=x.dtype), col, num_segments=N)
        deg_inv_sqrt = jnp.where(deg > 0, jax.lax.rsqrt(jnp.maximum(deg, 1e-30)), 0.0)
        norm = (deg_inv_sqrt[row] * deg_inv_sqrt[col])[:, None]
        h = x
        for _ in range(K):
            h_neighbors = jax.ops.segment_sum(norm * h[row], col, num_segments=N)
            h = (1.0 - ALPHA) * h_neighbors + ALPHA * x
        return h

    def _L1_gnn_ref(x, W0, b0, W1, b1, W2, b2, edge_src, edge_dst):
        import jax, jax.numpy as jnp
        import numpy as np
        N_NODES = 50000
        N_EDGES = 25000
        D = 96
        DEPTH = 2
        n = x.shape[0]
        depth = W0.shape[0]
        for i in range(depth):
            h_self = x @ W1[i] + b1[i]
            h_nb = x @ W0[i] + b0[i]
            agg = jax.ops.segment_sum(h_nb[edge_src], edge_dst, num_segments=n)
            x = jnp.concatenate([h_self, agg], axis=-1) @ W2[i] + b2[i]
            x = x / jnp.std(x, axis=-1, ddof=1, keepdims=True)
        return x

    def _L2_gnn_ref(X, edge_index, edge_weight):
        import jax, jax.numpy as jnp
        import numpy as np
        N_NODES = 50000
        N_EDGES = 25000
        D_FEAT = 96
        dst, src = (edge_index[0], edge_index[1])
        messages = edge_weight[:, None] * X[src]
        out = jax.ops.segment_sum(messages, dst, num_segments=X.shape[0])
        return out

    def _L3_gnn_ref(X, edge_index, edge_attr, W1_msg, W1_edge, W1_root, b1, W2_msg, W2_edge, W2_root, b2):
        import jax, jax.numpy as jnp
        import numpy as np
        N, E = (50000, 25000)
        DIN = DOUT = 96
        DE = 32

        def _egnn_conv(x, src, dst, edge_attr, W_msg, W_edge, W_root, b):
            msg = x[src] @ W_msg + edge_attr @ W_edge
            agg = jax.ops.segment_max(msg, dst, num_segments=x.shape[0])
            agg = jnp.where(jnp.isneginf(agg), 0.0, agg)
            return agg + x @ W_root + b
        src, dst = (edge_index[0], edge_index[1])
        c1 = jax.nn.leaky_relu(_egnn_conv(X, src, dst, edge_attr, W1_msg, W1_edge, W1_root, b1))
        c2 = jax.nn.leaky_relu(_egnn_conv(c1, src, dst, edge_attr, W2_msg, W2_edge, W2_root, b2))
        return c2
    edge_index = jnp.stack([src, dst])
    x = _layernorm(x + _L0_gnn_ref(x, edge_index), axis=-1)
    x = _layernorm(x + _L1_gnn_ref(x, L1_gnn_W0, L1_gnn_b0, L1_gnn_W1, L1_gnn_b1, L1_gnn_W2, L1_gnn_b2, src, dst), axis=-1)
    x = _layernorm(x + _L2_gnn_ref(x, edge_index, edge_weight), axis=-1)
    x = _layernorm(x + _L3_gnn_ref(x, edge_index, edge_attr_32, L3_gnn_W1_msg, L3_gnn_W1_edge, L3_gnn_W1_root, L3_gnn_b1, L3_gnn_W2_msg, L3_gnn_W2_edge, L3_gnn_W2_root, L3_gnn_b2), axis=-1)
    return x

_drawn_inputs = setup_inputs


def setup_inputs(seed=0):
    import zlib

    import numpy as np

    out = dict(_drawn_inputs(seed))
    spreads = {'L1_gnn_b0': (0.0, 0.1),
     'L1_gnn_b1': (0.0, 0.1),
     'L1_gnn_b2': (0.0, 0.1),
     'L3_gnn_b1': (0.0, 0.1),
     'L3_gnn_b2': (0.0, 0.1)}
    factors = {}
    for name, (base, spread) in spreads.items():
        noise = np.random.default_rng([zlib.crc32(name.encode()), seed]).standard_normal(out[name].shape)
        drawn = base * np.exp(spread * noise) if base else spread * noise
        out[name] = jnp.asarray(drawn.astype(out[name].dtype))
    for name, factor in factors.items():
        out[name] = (out[name] * factor).astype(out[name].dtype)
    return out
```

```python
from contextlib import ExitStack, contextmanager

import concourse.bass as bass
from concourse import mybir

F32 = mybir.dt.float32
F16 = mybir.dt.float16
I32 = mybir.dt.int32
ALU = mybir.AluOpType
ACT = mybir.ActivationFunctionType
AX = mybir.AxisListType
RMAX = bass.bass_isa.ReduceOp.max

P = 128
N, D, E, DE = 3125, 96, 50000, 32
NB = -(-N // P)
NP = NB * P
T = -(-E // P)
EP = T * P
W = 8
NW = -(-N // W)
SLOTS = -(-(T + NW) // 16) * 16
SG = -(-(SLOTS + 8) // P)
BT = -(-(T + NB) // 16) * 16
KEYS = NB * W
STEPS, ALPHA = 16, 0.1
HALF = (9, 8)
TURN = sum(HALF)
assert T % TURN == 0
EPS = 1e-5
BIG = 1.0e30


@contextmanager
def stage(nc, tag):
    used = []

    def sem(name):
        used.append(nc.alloc_semaphore(f"{name}_{tag}"))
        return used[-1]

    with ExitStack() as c:
        yield c, sem
    nc.clear_and_free_semaphores(used)
    nc.all_engine_barrier()


class Names:
    pass


class Chain:

    def __init__(self, eng, sem):
        self.eng, self.sem, self.n = eng, sem, 0

    def __call__(self, ins):
        self.n += 1
        ins.then_inc(self.sem, 1)
        self.eng.wait_ge(self.sem, self.n)


def carver(at):
    flat, at_byte = at[:].rearrange("p i n -> p (i n)"), [0]

    def take(name, shape, dtype):
        count = 1
        for n in shape[1:]:
            count *= n
        size = 2 if dtype == F16 else 4
        start = at_byte[0] // 2
        at_byte[0] += -(-count * size // 64) * 64
        part = flat[0:shape[0], start:start + count * size // 2]
        part = part if dtype == F16 else part.bitcast(dtype)
        return part.rearrange("p (a b) -> p a b", b=shape[2]) if len(shape) == 3 else part

    return take


def bc_mid(ap, n):
    return ap.unsqueeze(1).to_broadcast([ap.shape[0], n, ap.shape[1]])


def bc_last(ap, n):
    return ap.unsqueeze(2).to_broadcast([ap.shape[0], ap.shape[1], n])


def square_root(nc, act, m, n, x):
    act.wait_ge(m.var_ready, n)
    nc.scalar.activation(m.sd[:], x, ACT.Sqrt).then_inc(m.root_done, 1)


def inverse_root(nc, v, do, m, n, x):
    v.wait_ge(m.root_done, n)
    do(nc.vector.reciprocal(m.sd[:], m.sd[:]))
    do(nc.vector.tensor_tensor(m.nt[:], m.sd[:], m.sd[:], ALU.mult))
    do(nc.vector.tensor_tensor(m.nt[:], m.nt[:], x, ALU.mult))
    do(nc.vector.tensor_scalar(m.nt[:], m.nt[:], -0.5, 1.5, ALU.mult, ALU.add))
    do(nc.vector.tensor_tensor(x, m.sd[:], m.nt[:], ALU.mult))


def layer_norm(nc, v, do, m, out, t, sq, n):
    do(nc.vector.tensor_reduce(m.st1[:], t[:], AX.X, ALU.add))
    do(nc.vector.tensor_scalar(m.st1[:], m.st1[:], 1.0 / D, None, ALU.mult))
    do(nc.vector.tensor_tensor(t[:], t[:], bc_last(m.st1[:], D), ALU.subtract))
    do(nc.vector.tensor_tensor(sq[:], t[:], t[:], ALU.mult))
    do(nc.vector.tensor_reduce(m.st2[:], sq[:], AX.X, ALU.add))
    nc.vector.tensor_scalar(m.st2[:], m.st2[:], 1.0 / D, EPS, ALU.mult, ALU.add).then_inc(m.var_ready, 1)
    inverse_root(nc, v, do, m, n, m.st2[:])
    do(nc.vector.tensor_tensor(out[:], t[:], bc_last(m.st2[:], D), ALU.mult))


def scale_of(nc, do, m, big, scale, unscale):
    k = m.ki
    do(nc.vector.tensor_scalar(k[:, 0:1], big.bitcast(I32), 23, None, ALU.logical_shift_right))
    do(nc.vector.tensor_copy(m.kf[:], k[:, 0:1]))
    do(nc.vector.tensor_scalar(m.kf[:], m.kf[:], 40.0, None, ALU.max))
    do(nc.vector.tensor_scalar(m.kg[:], m.kf[:], -1.0, 254.0 + 13.0, ALU.mult, ALU.add))
    do(nc.vector.tensor_copy(k[:, 0:1], m.kg[:]))
    do(nc.vector.tensor_scalar(scale.bitcast(I32), k[:, 0:1], 23, None, ALU.logical_shift_left))
    do(nc.vector.tensor_scalar(m.kg[:], m.kf[:], 13.0, None, ALU.subtract))
    do(nc.vector.tensor_copy(k[:, 0:1], m.kg[:]))
    do(nc.vector.tensor_scalar(unscale.bitcast(I32), k[:, 0:1], 23, None, ALU.logical_shift_left))


def prepare(nc, m, d):
    with stage(nc, "prepare") as (c, sem):
        sb = carver(m.at)
        dsti = sb("dsti", [P, T], I32)
        rowi = sb("rowi", [P, 256], I32)
        coli = sb("coli", [P, 1], I32)
        lo16, hi16 = sb("lo16", [P, T], F16), sb("hi16", [P, T], F16)
        inti = sb("inti", [P, T], I32)
        onehi = sb("onehi", [P, T * NB], F16)
        onelo = sb("onelo", [P, TURN, P], F16)
        zero16 = sb("zero16", [P, P], F16)
        totincl = sb("totincl", [P, NB], F32)
        srow = sb("srow", [P, 16 * NB], F32)
        sint = sb("sint", [P, 16 * NB], I32)
        first, ceil = sb("first", [P, NW], F32), sb("ceil", [P, NW], F32)
        firsti = sb("firsti", [P, NW + 1], I32)
        cnt, pos, dlt = sb("cnt", [P, NW], F32), sb("pos", [P, NW], F32), sb("dlt", [P, NW], F32)
        junk = sb("junk", [P, NW], F32)
        jcol, bsum, tsum = sb("jcol", [P, SG], F32), sb("bsum", [P, SG], F32), sb("tsum", [P, SG], F32)
        jcoli = sb("jcoli", [P, SG], I32)
        b8 = sb("b8", [P, SG], F32)
        b8i, ti = sb("b8i", [P, SG], I32), sb("ti", [P, SG], I32)
        dg, sg = sb("dg", [P, SG, P], I32), sb("sg", [P, SG, P], I32)
        rel, ok = sb("rel", [P, SG, P], F32), sb("ok", [P, SG, P], F32)
        hi8, lof = sb("hi8", [P, SG, P], F32), sb("lof", [P, SG, P], F32)
        edges, nodes = sem("edges_loaded"), sem("x_loaded")
        iotas, consts, chain = sem("iotas"), sem("constants"), sem("vector_chain")
        lows, free = sem("low_onehots"), sem("low_buffer_free")
        zeroed, counted = sem("psum_zeroed"), sem("degrees_counted")
        degs, prefixed, ptrs = sem("degrees"), sem("prefixes"), sem("row_pointers")
        stored, read = sem("pointers_stored"), sem("pointers_read")
        slots, rows, offs = sem("slot_rows"), sem("slot_edges"), sem("offsets_stored")
        offr, keys, turned = sem("offsets_read"), sem("slot_keys"), sem("keys_turned")
        b = c.enter_context(nc.Block())

        @b.sync
        def _(sp):
            sp.dma_start(dsti[:], d.dst_s).then_inc(edges, 16)
            sp.dma_start(m.x[:], d.x.rearrange("(i p) f -> p i f", p=P)).then_inc(nodes, 16)
            sp.wait_ge(ptrs, 1)
            sp.dma_start(d.ptr.rearrange("(i q) -> q i", q=16), m.rowptr[0:P:8, :], allow_slow_non_contiguous=True).then_inc(stored, 16)
            sp.wait_ge(stored, 16)
            sp.dma_start(srow[:], d.ptr.rearrange("(a n) -> a n", a=1).to_broadcast([P, 16 * NB])).then_inc(read, 16)
            sp.wait_ge(slots, 1)
            sp.dma_start(d.off.rearrange("(g p) -> p g", p=P), b8i[:], allow_slow_non_contiguous=True).then_inc(offs, 16)
            sp.wait_ge(offs, 16)
            sp.dma_start(m.off[:], d.off.rearrange("(a n) -> a n", a=1)).then_inc(offr, 16)
            sp.wait_ge(nodes, 16)
            sp.wait_ge(offr, 16)

        @b.gpsimd
        def _(g):
            nc.gpsimd.iota(rowi[:], [[1, 256]], 0, 0).then_inc(iotas, 1)
            nc.gpsimd.iota(coli[:], [[0, 1]], 0, 1).then_inc(iotas, 1)
            nc.gpsimd.iota(jcoli[:], [[P, SG]], 0, 1).then_inc(iotas, 1)
            g.wait_ge(slots, 1)
            for k in range(SG):
                nc.gpsimd.indirect_dma_start(dg[:, k, :], None, d.dst_rows,
                                             bass.IndirectOffsetOnAxis(ti[:, k:k + 1], 0)).then_inc(rows, 16)
                nc.gpsimd.indirect_dma_start(sg[:, k, :], None, d.src_rows,
                                             bass.IndirectOffsetOnAxis(ti[:, k:k + 1], 0)).then_inc(rows, 16)
            g.wait_ge(rows, 32 * SG)

        @b.vector
        def _(v):
            do = Chain(v, chain)
            v.wait_ge(iotas, 3)
            do(nc.vector.tensor_copy(m.row[:], rowi[:]))
            do(nc.vector.tensor_copy(m.row16[:], rowi[:]))
            do(nc.vector.tensor_copy(m.col[:], coli[:]))
            do(nc.vector.tensor_copy(jcol[:], jcoli[:]))
            do(nc.vector.tensor_scalar(m.ident[:], m.row[:, 0:P], m.col[:], None, ALU.is_equal))
            do(nc.vector.tensor_scalar(m.ident16[:], m.row[:, 0:P], m.col[:], None, ALU.is_equal))
            do(nc.vector.tensor_scalar(m.upper[:], m.row[:, 0:P], m.col[:], None, ALU.is_gt))
            do(nc.vector.tensor_scalar(m.neglow16[:], m.row[:, 0:P], m.col[:], -1.0, ALU.is_le, ALU.mult))
            do(nc.vector.memset(m.ones[:], 1.0))
            do(nc.vector.memset(m.ones16[:], 1.0))
            nc.vector.memset(zero16[:], 0.0).then_inc(consts, 1)
            do(nc.vector.memset(m.padcol[:], 0.0))
            do(nc.vector.tensor_scalar(m.padcol[:, NB - 1:NB], m.col[:], float(N - (NB - 1) * P), None, ALU.is_ge))
            v.wait_ge(edges, 16)
            do(nc.vector.tensor_scalar(inti[:], dsti[:], 7, None, ALU.logical_shift_right))
            do(nc.vector.tensor_copy(hi16[:], inti[:]))
            do(nc.vector.tensor_scalar(inti[:], dsti[:], P - 1, None, ALU.bitwise_and))
            do(nc.vector.tensor_copy(lo16[:], inti[:]))
            do(nc.vector.tensor_tensor(onehi[:].rearrange("p (t i) -> p t i", i=NB), bc_last(hi16[:], NB),
                                       bc_mid(m.row16[:, 0:NB], T), ALU.is_equal))
            with v.Fori(0, T // TURN) as k:
                for h, (a, n) in enumerate(((0, HALF[0]), (HALF[0], HALF[1]))):
                    v.wait_ge(free, 2 * k + h + 1)
                    nc.vector.tensor_tensor(onelo[:, a:a + n, :], bc_last(lo16[:, bass.ds(k * TURN + a, n)], P),
                                            bc_mid(m.row16[:, 0:P], n), ALU.is_equal).then_inc(lows, 1)
            v.wait_ge(counted, 1)
            do(nc.vector.tensor_copy(m.deg[:], m.ps[:, 0, 0:NB]))
            nc.vector.tensor_scalar(m.dinv[:], m.deg[:], 1.0, None, ALU.add).then_inc(m.var_ready, 1)
            inverse_root(nc, v, do, m, 1, m.dinv[:])
            v.sem_inc(degs, 1)
            v.wait_ge(prefixed, 1)
            do(nc.vector.tensor_tensor_scan(totincl[:], m.ones[:, 0:NB], m.ps[:, 2, 0:NB], 0.0, ALU.mult, ALU.add))
            do(nc.vector.tensor_tensor(totincl[:], totincl[:], m.ps[:, 2, 0:NB], ALU.subtract))
            nc.vector.tensor_tensor(m.rowptr[:], totincl[:], m.ps[:, 1, 0:NB], ALU.add).then_inc(ptrs, 1)
            v.wait_ge(read, 16)
            do(nc.vector.tensor_copy(sint[:], srow[:]))
            do(nc.vector.tensor_scalar(firsti[:, 0:NW], sint[:, 0:NW], 7, None, ALU.logical_shift_right))
            do(nc.vector.tensor_copy(first[:], firsti[:, 0:NW]))
            do(nc.vector.tensor_scalar(srow[:], srow[:], float(P - 1), None, ALU.add))
            do(nc.vector.tensor_copy(sint[:], srow[:]))
            do(nc.vector.tensor_scalar(firsti[:, 0:NW], sint[:, 1:NW + 1], 7, None, ALU.logical_shift_right))
            do(nc.vector.tensor_copy(ceil[:], firsti[:, 0:NW]))
            do(nc.vector.tensor_tensor(cnt[:], ceil[:], first[:], ALU.subtract))
            do(nc.vector.tensor_scalar(cnt[:], cnt[:], 1.0, None, ALU.max))
            do(nc.vector.memset(junk[:], 1.0))
            do(nc.vector.tensor_tensor_scan(pos[:], junk[:], cnt[:], 0.0, ALU.mult, ALU.add))
            do(nc.vector.tensor_tensor(pos[:], pos[:], cnt[:], ALU.subtract))
            do(nc.vector.tensor_tensor(first[:], first[:], pos[:], ALU.subtract))
            do(nc.vector.tensor_copy(dlt[:], first[:]))
            do(nc.vector.tensor_tensor(dlt[:, 1:NW], first[:, 1:NW], first[:, 0:NW - 1], ALU.subtract))
            for k in range(SG):
                do(nc.vector.tensor_scalar(junk[:], pos[:], jcol[:, k:k + 1], 0.0, ALU.is_le, ALU.add,
                                           accum_out=bsum[:, k:k + 1]))
                do(nc.vector.scalar_tensor_tensor(junk[:], pos[:], jcol[:, k:k + 1], dlt[:], ALU.is_le, ALU.mult,
                                                  accum_out=tsum[:, k:k + 1]))
            do(nc.vector.tensor_tensor(tsum[:], tsum[:], jcol[:], ALU.add))
            do(nc.vector.tensor_scalar(tsum[:], tsum[:], float(T), None, ALU.min))
            do(nc.vector.tensor_scalar(b8[:], bsum[:], float(W), -float(W), ALU.mult, ALU.add))
            do(nc.vector.tensor_copy(b8i[:], b8[:]))
            nc.vector.tensor_copy(ti[:], tsum[:]).then_inc(slots, 1)
            v.wait_ge(rows, 32 * SG)
            do(nc.vector.tensor_copy(rel[:], dg[:]))
            do(nc.vector.tensor_tensor(rel[:], rel[:], bc_last(b8[:], P), ALU.subtract))
            do(nc.vector.tensor_scalar(ok[:], rel[:], 0.0, None, ALU.is_ge))
            do(nc.vector.scalar_tensor_tensor(ok[:], rel[:], float(W), ok[:], ALU.is_lt, ALU.mult))
            do(nc.vector.tensor_scalar(dg[:], sg[:], 7, 3, ALU.logical_shift_right, ALU.logical_shift_left))
            do(nc.vector.tensor_copy(hi8[:], dg[:]))
            do(nc.vector.scalar_tensor_tensor(rel[:], rel[:], 1.0, hi8[:], ALU.add, ALU.add))
            do(nc.vector.tensor_tensor(rel[:], rel[:], ok[:], ALU.mult))
            do(nc.vector.tensor_scalar(rel[:], rel[:], -1.0, None, ALU.add))
            do(nc.vector.tensor_scalar(dg[:], sg[:], P - 1, None, ALU.bitwise_and))
            nc.vector.tensor_copy(lof[:], dg[:]).then_inc(keys, 1)
            v.wait_ge(turned, 1)
            do(nc.vector.tensor_copy(m.keyT[:], m.ps[:, 4:6, :].rearrange("p a b -> p (a b)")[:, 0:SG * P]))
            do(nc.vector.tensor_scalar(m.neglowT[:], m.ps[:, 6:8, :].rearrange("p a b -> p (a b)")[:, 0:SG * P],
                                       -1.0, None, ALU.mult))

        @b.scalar
        def _(a):
            square_root(nc, a, m, 1, m.dinv[:])

        @b.tensor
        def _(pe):
            pe.wait_ge(consts, 1)
            nc.tensor.matmul(m.ps[:, 0, 0:NB], zero16[:], zero16[:, 0:NB], start=True, stop=False,
                             skip_group_check=True).then_inc(zeroed, 1)
            pe.wait_ge(zeroed, 1)
            pe.sem_inc(free, 2)
            with pe.Fori(0, T // TURN) as k:
                for h, (a, n) in enumerate(((0, HALF[0]), (HALF[0], HALF[1]))):
                    pe.wait_ge(lows, 2 * k + h + 1)
                    for j in range(a, a + n):
                        mm = nc.tensor.matmul(m.ps[:, 0, 0:NB], onelo[:, j, :],
                                              onehi[:, bass.ds((k * TURN + j) * NB, NB)],
                                              start=False, stop=False, skip_group_check=True)
                    mm.then_inc(free, 1)
            pe.wait_ge(free, 2 + 2 * (T // TURN))
            pe.sem_inc(counted, 1)
            pe.wait_ge(degs, 1)
            nc.tensor.matmul(m.ps[:, 1, 0:NB], m.upper[:], m.deg[:], start=True, stop=True)
            nc.tensor.matmul(m.ps[:, 2, 0:NB], m.ones[:], m.deg[:], start=True, stop=True).then_inc(prefixed, 1)
            pe.wait_ge(keys, 1)
            for k in range(SG):
                nc.tensor.transpose(m.ps[:, 4 + k // 4, (k % 4) * P:(k % 4 + 1) * P], rel[:, k, :], m.ident[:])
                mm = nc.tensor.transpose(m.ps[:, 6 + k // 4, (k % 4) * P:(k % 4 + 1) * P], lof[:, k, :], m.ident[:])
            mm.then_inc(turned, 1)


def build_counts(nc, m, d):
    with stage(nc, "build") as (c, sem):
        sb = lambda n, s, t: c.enter_context(nc.sbuf_tensor(n, s, t))
        RING, LEAD, PER = 8, 4, 16
        onekey = sb("onekey", [P, RING, KEYS], F16)
        square = sb("square", [P, RING, P], F16)
        oneplace = sb("oneplace", [P, RING, P], F16)
        cleared = sem("counts_cleared")
        keyed, placed, squared = sem("key_onehots"), sem("place_onehots"), sem("squares")
        product, added = sem("slot_products"), sem("slots_added")
        b = c.enter_context(nc.Block())

        @b.gpsimd
        def _(g):
            half = NB // 2
            nc.gpsimd.memset(m.at[:, half:NB, :], 0.0).then_inc(cleared, 1)

        @b.scalar
        def _(a):
            with a.Fori(0, SLOTS // PER) as k:
                for q in range(0, PER, 4):
                    r = q % RING
                    a.wait_ge(product, PER * k + (q + 4))
                    for j in range(4):
                        nc.scalar.activation(square[:, r + j, :], m.row[:, 0:P], ACT.Square,
                                             bias=m.neglowT[:, bass.ds(PER * k + (q + j), 1)]).then_inc(squared, 1)
                    a.wait_ge(squared, PER * k + q + 4)
                    nc.scalar.activation(oneplace[:, r:r + 4, :], square[:, r:r + 4, :], ACT.Relu,
                                         bias=1.0, scale=-1.0).then_inc(placed, 4)

        @b.vector
        def _(v):
            nc.vector.memset(m.at[:, 0:NB // 2, :], 0.0).then_inc(cleared, 1)
            for j in range(LEAD):
                nc.vector.tensor_scalar(onekey[:, j, :], m.row16[:, 0:KEYS], m.keyT[:, j:j + 1], None,
                                        ALU.is_equal).then_inc(keyed, 1)
            v.wait_ge(cleared, 2)
            v.sem_inc(added, RING)
            regs = [v.alloc_register(f"window{j}") for j in range(PER)]
            with v.Fori(0, SLOTS // PER) as k:
                for j in range(0, PER, 4):
                    v.load(regs[j:j + 4], m.off[0:1, bass.ds(PER * k + j, 4)])
                at = [v.snap(r) for r in regs]
                for j in range(PER):
                    v.wait_ge(product, PER * k + (j + LEAD + 1))
                    nc.vector.tensor_scalar(onekey[:, (j + LEAD) % RING, :], m.row16[:, 0:KEYS],
                                            m.keyT[:, bass.ds(PER * k + (j + LEAD), 1)], None,
                                            ALU.is_equal).then_inc(keyed, 1)
                    v.wait_ge(product, PER * k + (j + RING + 1))
                    v.wait_ge(added, PER * k + (j + RING))
                    win = m.at[:, :, bass.ds(at[j], W)]
                    nc.vector.tensor_tensor(win, win, m.ps[:, j % RING, 0:KEYS].rearrange("p (i w) -> p i w", w=W),
                                            ALU.add).then_inc(added, 1)

        @b.tensor
        def _(pe):
            pe.sem_inc(product, RING)
            with pe.Fori(0, SLOTS // PER) as k:
                for j in range(PER):
                    if j % 4 == 0:
                        pe.wait_ge(placed, PER * k + j + 4)
                    pe.wait_ge(keyed, PER * k + (j + 1))
                    pe.wait_ge(added, PER * k + (j + 1))
                    nc.tensor.matmul(m.ps[:, j % RING, 0:KEYS], oneplace[:, j % RING, :], onekey[:, j % RING, :],
                                     start=True, stop=True).then_inc(product, 1)


def bucket_ranks(nc, m, d):
    with stage(nc, "ranks") as (c, sem):
        sb = carver(m.at)
        inti = sb("inti2", [P, T], I32)
        dsti, srci = sb("dsti2", [P, T], I32), sb("srci2", [P, T], I32)
        w, rec = sb("w2", [P, T], F32), sb("rec", [P, T, 4], I32)
        hi = sb("hi2", [P, T], F16)
        lo = sb("lo2", [P, T], I32)
        onehi = sb("onehi2", [P, 2, T], F16)
        run, acc, tmp = sb("run", [P, T], F32), sb("acc", [P, T], F32), sb("tmp", [P, T], F32)
        one = sb("one_row", [P, T], F32)
        hif = sb("hif", [P, T], F32)
        cnt, base, incl = sb("bcnt", [P, NB], F32), sb("base", [P, NB], F32), sb("incl", [P, NB], F32)
        cnti = sb("bcnti", [P, NB], I32)
        rank = sb("rank", [P, T], I32)
        tj = sb("tj", [1, BT], F32)
        cmp = sb("cmp", [1, BT], F32)
        tji = sb("tji", [1, BT], I32)
        zeros = sb("zeros_i", [P, BT * 4 // 16], I32)
        chain, ones, sums = sem("rank_chain"), sem("block_onehots"), sem("block_sums")
        taken, io, cleared = sem("sums_taken"), sem("tile_iota"), sem("zeros_made")
        tabz, ld, made, stored = sem("table_cleared"), sem("edges_loaded"), sem("records_made"), sem("records_stored")
        b = c.enter_context(nc.Block())

        @b.gpsimd
        def _(g):
            nc.gpsimd.iota(tji[:], [[1, BT]], 0, 0).then_inc(io, 1)

        @b.sync
        def _(sp):
            sp.dma_start(dsti[:], d.dst_s).then_inc(ld, 16)
            sp.dma_start(srci[:], d.src_s).then_inc(ld, 16)
            sp.dma_start(w[:], d.w_s).then_inc(ld, 16)
            sp.wait_ge(cleared, 1)
            for q in range(16):
                n = BT * 4 // 16
                sp.dma_start(d.table.rearrange("(p t) c -> p (t c)", p=P)[:, q * n:(q + 1) * n], zeros[:]).then_inc(tabz, 16)
            sp.wait_ge(made, 1)
            sp.dma_start(d.rec, rec[:]).then_inc(stored, 16)
            sp.wait_ge(tabz, 256)
            sp.wait_ge(stored, 16)

        @b.vector
        def _(v):
            do = Chain(v, chain)
            nc.vector.memset(zeros[:], 0).then_inc(cleared, 1)
            do(nc.vector.memset(one[:], 1.0))
            do(nc.vector.memset(acc[:], 0.0))
            v.wait_ge(ld, 48)
            do(nc.vector.tensor_scalar(inti[:], srci[:], 7, None, ALU.logical_shift_right))
            do(nc.vector.tensor_copy(hif[:], inti[:]))
            do(nc.vector.tensor_scalar(lo[:], srci[:], P - 1, None, ALU.bitwise_and))
            do(nc.vector.tensor_copy(rec[:, :, 0:1], dsti[:].unsqueeze(2)))
            do(nc.vector.tensor_copy(rec[:, :, 1:2], lo[:].unsqueeze(2)))
            do(nc.vector.tensor_copy(rec[:, :, 2:3], w[:].bitcast(I32).unsqueeze(2)))
            for i in range(NB + 1):
                if i < NB:
                    if i >= 2:
                        v.wait_ge(sums, i - 1)
                    nc.vector.tensor_scalar(onehi[:, i % 2, :], hif[:], float(i), None, ALU.is_equal).then_inc(ones, 1)
                if i >= 1:
                    q = i - 1
                    v.wait_ge(sums, q + 1)
                    v.wait_ge(ones, q + 1)
                    do(nc.vector.tensor_tensor_scan(run[:], one[:], m.ps[:, 2 * (q % 2), 0:T], 0.0, ALU.mult, ALU.add))
                    do(nc.vector.tensor_copy(cnt[:, q:q + 1], run[:, T - 1:T]))
                    do(nc.vector.tensor_tensor(tmp[:], run[:], m.ps[:, 2 * (q % 2) + 1, 0:T], ALU.add))
                    v.sem_inc(taken, 1)
                    do(nc.vector.scalar_tensor_tensor(tmp[:], hif[:], float(q), tmp[:], ALU.is_equal, ALU.mult))
                    do(nc.vector.tensor_tensor(acc[:], acc[:], tmp[:], ALU.add))
            do(nc.vector.tensor_scalar(cnt[:], cnt[:], float(P - 1), None, ALU.add))
            do(nc.vector.tensor_copy(cnti[:], cnt[:]))
            do(nc.vector.tensor_scalar(cnti[:], cnti[:], 7, None, ALU.logical_shift_right))
            do(nc.vector.tensor_copy(cnt[:], cnti[:]))
            do(nc.vector.tensor_tensor_scan(incl[:], one[:, 0:NB], cnt[:], 0.0, ALU.mult, ALU.add))
            do(nc.vector.tensor_tensor(base[:], incl[:], cnt[:], ALU.subtract))
            v.wait_ge(io, 1)
            do(nc.vector.tensor_copy(tj[:], tji[:]))
            do(nc.vector.memset(cmp[:], -1.0))
            for i in range(NB):
                do(nc.vector.scalar_tensor_tensor(cmp[:], tj[:], base[0:1, i:i + 1], cmp[:], ALU.is_ge, ALU.add))
            do(nc.vector.tensor_scalar(cmp[:], cmp[:], float(D), None, ALU.mult))
            do(nc.vector.tensor_copy(m.bucket[:], cmp[:]))
            do(nc.vector.tensor_scalar(base[:], base[:], float(P), None, ALU.mult))
            for i in range(NB):
                do(nc.vector.tensor_scalar(tmp[:], hif[:], float(i), base[:, i:i + 1], ALU.is_equal, ALU.mult))
                do(nc.vector.tensor_tensor(acc[:], acc[:], tmp[:], ALU.add))
            do(nc.vector.tensor_copy(rank[:], acc[:]))
            do(nc.vector.tensor_scalar(inti[:], rank[:], 7, None, ALU.logical_shift_right))
            do(nc.vector.tensor_copy(run[:], inti[:]))
            do(nc.vector.tensor_scalar(inti[:], rank[:], P - 1, None, ALU.bitwise_and))
            do(nc.vector.tensor_copy(tmp[:], inti[:]))
            do(nc.vector.scalar_tensor_tensor(acc[:], tmp[:], float(BT), run[:], ALU.mult, ALU.add))
            nc.vector.tensor_copy(rec[:, :, 3:4], acc[:].unsqueeze(2)).then_inc(made, 1)

        @b.tensor
        def _(pe):
            for i in range(NB):
                pe.wait_ge(ones, i + 1)
                if i >= 2:
                    pe.wait_ge(taken, i - 1)
                nc.tensor.matmul(m.ps[:, 2 * (i % 2), 0:T], m.ones16[:], onehi[:, i % 2, :], start=True, stop=True)
                nc.tensor.matmul(m.ps[:, 2 * (i % 2) + 1, 0:T], m.neglow16[:], onehi[:, i % 2, :],
                                 start=True, stop=True).then_inc(sums, 1)


def count_product(nc, m, parts, blk, bank, before=None):
    for s in range(NB):
        if before:
            before(s)
        mm = nc.tensor.matmul(m.ps[:, bank, 0:2 * D], m.at[:, s, blk * P:(blk + 1) * P], parts[:, s, :],
                              start=(s == 0), stop=(s == NB - 1))
    return mm


def appnp(nc, m, d):
    with stage(nc, "l0") as (c, sem):
        sb = lambda n, s, t: c.enter_context(nc.sbuf_tensor(n, s, t))
        parts = sb("parts", [P, 2, NB, 2 * D], F16)
        g0 = sb("g0", [P, NB, D], F32)
        coef = sb("coef", [P, NB], F32)
        t1 = sb("t1", [P, 2, D], F32)
        t2 = sb("t2", [P, 2, D], F32)
        gm, ga = sb("gm", [P, 1], F32), sb("ga", [P, 1], F32)
        back = sb("back", [P, NB], F32)
        un, scl = sb("un0", [P, 1], F32), sb("scl0", [P, 1], F32)
        recs = sb("recs", [P, 2, HALF[0], 4], I32)
        chain, mx, amx, ready = sem("l0_chain"), sem("g_max"), sem("g_max_all"), sem("g_parts")
        prod, taken, high = sem("l0_products"), sem("l0_product_taken"), sem("high_part")
        tmp1, turns = sem("l0_partial"), sem("turns")
        staged, scat = [sem("records_a"), sem("records_b")], [sem("scattered_a"), sem("scattered_b")]
        b = c.enter_context(nc.Block())
        NBK = 5

        @b.gpsimd
        def _(g):
            g.wait_ge(mx, 1)
            nc.gpsimd.partition_all_reduce(ga[:], gm[:], P, RMAX).then_inc(amx, 1)
            with g.Fori(0, T // TURN) as k:
                for h, n in enumerate(HALF):
                    g.wait_ge(staged[h], 16 * k + 16)
                    g.sem_inc(turns, 1)
                    for j in range(n):
                        nc.gpsimd.indirect_dma_start(d.table, bass.IndirectOffsetOnAxis(recs[:, h, j, 3:4], 0),
                                                     recs[:, h, j, :], None).then_inc(scat[h], 16)
            for h, n in enumerate(HALF):
                g.wait_ge(scat[h], 16 * n * (T // TURN))

        @b.scalar
        def _(a):
            square_root(nc, a, m, 2, m.st2[:])

        @b.sync
        def _(sp):
            for h, n in enumerate(HALF):
                sp.dma_start(recs[:, h, 0:n, :], d.rec[:, h * HALF[0]:h * HALF[0] + n, :]).then_inc(staged[h], 16)
            with sp.Fori(1, T // TURN) as k:
                for h, n in enumerate(HALF):
                    sp.wait_ge(scat[h], 16 * n * k)
                    sp.dma_start(recs[:, h, 0:n, :], d.rec[:, bass.ds(k * TURN + h * HALF[0], n), :]).then_inc(staged[h], 16)

        @b.vector
        def _(v):
            do = Chain(v, chain)
            for i in range(NB):
                blk = m.at[:, i, i * P:(i + 1) * P]
                nc.vector.tensor_tensor(blk, blk, m.ident16[:], ALU.add)
            do(nc.vector.tensor_tensor(g0[:], m.x[:], bc_last(m.dinv[:], D), ALU.mult))
            nc.vector.tensor_reduce(gm[:], g0[:].rearrange("p i f -> p (i f)"), AX.X, ALU.max, apply_absolute_value=True).then_inc(mx, 1)
            do(nc.vector.tensor_tensor(coef[:], m.dinv[:], m.dinv[:], ALU.mult))
            do(nc.vector.tensor_scalar(coef[:], coef[:], 1.0 - ALPHA, None, ALU.mult))
            v.wait_ge(amx, 1)
            scale_of(nc, do, m, ga[:], scl[:], un[:])
            do(nc.vector.tensor_scalar(g0[:], g0[:], scl[:], None, ALU.mult))
            do(nc.vector.tensor_copy(parts[:, 0, :, 0:D], g0[:]))
            do(nc.vector.tensor_tensor(parts[:, 0, :, D:2 * D], g0[:], parts[:, 0, :, 0:D], ALU.subtract))
            v.sem_inc(ready, NB)
            do(nc.vector.tensor_scalar(g0[:], g0[:], ALPHA, None, ALU.mult))
            do(nc.vector.tensor_scalar(back[:], m.deg[:], 1.0, None, ALU.add))
            do(nc.vector.tensor_tensor(back[:], back[:], m.dinv[:], ALU.mult))
            do(nc.vector.tensor_scalar(back[:], back[:], un[:], None, ALU.mult))
            with v.Fori(0, STEPS // 2) as k:
                for r in range(2 * NB):
                    i, nxt = r % NB, 1 - r // NB
                    v.wait_ge(prod, 2 * NB * k + (r + 1))
                    nc.vector.scalar_tensor_tensor(t1[:, r % 2, :], m.ps[:, r % NBK, 0:D], coef[:, i:i + 1],
                                                   g0[:, i, :], ALU.mult, ALU.add).then_inc(tmp1, 1)
                    v.wait_ge(tmp1, 4 * NB * k + (2 * r + 1))
                    nc.vector.scalar_tensor_tensor(t2[:, r % 2, :], m.ps[:, r % NBK, D:2 * D], coef[:, i:i + 1],
                                                   t1[:, r % 2, :], ALU.mult, ALU.add).then_inc(tmp1, 1)
                    v.wait_ge(tmp1, 4 * NB * k + (2 * r + 2))
                    v.sem_inc(taken, 1)
                    nc.vector.tensor_copy(parts[:, nxt, i, 0:D], t2[:, r % 2, :]).then_inc(high, 1)
                    v.wait_ge(high, 2 * NB * k + (r + 1))
                    nc.vector.tensor_tensor(parts[:, nxt, i, D:2 * D], t2[:, r % 2, :], parts[:, nxt, i, 0:D],
                                            ALU.subtract).then_inc(ready, 1)
            v.wait_ge(ready, NB * (STEPS + 1))
            do(nc.vector.tensor_tensor(g0[:], parts[:, 0, :, 0:D], parts[:, 0, :, D:2 * D], ALU.add))
            do(nc.vector.tensor_tensor(g0[:], g0[:], bc_last(back[:], D), ALU.mult))
            do(nc.vector.tensor_tensor(g0[:], g0[:], m.x[:], ALU.add))
            sq = parts[:].rearrange("p a i f -> p (a i f)").bitcast(F32)[:, 0:NB * D]
            layer_norm(nc, v, do, m, m.x, g0, sq.rearrange("p (i f) -> p i f", f=D), 2)
            for i in range(NB):
                blk = m.at[:, i, i * P:(i + 1) * P]
                nc.vector.tensor_tensor(blk, blk, m.ident16[:], ALU.subtract)

        @b.tensor
        def _(pe):
            pe.sem_inc(taken, NBK)
            with pe.Fori(0, STEPS // 2) as k:
                for r in range(2 * NB):
                    pe.wait_ge(taken, 2 * NB * k + (r + 1))
                    before = (lambda s: pe.wait_ge(ready, 2 * NB * k + (r + s + 1))) if r % NB == 0 else None
                    count_product(nc, m, parts[:, r // NB], r % NB, r % NBK, before).then_inc(prod, 1)


def sage(nc, m, d, layer):
    with stage(nc, f"l1_{layer}") as (c, sem):
        sb = lambda n, s, t: c.enter_context(nc.sbuf_tensor(n + f"_{layer}", s, t))
        w0, w1 = sb("w0", [D, D], F32), sb("w1", [D, D], F32)
        w2a, w2b = sb("w2a", [D, D], F32), sb("w2b", [D, D], F32)
        b0, b1, b2 = sb("b0", [P, D], F32), sb("b1", [D, 1], F32), sb("b2", [P, D], F32)
        xT, hsT = sb("xT", [D, 2, P], F32), sb("hsT", [D, 2, P], F32)
        y = m.y
        nb = sb("nb", [P, NB, D], F32)
        parts = sb("nbparts", [P, NB, 2 * D], F16)
        agg, aggT = sb("agg", [P, 2, D], F32), sb("aggT", [D, 2, P], F32)
        gm, ga = sb("gm1", [P, 1], F32), sb("ga1", [P, 1], F32)
        un, scl = sb("un1", [P, 1], F32), sb("scl1", [P, 1], F32)
        wl, chain = sem("sage_weights"), sem("sage_chain")
        turned, xcp, nbd, hsd = sem("x_turned"), sem("xT_copied"), sem("nb_product"), sem("hs_product")
        nbc, hsc, outd, outc = sem("nb_copied"), sem("hs_copied"), sem("self_out"), sem("self_out_taken")
        mx, amx, ready = sem("nb_max"), sem("nb_max_all"), sem("nb_parts")
        prod, aggc, aggt, aggtc = sem("agg_product"), sem("agg_copied"), sem("agg_turned"), sem("aggT_copied")
        outb, outbc, half = sem("agg_out"), sem("agg_out_taken"), sem("agg_half")
        b = c.enter_context(nc.Block())
        src = m.x if layer == 0 else m.y

        @b.sync
        def _(sp):
            sp.dma_start(w0[:], d.W0[layer]).then_inc(wl, 16)
            sp.dma_start(w1[:], d.W1[layer]).then_inc(wl, 16)
            sp.dma_start(w2a[:], d.W2[layer, 0:D, :]).then_inc(wl, 16)
            sp.dma_start(w2b[:], d.W2[layer, D:2 * D, :]).then_inc(wl, 16)
            sp.dma_start(b0[:], d.b0[layer:layer + 1, :].to_broadcast([P, D])).then_inc(wl, 16)
            sp.dma_start(b2[:], d.b2[layer:layer + 1, :].to_broadcast([P, D])).then_inc(wl, 16)
            sp.dma_start(b1[:], d.b1[layer].rearrange("(f a) -> f a", a=1), allow_slow_non_contiguous=True).then_inc(wl, 16)
            sp.wait_ge(wl, 112)

        @b.gpsimd
        def _(g):
            g.wait_ge(mx, 1)
            nc.gpsimd.partition_all_reduce(ga[:], gm[:], P, RMAX).then_inc(amx, 1)

        @b.scalar
        def _(a):
            a.wait_ge(wl, 112)
            for i in range(NB):
                a.wait_ge(turned, i + 1)
                if i >= 2:
                    a.wait_ge(hsd, i - 1)
                nc.scalar.activation(xT[:, i % 2, :], m.ps[0:D, i % 2, 0:P], ACT.Copy).then_inc(xcp, 1)
                a.wait_ge(hsd, i + 1)
                if i >= 2:
                    a.wait_ge(outd, i - 1)
                nc.scalar.activation(hsT[:, i % 2, :], m.ps[0:D, 4 + i % 2, 0:P], ACT.Identity,
                                     bias=b1[:]).then_inc(hsc, 1)
            for i in range(NB):
                a.wait_ge(aggt, i + 1)
                if i >= 2:
                    a.wait_ge(outb, i - 1)
                nc.scalar.activation(aggT[:, i % 2, :], m.ps[0:D, 4 + i % 2, 0:P], ACT.Copy).then_inc(aggtc, 1)
            square_root(nc, a, m, 3 + layer, m.st2[:])
            if layer == 1:
                square_root(nc, a, m, 5, m.st2[:])

        @b.vector
        def _(v):
            do = Chain(v, chain)
            v.wait_ge(wl, 112)
            for i in range(NB):
                v.wait_ge(nbd, i + 1)
                nc.vector.tensor_tensor(nb[:, i, :], m.ps[:, 2 + i % 2, 0:D], b0[:], ALU.add).then_inc(nbc, 1)
                v.wait_ge(outd, i + 1)
                nc.vector.tensor_tensor(y[:, i, :], m.ps[:, 6 + i % 2, 0:D], b2[:], ALU.add).then_inc(outc, 1)
            v.wait_ge(nbc, NB)
            v.wait_ge(outc, NB)
            nc.vector.tensor_reduce(gm[:], nb[:].rearrange("p i f -> p (i f)"), AX.X, ALU.max, apply_absolute_value=True).then_inc(mx, 1)
            v.wait_ge(amx, 1)
            scale_of(nc, do, m, ga[:], scl[:], un[:])
            do(nc.vector.tensor_scalar(nb[:], nb[:], scl[:], None, ALU.mult))
            do(nc.vector.tensor_copy(parts[:, :, 0:D], nb[:]))
            nc.vector.tensor_tensor(parts[:, :, D:2 * D], nb[:], parts[:, :, 0:D], ALU.subtract).then_inc(ready, 1)
            for i in range(NB + 2):
                if i < NB:
                    v.wait_ge(prod, i + 1)
                    if i >= 2:
                        v.wait_ge(aggt, i - 1)
                    nc.vector.tensor_scalar(agg[:, i % 2, :], m.ps[:, i % 4, 0:D], un[:], None,
                                            ALU.mult).then_inc(half, 1)
                    v.wait_ge(half, i + 1)
                    nc.vector.scalar_tensor_tensor(agg[:, i % 2, :], m.ps[:, i % 4, D:2 * D], un[:],
                                                   agg[:, i % 2, :], ALU.mult, ALU.add).then_inc(aggc, 1)
                if i >= 2:
                    q = i - 2
                    v.wait_ge(outb, q + 1)
                    nc.vector.tensor_tensor(y[:, q, :], y[:, q, :], m.ps[:, 6 + q % 2, 0:D], ALU.add).then_inc(outbc, 1)
            v.wait_ge(outbc, NB)
            do(nc.vector.tensor_reduce(m.st1[:], y[:], AX.X, ALU.add))
            do(nc.vector.tensor_scalar(m.st1[:], m.st1[:], 1.0 / D, None, ALU.mult))
            do(nc.vector.tensor_tensor(nb[:], y[:], bc_last(m.st1[:], D), ALU.subtract))
            do(nc.vector.tensor_tensor(nb[:], nb[:], nb[:], ALU.mult))
            do(nc.vector.tensor_reduce(m.st2[:], nb[:], AX.X, ALU.add))
            nc.vector.scalar_tensor_tensor(m.st2[:], m.st2[:], 1.0 / (D - 1), m.padcol[:], ALU.mult,
                                           ALU.add).then_inc(m.var_ready, 1)
            inverse_root(nc, v, do, m, 3 + layer, m.st2[:])
            do(nc.vector.tensor_tensor(y[:], y[:], bc_last(m.st2[:], D), ALU.mult))
            if layer == 1:
                do(nc.vector.tensor_tensor(y[:], y[:], m.x[:], ALU.add))
                layer_norm(nc, v, do, m, m.x, y, nb, 5)

        @b.tensor
        def _(pe):
            pe.wait_ge(wl, 112)
            for i in range(NB + 2):
                if i < NB:
                    if i >= 2:
                        pe.wait_ge(xcp, i - 1)
                    nc.tensor.transpose(m.ps[0:D, i % 2, 0:P], src[:, i, :], m.ident[:]).then_inc(turned, 1)
                if 1 <= i <= NB:
                    q = i - 1
                    pe.wait_ge(xcp, q + 1)
                    if q >= 2:
                        pe.wait_ge(nbc, q - 1)
                        pe.wait_ge(hsc, q - 1)
                    nc.tensor.matmul(m.ps[:, 2 + q % 2, 0:D], xT[:, q % 2, :], w0[:], start=True, stop=True).then_inc(nbd, 1)
                    nc.tensor.matmul(m.ps[0:D, 4 + q % 2, 0:P], w1[:], xT[:, q % 2, :], start=True,
                                     stop=True).then_inc(hsd, 1)
                if i >= 2:
                    q = i - 2
                    pe.wait_ge(hsc, q + 1)
                    if q >= 2:
                        pe.wait_ge(outc, q - 1)
                    nc.tensor.matmul(m.ps[:, 6 + q % 2, 0:D], hsT[:, q % 2, :], w2a[:], start=True,
                                     stop=True).then_inc(outd, 1)
            pe.wait_ge(ready, 1)
            for i in range(NB + 2):
                if i < NB:
                    if i >= 4:
                        pe.wait_ge(aggc, i - 3)
                    count_product(nc, m, parts, i, i % 4).then_inc(prod, 1)
                if 1 <= i <= NB:
                    q = i - 1
                    pe.wait_ge(aggc, q + 1)
                    if q >= 2:
                        pe.wait_ge(aggtc, q - 1)
                    nc.tensor.transpose(m.ps[0:D, 4 + q % 2, 0:P], agg[:, q % 2, :], m.ident[:]).then_inc(aggt, 1)
                if i >= 2:
                    q = i - 2
                    pe.wait_ge(aggtc, q + 1)
                    if q >= 2:
                        pe.wait_ge(outbc, q - 1)
                    nc.tensor.matmul(m.ps[:, 6 + q % 2, 0:D], aggT[:, q % 2, :], w2b[:], start=True,
                                     stop=True).then_inc(outb, 1)


def weighted_sum(nc, m, d):
    with stage(nc, "l2") as (c, sem):
        sb = lambda n, s, t: c.enter_context(nc.sbuf_tensor(n, s, t))
        R = 16
        tab = sb("tab", [P, BT, 4], I32)
        low, wt = sb("low", [P, BT], F32), sb("wt", [P, BT], F32)
        targets = sb("targets", [P, BT], I32)
        idx = sb("idx", [P, 2, R // 2], I32)
        rows = sb("rows", [P, R, D], F32)
        onew = sb("onew", [P, 4, P], F32)
        sq = sb("sq2", [P, NB, D], F32)
        acc = sb("acc2", [P, NB * D], F32)
        loaded, chain, xst = sem("table_loaded"), sem("l2_chain"), sem("x_stored")
        turns = sem("turns")
        staged, split = sem("index_staged"), sem("targets_split")
        got = [sem(f"row_{j}_gathered") for j in range(R)]
        hot, prod, add = sem("weighted_onehots"), sem("l2_products"), sem("l2_added")
        b = c.enter_context(nc.Block())

        @b.sync
        def _(sp):
            sp.dma_start(tab[:], d.table.rearrange("(p t) c -> p t c", p=P)).then_inc(loaded, 16)
            sp.dma_start(d.xt.rearrange("(i p) f -> p i f", p=P), m.x[:]).then_inc(xst, 16)
            sp.wait_ge(xst, 16)

        @b.gpsimd
        def _(g):
            g.wait_ge(split, 1)
            g.wait_ge(xst, 16)
            g.sem_inc(prod, R)
            with g.Fori(0, BT // R) as k:
                for h in range(2):
                    g.wait_ge(prod, R * k + (R // 2) * (h + 1))
                    nc.gpsimd.tensor_copy(idx[:, h, :], targets[:, bass.ds(R * k + (R // 2) * h, R // 2)]).then_inc(staged, 1)
                    g.wait_ge(staged, 2 * k + (h + 1))
                    g.sem_inc(turns, 1)
                    for j in range(R // 2):
                        r = R // 2 * h + j
                        nc.gpsimd.indirect_dma_start(rows[:, r, :], None, d.xt,
                                                     bass.IndirectOffsetOnAxis(idx[:, h, j:j + 1], 0)).then_inc(got[r], 16)

        @b.vector
        def _(v):
            do = Chain(v, chain)
            do(nc.vector.memset(acc[:], 0.0))
            v.wait_ge(loaded, 16)
            nc.vector.tensor_copy(targets[:], tab[:, :, 0]).then_inc(split, 1)
            do(nc.vector.tensor_copy(low[:], tab[:, :, 1]))
            do(nc.vector.tensor_copy(wt[:], tab[:, :, 2].bitcast(F32)))
            regs = [v.alloc_register(f"bucket{j}") for j in range(R)]
            v.sem_inc(add, 8)
            with v.Fori(0, BT // R) as k:
                for j in range(0, R, 4):
                    v.load(regs[j:j + 4], m.bucket[0:1, bass.ds(R * k + j, 4)])
                at = [v.snap(r) for r in regs]
                for j in range(R + 1):
                    if j < R:
                        v.wait_ge(prod, R * k + (j + R - 3))
                        nc.vector.tensor_scalar(onew[:, j % 4, :], m.row[:, 0:P], low[:, bass.ds(R * k + j, 1)],
                                                wt[:, bass.ds(R * k + j, 1)], ALU.is_equal,
                                                ALU.mult).then_inc(hot, 1)
                    if j >= 1:
                        q = j - 1
                        v.wait_ge(prod, R * k + (q + R + 1))
                        v.wait_ge(add, R * k + (q + 8))
                        dst = acc[:, bass.ds(at[q], D)]
                        nc.vector.tensor_tensor(dst, dst, m.ps[:, q % 8, 0:D], ALU.add).then_inc(add, 1)
            v.wait_ge(add, BT + 8)
            s = acc[:].rearrange("p (i f) -> p i f", f=D)
            do(nc.vector.tensor_tensor(s, s, m.x[:], ALU.add))
            layer_norm(nc, v, do, m, m.x, s, sq, 6)

        @b.scalar
        def _(a):
            square_root(nc, a, m, 6, m.st2[:])

        @b.tensor
        def _(pe):
            with pe.Fori(0, BT // R) as k:
                for j in range(R):
                    pe.wait_ge(hot, R * k + (j + 1))
                    pe.wait_ge(got[j], 16 * k + 16)
                    pe.wait_ge(add, R * k + (j + 1))
                    nc.tensor.matmul(m.ps[:, j % 8, 0:D], onew[:, j % 4, :], rows[:, j, :], start=True,
                                     stop=True).then_inc(prod, 1)


def edge_masks(nc, m, d):
    with stage(nc, "masks") as (c, sem):
        sb = lambda n, s, t: c.enter_context(nc.sbuf_tensor(n, s, t))
        dsti = sb("dsti3", [P, T], I32)
        prev, dstf, prevf = sb("prev", [P, 1], I32), sb("dstf", [P, T], F32), sb("prevf", [P, 1], F32)
        cont, mcol = sb("cont", [P, 1], F32), sb("mcol", [P, 1], F32)
        mrep, rem = sb("mrep", [P, D], F32), sb("rem", [P, NB], F32)
        e, q, s = sb("e_end", [P, NB], F32), sb("q_end", [P, NB], F32), sb("q_start", [P, NB], F32)
        eld = sem("edges_loaded3")
        chain, z, ld = sem("mask_chain"), sem("prev_cleared"), sem("prev_loaded")
        rep, rowd = sem("carry_column"), sem("carry_row")
        b = c.enter_context(nc.Block())

        @b.sync
        def _(sp):
            sp.dma_start(dsti[:], d.dst_s).then_inc(eld, 16)
            sp.dma_start(m.srci[:], d.src_s).then_inc(eld, 16)
            sp.wait_ge(z, 1)
            sp.dma_start(prev[1:P, :], d.dst_s[0:P - 1, T - 1:T], allow_slow_non_contiguous=True).then_inc(ld, 16)
            sp.wait_ge(ld, 16)

        @b.vector
        def _(v):
            do = Chain(v, chain)
            nc.vector.memset(prev[:], -1).then_inc(z, 1)
            v.wait_ge(eld, 32)
            do(nc.vector.tensor_copy(dstf[:], dsti[:]))
            do(nc.vector.memset(m.brk[:], 0.0))
            do(nc.vector.tensor_tensor(m.brk[:, 1:T], dstf[:, 1:T], dstf[:, 0:T - 1], ALU.not_equal))
            do(nc.vector.tensor_scalar(m.brk[:], m.brk[:], -BIG, None, ALU.mult))
            v.wait_ge(ld, 16)
            do(nc.vector.tensor_copy(prevf[:], prev[:]))
            do(nc.vector.tensor_tensor(cont[:], dstf[:, 0:1], prevf[:], ALU.is_equal))
            do(nc.vector.tensor_tensor(mcol[:], dstf[:, 0:1], dstf[:, T - 1:T], ALU.is_equal))
            do(nc.vector.tensor_tensor(mcol[:], mcol[:], cont[:], ALU.mult))
            do(nc.vector.tensor_scalar(mcol[:], mcol[:], 1.0, BIG, ALU.subtract, ALU.mult))
            nc.vector.tensor_scalar(mrep[:], m.ones[:, 0:D], mcol[:], None, ALU.mult).then_inc(rep, 1)
            do(nc.vector.tensor_tensor(e[:], m.rowptr[:], m.deg[:], ALU.add))
            do(nc.vector.tensor_scalar(e[:], e[:], 1.0, 0.0, ALU.subtract, ALU.max))
            do(nc.vector.tensor_copy(m.endi[:], e[:]))

            def stream_of(out, x):
                do(nc.vector.tensor_scalar(out[:], x[:], 1.0 / T, 0.5 / T - 0.5, ALU.mult, ALU.add))
                do(nc.vector.tensor_copy(m.streami[:], out[:]))
                do(nc.vector.tensor_copy(out[:], m.streami[:]))
                do(nc.vector.scalar_tensor_tensor(rem[:], out[:], -float(T), x[:], ALU.mult, ALU.add))
                do(nc.vector.scalar_tensor_tensor(out[:], rem[:], float(T), out[:], ALU.is_ge, ALU.add))
                do(nc.vector.tensor_scalar(rem[:], rem[:], 0.0, None, ALU.is_lt))
                do(nc.vector.tensor_tensor(out[:], out[:], rem[:], ALU.subtract))
                do(nc.vector.tensor_copy(m.streami[:], out[:]))

            stream_of(s, m.rowptr)
            stream_of(q, e)
            do(nc.vector.tensor_tensor(m.nocarry[:], s[:], q[:], ALU.is_ge))
            do(nc.vector.tensor_scalar(m.nocarry[:], m.nocarry[:], -BIG, None, ALU.mult))
            do(nc.vector.tensor_scalar(m.some[:], m.deg[:], 0.0, None, ALU.is_gt))
            v.wait_ge(rowd, 1)
            do(nc.vector.tensor_copy(m.mrow[:], m.ps[0:D, 0, 0:P]))

        @b.tensor
        def _(pe):
            pe.wait_ge(rep, 1)
            nc.tensor.matmul(m.ps[0:D, 0, 0:P], mrep[:], m.ident[:], start=True, stop=True).then_inc(rowd, 1)


def edge_conv(nc, m, d, layer, out):
    with stage(nc, f"conv_{layer}") as (c, sem):
        sb = lambda n, s, t: c.enter_context(nc.sbuf_tensor(n + f"_c{layer}", s, t))
        wmr, we = sb("wmr", [D, 2 * D], F32), sb("we", [DE, D], F32)
        bias = sb("bias", [P, D], F32)
        xT = sb("xT", [D, 2, P], F32)
        ytab, root = sb("ytab", [P, NB, D], F32), sb("root", [P, NB, D], F32)
        ea = sb("ea", [DE, TURN, P], F32)
        idx = sb("idx", [P, 2, HALF[0]], I32)
        rows = sb("rows", [P, TURN, D], F32)
        run = sb("run", [P, TURN, D], F32)
        carT, carr, lastT = sb("carT", [D, P], F32), sb("carr", [P, D], F32), sb("lastT", [D, P], F32)
        rg, cg = sb("rg", [P, NB, D], F32), sb("cg", [P, NB, D], F32)
        wl, chain, turned, xcp = sem("conv_weights"), sem("conv_chain"), sem("x_turned"), sem("xT_copied")
        yd, yc, yst, eal = sem("y_product"), sem("y_copied"), sem("y_stored"), [sem("ea_a"), sem("ea_b")]
        staged, got = sem("index_staged"), [sem(f"g{j}") for j in range(TURN)]
        runz, turns = sem("run_cleared"), sem("turns")
        msg, ran, rst = sem("messages"), sem("running_max"), [sem("run_a"), sem("run_b")]
        lt, sc, ct, cc, cst = sem("last_turned"), sem("carries"), sem("carry_turned"), sem("carry_copied"), sem("carry_stored")
        rgd, cgd, res, ost = sem("ends_gathered"), sem("carries_gathered"), sem("result"), sem("out_stored")
        b = c.enter_context(nc.Block())
        cur = m.x if layer == 0 else m.y
        TN = T // TURN
        spans = ((0, HALF[0]), (HALF[0], HALF[1]))
        NBK = 6

        @b.sync
        def _(sp):
            sp.dma_start(wmr[:, 0:D], d.Wmsg[layer]).then_inc(wl, 16)
            sp.dma_start(wmr[:, D:2 * D], d.Wroot[layer]).then_inc(wl, 16)
            sp.dma_start(we[:], d.Wedge[layer]).then_inc(wl, 16)
            sp.dma_start(bias[:], d.bias[layer].rearrange("(a f) -> a f", a=1).to_broadcast([P, D])).then_inc(wl, 16)
            sp.wait_ge(yc, 2 * NB)
            sp.dma_start(d.yt.rearrange("(i p) f -> p i f", p=P), ytab[:]).then_inc(yst, 16)
            rdram = d.run.rearrange("(p t) f -> p t f", t=T)
            with sp.Fori(0, TN) as k:
                for h, (a, n) in enumerate(spans):
                    sp.wait_ge(msg, TURN * k + a + n)
                    sp.dma_start(ea[:, a:a + n, :], d.eaT[:, bass.ds(k * TURN + a, n), :]).then_inc(eal[h], 16)
            sp.wait_ge(yst, 16)
            sp.wait_ge(cc, 1)
            sp.dma_start(d.car, carr[:]).then_inc(cst, 16)
            sp.wait_ge(cst, 16)
            if layer == 1:
                sp.wait_ge(res, 1)
                sp.dma_start(out.rearrange("(i p) f -> p i f", p=P), m.x[:]).then_inc(ost, 16)
                sp.wait_ge(ost, 16)

        @b.gpsimd
        def _(g):
            g.wait_ge(yst, 16)
            g.sem_inc(msg, TURN)
            with g.Fori(0, TN) as k:
                for h, (a, n) in enumerate(spans):
                    g.wait_ge(msg, TURN * k + (a + n))
                    nc.gpsimd.tensor_copy(idx[:, h, 0:n], m.srci[:, bass.ds(k * TURN + a, n)]).then_inc(staged, 1)
                    g.wait_ge(staged, 2 * k + (h + 1))
                    g.sem_inc(turns, 1)
                    for j in range(n):
                        nc.gpsimd.indirect_dma_start(rows[:, a + j, :], None, d.yt,
                                                     bass.IndirectOffsetOnAxis(idx[:, h, j:j + 1], 0)).then_inc(got[a + j], 16)
            for r in rst:
                g.wait_ge(r, 16 * TN + 16)
            for i in range(NB):
                nc.gpsimd.indirect_dma_start(rg[:, i, :], None, d.run,
                                             bass.IndirectOffsetOnAxis(m.endi[:, i:i + 1], 0)).then_inc(rgd, 16)
            g.wait_ge(cst, 16)
            for i in range(NB):
                nc.gpsimd.indirect_dma_start(cg[:, i, :], None, d.car,
                                             bass.IndirectOffsetOnAxis(m.streami[:, i:i + 1], 0)).then_inc(cgd, 16)
            g.wait_ge(rgd, 16 * NB)
            g.wait_ge(cgd, 16 * NB)

        @b.scalar
        def _(a_):
            for i in range(NB):
                a_.wait_ge(turned, i + 1)
                if i >= 2:
                    a_.wait_ge(yd, i - 1)
                nc.scalar.activation(xT[:, i % 2, :], m.ps[0:D, i % 2, 0:P], ACT.Copy).then_inc(xcp, 1)
            rdram = d.run.rearrange("(p t) f -> p t f", t=T)
            a_.wait_ge(runz, 1)
            for h, (a, n) in enumerate(spans):
                a_.dma_start(rdram[:, a:a + n, :], run[:, a:a + n, :]).then_inc(rst[h], 16)
            with a_.Fori(0, TN) as k:
                for h, (a, n) in enumerate(spans):
                    a_.wait_ge(ran, TURN * k + (a + n + TURN))
                    a_.wait_ge(rst[h], 16 * k + 16)
                    a_.dma_start(rdram[:, bass.ds(k * TURN + a, n), :], run[:, a:a + n, :]).then_inc(rst[h], 16)
            for r in rst:
                a_.wait_ge(r, 16 * TN + 16)
            if layer == 1:
                square_root(nc, a_, m, 7, m.st2[:])

        @b.vector
        def _(v):
            do = Chain(v, chain)
            v.wait_ge(wl, 64)
            for i in range(NB):
                v.wait_ge(yd, i + 1)
                nc.vector.tensor_copy(ytab[:, i, :], m.ps[:, 2 + i % 2, 0:D]).then_inc(yc, 1)
                nc.vector.tensor_tensor(root[:, i, :], m.ps[:, 2 + i % 2, D:2 * D], bias[:], ALU.add).then_inc(yc, 1)
            nc.vector.memset(run[:], -BIG).then_inc(runz, 1)
            v.wait_ge(runz, 1)
            v.sem_inc(ran, TURN)
            with v.Fori(0, TN) as k:
                for h, (a, n) in enumerate(spans):
                    for j in range(a, a + n):
                        v.wait_ge(msg, TURN * k + (j + 1 + TURN))
                        if j == a:
                            v.wait_ge(rst[h], 16 * k + 16)
                        nc.vector.scalar_tensor_tensor(run[:, j, :], run[:, (j - 1) % TURN, :],
                                                       m.brk[:, bass.ds(k * TURN + j, 1)],
                                                       m.ps[:, j % NBK, 0:D], ALU.add, ALU.max).then_inc(ran, 1)
                        v.wait_ge(ran, TURN * k + (j + 1 + TURN))
            v.wait_ge(lt, 1)
            do(nc.vector.tensor_copy(lastT[:], m.ps[0:D, 6, 0:P]))
            do(nc.vector.memset(carT[:, 0:1], -BIG))
            nc.vector.tensor_tensor_scan(carT[:, 1:P], m.mrow[:, 0:P - 1], lastT[:, 0:P - 1], -BIG,
                                         ALU.add, ALU.max).then_inc(sc, 1)
            v.wait_ge(ct, 1)
            nc.vector.tensor_copy(carr[:], m.ps[:, 7, 0:D]).then_inc(cc, 1)
            v.wait_ge(rgd, 16 * NB)
            v.wait_ge(cgd, 16 * NB)
            do(nc.vector.tensor_tensor(cg[:], cg[:], bc_last(m.nocarry[:], D), ALU.add))
            do(nc.vector.tensor_tensor(rg[:], rg[:], cg[:], ALU.max))
            do(nc.vector.tensor_tensor(rg[:], rg[:], bc_last(m.some[:], D), ALU.mult))
            do(nc.vector.tensor_tensor(rg[:], rg[:], root[:], ALU.add))
            do(nc.vector.scalar_tensor_tensor(m.y[:], rg[:], 0.01, rg[:], ALU.mult, ALU.max))
            if layer == 1:
                do(nc.vector.tensor_tensor(m.y[:], m.y[:], m.x[:], ALU.add))
                layer_norm(nc, v, do, m, m.x, m.y, rg, 7)
                v.sem_inc(res, 1)

        @b.tensor
        def _(pe):
            pe.wait_ge(wl, 64)
            for i in range(NB + 1):
                if i < NB:
                    if i >= 2:
                        pe.wait_ge(xcp, i - 1)
                    nc.tensor.transpose(m.ps[0:D, i % 2, 0:P], cur[:, i, :], m.ident[:]).then_inc(turned, 1)
                if i >= 1:
                    q = i - 1
                    pe.wait_ge(xcp, q + 1)
                    if q >= 2:
                        pe.wait_ge(yc, 2 * (q - 1))
                    nc.tensor.matmul(m.ps[:, 2 + q % 2, 0:2 * D], xT[:, q % 2, :], wmr[:], start=True,
                                     stop=True).then_inc(yd, 1)
            pe.wait_ge(xcp, NB)
            pe.wait_ge(yc, 2 * NB)
            with pe.Fori(0, TN) as k:
                for h, (a, n) in enumerate(spans):
                    pe.wait_ge(eal[h], 16 * k + 16)
                    for j in range(a, a + n):
                        pe.wait_ge(got[j], 16 * k + 16)
                        pe.wait_ge(ran, TURN * k + (j + TURN - 4))
                        nc.tensor.matmul(m.ps[:, j % NBK, 0:D], ea[:, j, :], we[:], start=True, stop=False)
                        nc.tensor.matmul(m.ps[:, j % NBK, 0:D], m.ident[:], rows[:, j, :], start=False,
                                         stop=True).then_inc(msg, 1)
            pe.wait_ge(ran, T + TURN)
            nc.tensor.transpose(m.ps[0:D, 6, 0:P], run[:, TURN - 1, :], m.ident[:]).then_inc(lt, 1)
            pe.wait_ge(sc, 1)
            nc.tensor.transpose(m.ps[:, 7, 0:D], carT[:], m.ident[0:D, 0:D]).then_inc(ct, 1)


def program(nc, x, src_s, dst_s, w_s, src_rows, dst_rows, eaT, W0, b0, W1, b1, W2, b2,
            Wm1, We1, Wr1, c1, Wm2, We2, Wr2, c2, out):
    dram = lambda n, s, t: nc.dram_tensor(n, s, t).ap()
    d = Names()
    d.x, d.src_s, d.dst_s, d.w_s, d.src_rows, d.dst_rows, d.eaT = x, src_s, dst_s, w_s, src_rows, dst_rows, eaT
    d.W0, d.b0, d.W1, d.b1, d.W2, d.b2 = W0, b0, W1, b1, W2, b2
    d.Wmsg, d.Wedge, d.Wroot, d.bias = [Wm1, Wm2], [We1, We2], [Wr1, Wr2], [c1, c2]
    d.ptr, d.off = dram("ptr", [16 * NB], F32), dram("off", [SG * P], I32)
    d.table, d.rec = dram("table", [P * BT, 4], I32), dram("records", [P, T, 4], I32)
    d.xt, d.yt = dram("x_table", [NP, D], F32), dram("y_table", [NP, D], F32)
    d.run, d.car = dram("run_max", [EP, D], F32), dram("carries", [P, D], F32)
    with ExitStack() as c:
        sb = lambda n, s, t: c.enter_context(nc.sbuf_tensor(n, s, t))
        m = Names()
        m.ps = c.enter_context(nc.psum_tensor("ps", [P, 8, 512], F32))
        m.x = sb("x_sb", [P, NB, D], F32)
        m.row, m.row16, m.col = sb("row", [P, 256], F32), sb("row16", [P, 256], F16), sb("col", [P, 1], F32)
        m.ident, m.ident16 = sb("ident", [P, P], F32), sb("ident16", [P, P], F16)
        m.upper, m.neglow16 = sb("upper", [P, P], F32), sb("neglow16", [P, P], F16)
        m.ones, m.ones16 = sb("ones", [P, P], F32), sb("ones16", [P, P], F16)
        m.deg, m.dinv, m.rowptr = sb("deg", [P, NB], F32), sb("dinv", [P, NB], F32), sb("rowptr", [P, NB], F32)
        m.padcol = sb("padcol", [P, NB], F32)
        m.sd, m.nt = sb("sd", [P, NB], F32), sb("nt", [P, NB], F32)
        m.var_ready, m.root_done = c.enter_context(nc.semaphore("variances")), c.enter_context(nc.semaphore("roots"))
        m.st1, m.st2 = sb("st1", [P, NB], F32), sb("st2", [P, NB], F32)
        m.ki, m.kf, m.kg = sb("ki", [P, 1], I32), sb("kf", [P, 1], F32), sb("kg", [P, 1], F32)
        m.bucket = sb("bucket", [1, BT], I32)
        with ExitStack() as with_at:
            m.at = with_at.enter_context(nc.sbuf_tensor("at", [P, NB, NP], F16))
            with ExitStack() as k:
                m.keyT = k.enter_context(nc.sbuf_tensor("keyT", [P, SG * P], F32))
                m.neglowT = k.enter_context(nc.sbuf_tensor("neglowT", [P, SG * P], F32))
                m.off = k.enter_context(nc.sbuf_tensor("off_sb", [1, SG * P], I32))
                prepare(nc, m, d)
                bucket_ranks(nc, m, d)
                build_counts(nc, m, d)
            appnp(nc, m, d)
            m.y = with_at.enter_context(nc.sbuf_tensor("y_sb", [P, NB, D], F32))
            sage(nc, m, d, 0)
            sage(nc, m, d, 1)
        m.y = sb("y2_sb", [P, NB, D], F32)
        m.srci = sb("srci_sb", [P, T], I32)
        m.brk = sb("brk", [P, T], F32)
        m.mrow = sb("mrow", [D, P], F32)
        m.endi, m.streami = sb("endi", [P, NB], I32), sb("streami", [P, NB], I32)
        m.nocarry, m.some = sb("nocarry", [P, NB], F32), sb("some", [P, NB], F32)
        weighted_sum(nc, m, d)
        edge_masks(nc, m, d)
        edge_conv(nc, m, d, 0, out)
        edge_conv(nc, m, d, 1, out)


def kernel(x, src, dst, edge_attr_32, edge_weight, L1_gnn_W0, L1_gnn_b0, L1_gnn_W1, L1_gnn_b1, L1_gnn_W2,
           L1_gnn_b2, L3_gnn_W1_msg, L3_gnn_W1_edge, L3_gnn_W1_root, L3_gnn_b1, L3_gnn_W2_msg,
           L3_gnn_W2_edge, L3_gnn_W2_root, L3_gnn_b2):
    import numpy as np
    import concourse.bacc as bacc
    from concourse.bass_utils import run_bass_kernel_spmd

    def padded(a, rows, value=0):
        a = np.asarray(a)
        out = np.full((rows,) + a.shape[1:], value, a.dtype)
        out[:a.shape[0]] = a
        return out

    s, t = padded(src, EP + P, NP - 1), padded(dst, EP + P, NP - 1)
    ea = padded(edge_attr_32, EP).reshape(P, T, DE)
    arrays = {
        "x": padded(x, NP), "src_s": s[:EP].reshape(P, T), "dst_s": t[:EP].reshape(P, T),
        "w_s": padded(edge_weight, EP).reshape(P, T),
        "src_rows": s.reshape(T + 1, P), "dst_rows": t.reshape(T + 1, P),
        "eaT": np.ascontiguousarray(ea.transpose(2, 1, 0)),
        "W0": L1_gnn_W0, "b0": L1_gnn_b0, "W1": L1_gnn_W1, "b1": L1_gnn_b1, "W2": L1_gnn_W2, "b2": L1_gnn_b2,
        "Wm1": L3_gnn_W1_msg, "We1": L3_gnn_W1_edge, "Wr1": L3_gnn_W1_root, "c1": L3_gnn_b1,
        "Wm2": L3_gnn_W2_msg, "We2": L3_gnn_W2_edge, "Wr2": L3_gnn_W2_root, "c2": L3_gnn_b2,
    }
    nc = bacc.Bacc("TRN2", target_bir_lowering=False, num_devices=1)
    feeds, args = {}, []
    for name, a in arrays.items():
        a = np.ascontiguousarray(a)
        feeds["in_" + name] = a
        args.append(nc.dram_tensor("in_" + name, a.shape, mybir.dt.from_np(a.dtype), kind="ExternalInput").ap())
    args.append(nc.dram_tensor("out", (NP, D), F32, kind="ExternalOutput").ap())
    program(nc, *args)
    got = run_bass_kernel_spmd(nc, [feeds], core_ids=[0])
    return got.results[0]["out"][:N]
```

```python
from contextlib import ExitStack, contextmanager

import concourse.bass as bass
from concourse import mybir

F32 = mybir.dt.float32
F16 = mybir.dt.float16
I32 = mybir.dt.int32
ALU = mybir.AluOpType
ACT = mybir.ActivationFunctionType
AX = mybir.AxisListType
RMAX = bass.bass_isa.ReduceOp.max

P = 128
N, D, E, DE = 3125, 96, 50000, 32
NB = -(-N // P)
NP = NB * P
T = -(-E // P)
EP = T * P
W = 8
NW = -(-N // W)
SLOTS = -(-(T + NW) // 16) * 16
SG = -(-(SLOTS + 8) // P)
BT = -(-(T + NB) // 16) * 16
KEYS = NB * W
STEPS, ALPHA = 16, 0.1
GROUP = 4
GROUPS = [(a, min(GROUP, NB - a)) for a in range(0, NB, GROUP)]
NG = len(GROUPS)
ENDS = 5
HALF = (9, 8)
TURN = sum(HALF)
assert T % TURN == 0
EPS = 1e-5
BIG = 1.0e30


@contextmanager
def stage(nc, tag):
    used = []

    def sem(name):
        used.append(nc.alloc_semaphore(f"{name}_{tag}"))
        return used[-1]

    with ExitStack() as c:
        yield c, sem
    nc.clear_and_free_semaphores(used)
    nc.all_engine_barrier()


class Names:
    pass


class Chain:

    def __init__(self, eng, sem):
        self.eng, self.sem, self.n = eng, sem, 0

    def __call__(self, ins):
        self.n += 1
        ins.then_inc(self.sem, 1)
        self.eng.wait_ge(self.sem, self.n)


def carver(at):
    flat, at_byte = at[:].rearrange("p i n -> p (i n)"), [0]

    def take(name, shape, dtype):
        count = 1
        for n in shape[1:]:
            count *= n
        size = 2 if dtype == F16 else 4
        start = at_byte[0] // 2
        at_byte[0] += -(-count * size // 64) * 64
        part = flat[0:shape[0], start:start + count * size // 2]
        part = part if dtype == F16 else part.bitcast(dtype)
        return part.rearrange("p (a b) -> p a b", b=shape[2]) if len(shape) == 3 else part

    return take


def bc_mid(ap, n):
    return ap.unsqueeze(1).to_broadcast([ap.shape[0], n, ap.shape[1]])


def blocks_of(ap):
    return ap.rearrange("p (i f) -> p i f", f=D)


def bc_last(ap, n):
    return ap.unsqueeze(2).to_broadcast([ap.shape[0], ap.shape[1], n])


def square_root(nc, act, m, n, x):
    act.wait_ge(m.var_ready, n)
    nc.scalar.activation(m.sd[:], x, ACT.Sqrt).then_inc(m.root_done, 1)


def inverse_root(nc, v, do, m, n, x):
    v.wait_ge(m.root_done, n)
    do(nc.vector.reciprocal(m.sd[:], m.sd[:]))
    do(nc.vector.tensor_tensor(m.nt[:], m.sd[:], m.sd[:], ALU.mult))
    do(nc.vector.tensor_tensor(m.nt[:], m.nt[:], x, ALU.mult))
    do(nc.vector.tensor_scalar(m.nt[:], m.nt[:], -0.5, 1.5, ALU.mult, ALU.add))
    do(nc.vector.tensor_tensor(x, m.sd[:], m.nt[:], ALU.mult))


def layer_norm(nc, v, do, m, out, t, sq, n):
    centre(nc, do, m, t, sq, slice(0, NB))
    scale_by_deviation(nc, v, do, m, out, t, n)


def centre(nc, do, m, t, sq, blk):
    do(nc.vector.tensor_reduce(m.st1[:, blk], t[:, blk, :], AX.X, ALU.add))
    do(nc.vector.tensor_scalar(m.st1[:, blk], m.st1[:, blk], 1.0 / D, None, ALU.mult))
    do(nc.vector.tensor_tensor(t[:, blk, :], t[:, blk, :], bc_last(m.st1[:, blk], D), ALU.subtract))
    do(nc.vector.tensor_tensor(sq[:, blk, :], t[:, blk, :], t[:, blk, :], ALU.mult))
    do(nc.vector.tensor_reduce(m.st2[:, blk], sq[:, blk, :], AX.X, ALU.add))


def scale_by_deviation(nc, v, do, m, out, t, n):
    nc.vector.tensor_scalar(m.st2[:], m.st2[:], 1.0 / D, EPS, ALU.mult, ALU.add).then_inc(m.var_ready, 1)
    inverse_root(nc, v, do, m, n, m.st2[:])
    do(nc.vector.tensor_tensor(out[:], t[:], bc_last(m.st2[:], D), ALU.mult))


def scale_of(nc, do, m, big, scale, unscale):
    k = m.ki
    do(nc.vector.tensor_scalar(k[:, 0:1], big.bitcast(I32), 23, None, ALU.logical_shift_right))
    do(nc.vector.tensor_copy(m.kf[:], k[:, 0:1]))
    do(nc.vector.tensor_scalar(m.kf[:], m.kf[:], 40.0, None, ALU.max))
    do(nc.vector.tensor_scalar(m.kg[:], m.kf[:], -1.0, 254.0 + 13.0, ALU.mult, ALU.add))
    do(nc.vector.tensor_copy(k[:, 0:1], m.kg[:]))
    do(nc.vector.tensor_scalar(scale.bitcast(I32), k[:, 0:1], 23, None, ALU.logical_shift_left))
    do(nc.vector.tensor_scalar(m.kg[:], m.kf[:], 13.0, None, ALU.subtract))
    do(nc.vector.tensor_copy(k[:, 0:1], m.kg[:]))
    do(nc.vector.tensor_scalar(unscale.bitcast(I32), k[:, 0:1], 23, None, ALU.logical_shift_left))


def prepare(nc, m, d):
    with stage(nc, "prepare") as (c, sem):
        sb = carver(m.at)
        dsti = sb("dsti", [P, T], I32)
        rowi = sb("rowi", [P, 256], I32)
        coli = sb("coli", [P, 1], I32)
        lo16, hi16 = sb("lo16", [P, T], F16), sb("hi16", [P, T], F16)
        inti = sb("inti", [P, T], I32)
        onehi = sb("onehi", [P, T * NB], F16)
        onelo = sb("onelo", [P, TURN, P], F16)
        zero16 = sb("zero16", [P, P], F16)
        totincl = sb("totincl", [P, NB], F32)
        srow = sb("srow", [P, 16 * NB], F32)
        sint = sb("sint", [P, 16 * NB], I32)
        first, ceil = sb("first", [P, NW], F32), sb("ceil", [P, NW], F32)
        firsti = sb("firsti", [P, NW + 1], I32)
        cnt, pos, dlt = sb("cnt", [P, NW], F32), sb("pos", [P, NW], F32), sb("dlt", [P, NW], F32)
        junk = sb("junk", [P, NW], F32)
        jcol, bsum, tsum = sb("jcol", [P, SG], F32), sb("bsum", [P, SG], F32), sb("tsum", [P, SG], F32)
        jcoli = sb("jcoli", [P, SG], I32)
        b8 = sb("b8", [P, SG], F32)
        b8i, ti = sb("b8i", [P, SG], I32), sb("ti", [P, SG], I32)
        dg, sg = sb("dg", [P, SG, P], I32), sb("sg", [P, SG, P], I32)
        rel, ok = sb("rel", [P, SG, P], F32), sb("ok", [P, SG, P], F32)
        hi8, lof = sb("hi8", [P, SG, P], F32), sb("lof", [P, SG, P], F32)
        edges, nodes = sem("edges_loaded"), sem("x_loaded")
        iotas, consts, chain = sem("iotas"), sem("constants"), sem("vector_chain")
        lows, free = sem("low_onehots"), sem("low_buffer_free")
        zeroed, counted = sem("psum_zeroed"), sem("degrees_counted")
        degs, prefixed, ptrs = sem("degrees"), sem("prefixes"), sem("row_pointers")
        stored, read = sem("pointers_stored"), sem("pointers_read")
        slots, rows, offs = sem("slot_rows"), sem("slot_edges"), sem("offsets_stored")
        offr, keys, turned = sem("offsets_read"), sem("slot_keys"), sem("keys_turned")
        b = c.enter_context(nc.Block())

        @b.sync
        def _(sp):
            sp.dma_start(dsti[:], d.dst_s).then_inc(edges, 16)
            sp.dma_start(m.x[:], d.x.rearrange("(i p) f -> p i f", p=P)).then_inc(nodes, 16)
            sp.wait_ge(ptrs, 1)
            sp.dma_start(d.ptr.rearrange("(i q) -> q i", q=16), m.rowptr[0:P:8, :], allow_slow_non_contiguous=True).then_inc(stored, 16)
            sp.wait_ge(stored, 16)
            sp.dma_start(srow[:], d.ptr.rearrange("(a n) -> a n", a=1).to_broadcast([P, 16 * NB])).then_inc(read, 16)
            sp.wait_ge(slots, 1)
            sp.dma_start(d.off.rearrange("(g p) -> p g", p=P), b8i[:], allow_slow_non_contiguous=True).then_inc(offs, 16)
            sp.wait_ge(offs, 16)
            sp.dma_start(m.off[:], d.off.rearrange("(a n) -> a n", a=1)).then_inc(offr, 16)
            sp.wait_ge(nodes, 16)
            sp.wait_ge(offr, 16)

        @b.gpsimd
        def _(g):
            nc.gpsimd.iota(rowi[:], [[1, 256]], 0, 0).then_inc(iotas, 1)
            nc.gpsimd.iota(coli[:], [[0, 1]], 0, 1).then_inc(iotas, 1)
            nc.gpsimd.iota(jcoli[:], [[P, SG]], 0, 1).then_inc(iotas, 1)
            g.wait_ge(slots, 1)
            for k in range(SG):
                nc.gpsimd.indirect_dma_start(dg[:, k, :], None, d.dst_rows,
                                             bass.IndirectOffsetOnAxis(ti[:, k:k + 1], 0)).then_inc(rows, 16)
                nc.gpsimd.indirect_dma_start(sg[:, k, :], None, d.src_rows,
                                             bass.IndirectOffsetOnAxis(ti[:, k:k + 1], 0)).then_inc(rows, 16)
            g.wait_ge(rows, 32 * SG)

        @b.vector
        def _(v):
            do = Chain(v, chain)
            v.wait_ge(iotas, 3)
            do(nc.vector.tensor_copy(m.row[:], rowi[:]))
            do(nc.vector.tensor_copy(m.row16[:], rowi[:]))
            do(nc.vector.tensor_copy(m.col[:], coli[:]))
            do(nc.vector.tensor_copy(jcol[:], jcoli[:]))
            do(nc.vector.tensor_scalar(m.ident[:], m.row[:, 0:P], m.col[:], None, ALU.is_equal))
            do(nc.vector.tensor_scalar(m.ident16[:], m.row[:, 0:P], m.col[:], None, ALU.is_equal))
            do(nc.vector.tensor_scalar(m.upper[:], m.row[:, 0:P], m.col[:], None, ALU.is_gt))
            do(nc.vector.tensor_scalar(m.neglow16[:], m.row[:, 0:P], m.col[:], -1.0, ALU.is_le, ALU.mult))
            do(nc.vector.memset(m.ones[:], 1.0))
            do(nc.vector.memset(m.ones16[:], 1.0))
            nc.vector.memset(zero16[:], 0.0).then_inc(consts, 1)
            do(nc.vector.memset(m.padcol[:], 0.0))
            do(nc.vector.tensor_scalar(m.padcol[:, NB - 1:NB], m.col[:], float(N - (NB - 1) * P), None, ALU.is_ge))
            v.wait_ge(edges, 16)
            do(nc.vector.tensor_scalar(inti[:], dsti[:], 7, None, ALU.logical_shift_right))
            do(nc.vector.tensor_copy(hi16[:], inti[:]))
            do(nc.vector.tensor_scalar(inti[:], dsti[:], P - 1, None, ALU.bitwise_and))
            do(nc.vector.tensor_copy(lo16[:], inti[:]))
            do(nc.vector.tensor_tensor(onehi[:].rearrange("p (t i) -> p t i", i=NB), bc_last(hi16[:], NB),
                                       bc_mid(m.row16[:, 0:NB], T), ALU.is_equal))
            with v.Fori(0, T // TURN) as k:
                for h, (a, n) in enumerate(((0, HALF[0]), (HALF[0], HALF[1]))):
                    v.wait_ge(free, 2 * k + h + 1)
                    nc.vector.tensor_tensor(onelo[:, a:a + n, :], bc_last(lo16[:, bass.ds(k * TURN + a, n)], P),
                                            bc_mid(m.row16[:, 0:P], n), ALU.is_equal).then_inc(lows, 1)
            v.wait_ge(counted, 1)
            do(nc.vector.tensor_copy(m.deg[:], m.ps[:, 0, 0:NB]))
            nc.vector.tensor_scalar(m.dinv[:], m.deg[:], 1.0, None, ALU.add).then_inc(m.var_ready, 1)
            inverse_root(nc, v, do, m, 1, m.dinv[:])
            v.sem_inc(degs, 1)
            v.wait_ge(prefixed, 1)
            do(nc.vector.tensor_tensor_scan(totincl[:], m.ones[:, 0:NB], m.ps[:, 2, 0:NB], 0.0, ALU.mult, ALU.add))
            do(nc.vector.tensor_tensor(totincl[:], totincl[:], m.ps[:, 2, 0:NB], ALU.subtract))
            nc.vector.tensor_tensor(m.rowptr[:], totincl[:], m.ps[:, 1, 0:NB], ALU.add).then_inc(ptrs, 1)
            v.wait_ge(read, 16)
            do(nc.vector.tensor_copy(sint[:], srow[:]))
            do(nc.vector.tensor_scalar(firsti[:, 0:NW], sint[:, 0:NW], 7, None, ALU.logical_shift_right))
            do(nc.vector.tensor_copy(first[:], firsti[:, 0:NW]))
            do(nc.vector.tensor_scalar(srow[:], srow[:], float(P - 1), None, ALU.add))
            do(nc.vector.tensor_copy(sint[:], srow[:]))
            do(nc.vector.tensor_scalar(firsti[:, 0:NW], sint[:, 1:NW + 1], 7, None, ALU.logical_shift_right))
            do(nc.vector.tensor_copy(ceil[:], firsti[:, 0:NW]))
            do(nc.vector.tensor_tensor(cnt[:], ceil[:], first[:], ALU.subtract))
            do(nc.vector.tensor_scalar(cnt[:], cnt[:], 1.0, None, ALU.max))
            do(nc.vector.memset(junk[:], 1.0))
            do(nc.vector.tensor_tensor_scan(pos[:], junk[:], cnt[:], 0.0, ALU.mult, ALU.add))
            do(nc.vector.tensor_tensor(pos[:], pos[:], cnt[:], ALU.subtract))
            do(nc.vector.tensor_tensor(first[:], first[:], pos[:], ALU.subtract))
            do(nc.vector.tensor_copy(dlt[:], first[:]))
            do(nc.vector.tensor_tensor(dlt[:, 1:NW], first[:, 1:NW], first[:, 0:NW - 1], ALU.subtract))
            for k in range(SG):
                do(nc.vector.tensor_scalar(junk[:], pos[:], jcol[:, k:k + 1], 0.0, ALU.is_le, ALU.add,
                                           accum_out=bsum[:, k:k + 1]))
                do(nc.vector.scalar_tensor_tensor(junk[:], pos[:], jcol[:, k:k + 1], dlt[:], ALU.is_le, ALU.mult,
                                                  accum_out=tsum[:, k:k + 1]))
            do(nc.vector.tensor_tensor(tsum[:], tsum[:], jcol[:], ALU.add))
            do(nc.vector.tensor_scalar(tsum[:], tsum[:], float(T), None, ALU.min))
            do(nc.vector.tensor_scalar(b8[:], bsum[:], float(W), -float(W), ALU.mult, ALU.add))
            do(nc.vector.tensor_copy(b8i[:], b8[:]))
            nc.vector.tensor_copy(ti[:], tsum[:]).then_inc(slots, 1)
            v.wait_ge(rows, 32 * SG)
            do(nc.vector.tensor_copy(rel[:], dg[:]))
            do(nc.vector.tensor_tensor(rel[:], rel[:], bc_last(b8[:], P), ALU.subtract))
            do(nc.vector.tensor_scalar(ok[:], rel[:], 0.0, None, ALU.is_ge))
            do(nc.vector.scalar_tensor_tensor(ok[:], rel[:], float(W), ok[:], ALU.is_lt, ALU.mult))
            do(nc.vector.tensor_scalar(dg[:], sg[:], 7, 3, ALU.logical_shift_right, ALU.logical_shift_left))
            do(nc.vector.tensor_copy(hi8[:], dg[:]))
            do(nc.vector.scalar_tensor_tensor(rel[:], rel[:], 1.0, hi8[:], ALU.add, ALU.add))
            do(nc.vector.tensor_tensor(rel[:], rel[:], ok[:], ALU.mult))
            do(nc.vector.tensor_scalar(rel[:], rel[:], -1.0, None, ALU.add))
            do(nc.vector.tensor_scalar(dg[:], sg[:], P - 1, None, ALU.bitwise_and))
            nc.vector.tensor_copy(lof[:], dg[:]).then_inc(keys, 1)
            v.wait_ge(turned, 1)
            do(nc.vector.tensor_copy(m.keyT[:], m.ps[:, 4:6, :].rearrange("p a b -> p (a b)")[:, 0:SG * P]))
            do(nc.vector.tensor_copy(m.lowT[:], m.ps[:, 6:8, :].rearrange("p a b -> p (a b)")[:, 0:SG * P]))

        @b.scalar
        def _(a):
            square_root(nc, a, m, 1, m.dinv[:])

        @b.tensor
        def _(pe):
            pe.wait_ge(consts, 1)
            nc.tensor.matmul(m.ps[:, 0, 0:NB], zero16[:], zero16[:, 0:NB], start=True, stop=False,
                             skip_group_check=True).then_inc(zeroed, 1)
            pe.wait_ge(zeroed, 1)
            pe.sem_inc(free, 2)
            with pe.Fori(0, T // TURN) as k:
                for h, (a, n) in enumerate(((0, HALF[0]), (HALF[0], HALF[1]))):
                    pe.wait_ge(lows, 2 * k + h + 1)
                    for j in range(a, a + n):
                        mm = nc.tensor.matmul(m.ps[:, 0, 0:NB], onelo[:, j, :],
                                              onehi[:, bass.ds((k * TURN + j) * NB, NB)],
                                              start=False, stop=False, skip_group_check=True)
                    mm.then_inc(free, 1)
            pe.wait_ge(free, 2 + 2 * (T // TURN))
            pe.sem_inc(counted, 1)
            pe.wait_ge(degs, 1)
            nc.tensor.matmul(m.ps[:, 1, 0:NB], m.upper[:], m.deg[:], start=True, stop=True)
            nc.tensor.matmul(m.ps[:, 2, 0:NB], m.ones[:], m.deg[:], start=True, stop=True).then_inc(prefixed, 1)
            pe.wait_ge(keys, 1)
            for k in range(SG):
                nc.tensor.transpose(m.ps[:, 4 + k // 4, (k % 4) * P:(k % 4 + 1) * P], rel[:, k, :], m.ident[:])
                mm = nc.tensor.transpose(m.ps[:, 6 + k // 4, (k % 4) * P:(k % 4 + 1) * P], lof[:, k, :], m.ident[:])
            mm.then_inc(turned, 1)


def build_counts(nc, m, d):
    with stage(nc, "build") as (c, sem):
        sb = lambda n, s, t: c.enter_context(nc.sbuf_tensor(n, s, t))
        RING, LEAD, PER, PAIRS = 8, 4, 16, 4
        onekey = sb("onekey", [P, RING, KEYS], F16)
        oneplace = sb("oneplace", [P, RING, P], F16)
        counts = sb("counts", [P, PAIRS, 2, KEYS], F16)
        cleared = sem("counts_cleared")
        onehot, product = sem("onehots"), sem("slot_products")
        copied, added = sem("pairs_copied"), sem("slots_added")
        b = c.enter_context(nc.Block())

        @b.gpsimd
        def _(g):
            nc.gpsimd.memset(m.at[:, NB // 2:NB, :], 0.0).then_inc(cleared, 1)

        @b.scalar
        def _(a):
            for n in range(SLOTS // 2):
                a.wait_ge(product, 2 * n + 2)
                if n >= PAIRS:
                    a.wait_ge(added, 2 * (n - PAIRS) + 2)
                nc.scalar.activation(counts[:, n % PAIRS, :, :],
                                     m.ps[:, n % 8, :].rearrange("p (a k) -> p a k", a=2)[:, :, 0:KEYS],
                                     ACT.Copy).then_inc(copied, 1)

        @b.vector
        def _(v):
            nc.vector.memset(m.at[:, 0:NB // 2, :], 0.0).then_inc(cleared, 1)

            def onehots(s):
                if s >= RING:
                    v.wait_ge(product, s - RING + 1)
                nc.vector.tensor_scalar(onekey[:, s % RING, :], m.row16[:, 0:KEYS], m.keyT[:, s:s + 1], None,
                                        ALU.is_equal)
                nc.vector.tensor_scalar(oneplace[:, s % RING, :], m.row16[:, 0:P], m.lowT[:, s:s + 1], None,
                                        ALU.is_equal).then_inc(onehot, 1)

            for s in range(LEAD):
                onehots(s)
            v.wait_ge(cleared, 2)
            regs = [v.alloc_register(f"window{j}") for j in range(PER)]
            for s in range(SLOTS):
                if s % PER == 0:
                    v.load(regs, m.off[0:1, s:s + PER])
                if s + LEAD < SLOTS:
                    onehots(s + LEAD)
                window = m.at[:, :, bass.ds(v.snap(regs[s % PER], min_val=0, max_val=(NW - 1) * W), W)]
                v.wait_ge(copied, s // 2 + 1)
                if s >= 1:
                    v.wait_ge(added, s)
                nc.vector.tensor_tensor(window, window,
                                        counts[:, s // 2 % PAIRS, s % 2, :].rearrange("p (i w) -> p i w", w=W),
                                        ALU.add).then_inc(added, 1)

        @b.tensor
        def _(pe):
            for s in range(SLOTS):
                pe.wait_ge(onehot, s + 1)
                if s >= 16 and s % 2 == 0:
                    pe.wait_ge(copied, s // 2 - 8 + 1)
                nc.tensor.matmul(m.ps[:, s // 2 % 8, 256 * (s % 2):256 * (s % 2) + KEYS], oneplace[:, s % RING, :],
                                 onekey[:, s % RING, :], start=True, stop=True).then_inc(product, 1)


def bucket_ranks(nc, m, d):
    with stage(nc, "ranks") as (c, sem):
        sb = carver(m.at)
        inti, hii = sb("inti", [P, T], I32), sb("hii", [P, T], I32)
        dsti, srci = sb("dsti", [P, T], I32), sb("srci", [P, T], I32)
        w, rec = sb("w", [P, T], F32), sb("rec", [P, T, 4], I32)
        hi = sb("hi", [P, T], F16)
        onehi = sb("onehi", [P, NB, T], F16)
        mask = sb("mask", [P, 2, T], I32)
        run, acc, tmp = sb("run", [P, 2, T], F32), sb("acc", [P, T], F32), sb("tmp", [P, T], F32)
        one = sb("one_row", [P, T], F32)
        cnt, tiles, base = sb("cnt", [P, NB], F32), sb("tiles", [P, NB], F32), sb("base", [P, NB], F32)
        cnti = sb("cnti", [P, NB], I32)
        rank = sb("rank", [P, T], I32)
        zeros = sb("zeros", [P, BT * 4 // 16], I32)
        chain, counted, summed = sem("rank_chain"), sem("row_counts"), sem("count_sums")
        cleared, tabz = sem("zeros_made"), sem("table_cleared")
        ld, made, stored = sem("edges_loaded"), sem("records_made"), sem("records_stored")
        b = c.enter_context(nc.Block())

        @b.sync
        def _(sp):
            sp.dma_start(srci[:], d.src_s).then_inc(ld, 16)
            sp.dma_start(dsti[:], d.dst_s).then_inc(ld, 16)
            sp.dma_start(w[:], d.w_s).then_inc(ld, 16)
            sp.wait_ge(cleared, 1)
            for q in range(16):
                n = BT * 4 // 16
                sp.dma_start(d.table.rearrange("(p t) c -> p (t c)", p=P)[:, q * n:(q + 1) * n], zeros[:]).then_inc(tabz, 16)
            sp.wait_ge(made, 1)
            sp.dma_start(d.rec, rec[:]).then_inc(stored, 16)
            sp.wait_ge(tabz, 256)
            sp.wait_ge(stored, 16)

        @b.vector
        def _(v):
            do = Chain(v, chain)
            nc.vector.memset(zeros[:], 0).then_inc(cleared, 1)
            do(nc.vector.memset(one[:], 1.0))
            v.wait_ge(ld, 48)
            do(nc.vector.tensor_scalar(hii[:], srci[:], 7, None, ALU.logical_shift_right))
            do(nc.vector.tensor_copy(hi[:], hii[:]))
            for i in range(NB):
                ins = nc.vector.tensor_scalar(onehi[:, i, :], hi[:], float(i), 0.0, ALU.is_equal, ALU.add,
                                              accum_out=cnt[:, i:i + 1])
            ins.then_inc(counted, 1)
            v.wait_ge(counted, 1)
            do(nc.vector.tensor_scalar(inti[:], srci[:], P - 1, None, ALU.bitwise_and))
            nc.vector.tensor_copy(rec[:, :, 0:1], dsti[:].unsqueeze(2))
            nc.vector.tensor_copy(rec[:, :, 1:2], inti[:].unsqueeze(2))
            do(nc.vector.tensor_copy(rec[:, :, 2:3], w[:].bitcast(I32).unsqueeze(2)))
            v.wait_ge(summed, 1)
            do(nc.vector.tensor_scalar(tiles[:], m.ps[:, 1, 0:NB], float(P - 1), None, ALU.add))
            do(nc.vector.tensor_copy(cnti[:], tiles[:]))
            do(nc.vector.tensor_scalar(cnti[:], cnti[:], 7, None, ALU.logical_shift_right))
            do(nc.vector.tensor_copy(tiles[:], cnti[:]))
            do(nc.vector.tensor_tensor_scan(base[:], one[:, 0:NB], tiles[:], 0.0, ALU.mult, ALU.add))
            do(nc.vector.tensor_tensor(base[:], base[:], tiles[:], ALU.subtract))
            do(nc.vector.tensor_copy(m.first_tile[:], base[0:1, :]))
            do(nc.vector.tensor_scalar(base[:], base[:], float(P), -1.0, ALU.mult, ALU.add))
            do(nc.vector.tensor_tensor(base[:], base[:], m.ps[:, 0, 0:NB], ALU.add))
            for i in range(NB + 1):
                if i < NB:
                    nc.vector.tensor_scalar(mask[:, i % 2, :], hii[:], float(i), None, ALU.is_equal)
                if i >= 1:
                    do(nc.vector.copy_predicated(acc[:], mask[:, (i - 1) % 2, :], run[:, (i - 1) % 2, :]))
                if i < NB:
                    do(nc.vector.tensor_tensor_scan(run[:, i % 2, :], one[:], onehi[:, i, :], base[:, i:i + 1],
                                                    ALU.mult, ALU.add))
            do(nc.vector.tensor_copy(rank[:], acc[:]))
            do(nc.vector.tensor_scalar(inti[:], rank[:], 7, None, ALU.logical_shift_right))
            do(nc.vector.tensor_scalar(hii[:], rank[:], P - 1, None, ALU.bitwise_and))
            do(nc.vector.tensor_copy(tmp[:], inti[:]))
            do(nc.vector.tensor_copy(acc[:], hii[:]))
            do(nc.vector.scalar_tensor_tensor(acc[:], acc[:], float(BT), tmp[:], ALU.mult, ALU.add))
            nc.vector.tensor_copy(rec[:, :, 3:4], acc[:].unsqueeze(2)).then_inc(made, 1)

        @b.tensor
        def _(pe):
            pe.wait_ge(counted, 1)
            nc.tensor.matmul(m.ps[:, 0, 0:NB], m.upper[:], cnt[:], start=True, stop=True)
            nc.tensor.matmul(m.ps[:, 1, 0:NB], m.ones[:], cnt[:], start=True, stop=True).then_inc(summed, 1)


def count_product(nc, m, parts, blk, bank, before=None):
    for s in range(NB):
        if before:
            before(s)
        mm = nc.tensor.matmul(m.ps[:, bank, 0:2 * D], m.at[:, s, blk * P:(blk + 1) * P], parts[:, s, :],
                              start=(s == 0), stop=(s == NB - 1))
    return mm


def appnp(nc, m, d):
    with stage(nc, "l0") as (c, sem):
        sb = lambda n, s, t: c.enter_context(nc.sbuf_tensor(n, s, t))
        parts = sb("parts", [P, 2, NB, 2 * D], F16)
        g0 = sb("g0", [P, NB, D], F32)
        coef = sb("coef", [P, NB], F32)
        t1 = sb("t1", [P, 2, D], F32)
        t2 = sb("t2", [P, 2, D], F32)
        gm, ga = sb("gm", [P, 1], F32), sb("ga", [P, 1], F32)
        back = sb("back", [P, NB], F32)
        un, scl = sb("un0", [P, 1], F32), sb("scl0", [P, 1], F32)
        recs = sb("recs", [P, 2, HALF[0], 4], I32)
        chain, mx, amx, ready = sem("l0_chain"), sem("g_max"), sem("g_max_all"), sem("g_parts")
        prod, taken, high = sem("l0_products"), sem("l0_product_taken"), sem("high_part")
        tmp1, turns = sem("l0_partial"), sem("turns")
        staged, scat = [sem("records_a"), sem("records_b")], [sem("scattered_a"), sem("scattered_b")]
        b = c.enter_context(nc.Block())
        NBK = 5

        @b.gpsimd
        def _(g):
            g.wait_ge(mx, 1)
            nc.gpsimd.partition_all_reduce(ga[:], gm[:], P, RMAX).then_inc(amx, 1)
            with g.Fori(0, T // TURN) as k:
                for h, n in enumerate(HALF):
                    g.wait_ge(staged[h], 16 * k + 16)
                    g.sem_inc(turns, 1)
                    for j in range(n):
                        nc.gpsimd.indirect_dma_start(d.table, bass.IndirectOffsetOnAxis(recs[:, h, j, 3:4], 0),
                                                     recs[:, h, j, :], None).then_inc(scat[h], 16)
            for h, n in enumerate(HALF):
                g.wait_ge(scat[h], 16 * n * (T // TURN))

        @b.scalar
        def _(a):
            square_root(nc, a, m, 2, m.st2[:])

        @b.sync
        def _(sp):
            for h, n in enumerate(HALF):
                sp.dma_start(recs[:, h, 0:n, :], d.rec[:, h * HALF[0]:h * HALF[0] + n, :]).then_inc(staged[h], 16)
            with sp.Fori(1, T // TURN) as k:
                for h, n in enumerate(HALF):
                    sp.wait_ge(scat[h], 16 * n * k)
                    sp.dma_start(recs[:, h, 0:n, :], d.rec[:, bass.ds(k * TURN + h * HALF[0], n), :]).then_inc(staged[h], 16)

        @b.vector
        def _(v):
            do = Chain(v, chain)
            do(nc.vector.tensor_tensor(g0[:], m.x[:], bc_last(m.dinv[:], D), ALU.mult))
            nc.vector.tensor_reduce(gm[:], g0[:].rearrange("p i f -> p (i f)"), AX.X, ALU.max, apply_absolute_value=True).then_inc(mx, 1)
            for i in range(NB):
                blk = m.at[:, i, i * P:(i + 1) * P]
                nc.vector.tensor_tensor(blk, blk, m.ident16[:], ALU.add)
            do(nc.vector.tensor_tensor(coef[:], m.dinv[:], m.dinv[:], ALU.mult))
            do(nc.vector.tensor_scalar(coef[:], coef[:], 1.0 - ALPHA, None, ALU.mult))
            v.wait_ge(amx, 1)
            scale_of(nc, do, m, ga[:], scl[:], un[:])
            do(nc.vector.tensor_scalar(g0[:], g0[:], scl[:], None, ALU.mult))
            do(nc.vector.tensor_copy(parts[:, 0, :, 0:D], g0[:]))
            do(nc.vector.tensor_tensor(parts[:, 0, :, D:2 * D], g0[:], parts[:, 0, :, 0:D], ALU.subtract))
            v.sem_inc(ready, NB)
            do(nc.vector.tensor_scalar(g0[:], g0[:], ALPHA, None, ALU.mult))
            do(nc.vector.tensor_scalar(back[:], m.deg[:], 1.0, None, ALU.add))
            do(nc.vector.tensor_tensor(back[:], back[:], m.dinv[:], ALU.mult))
            do(nc.vector.tensor_scalar(back[:], back[:], un[:], None, ALU.mult))
            with v.Fori(0, STEPS // 2) as k:
                for r in range(2 * NB):
                    i, nxt = r % NB, 1 - r // NB
                    v.wait_ge(prod, 2 * NB * k + (r + 1))
                    nc.vector.scalar_tensor_tensor(t1[:, r % 2, :], m.ps[:, r % NBK, 0:D], coef[:, i:i + 1],
                                                   g0[:, i, :], ALU.mult, ALU.add).then_inc(tmp1, 1)
                    v.wait_ge(tmp1, 4 * NB * k + (2 * r + 1))
                    nc.vector.scalar_tensor_tensor(t2[:, r % 2, :], m.ps[:, r % NBK, D:2 * D], coef[:, i:i + 1],
                                                   t1[:, r % 2, :], ALU.mult, ALU.add).then_inc(tmp1, 1)
                    v.wait_ge(tmp1, 4 * NB * k + (2 * r + 2))
                    v.sem_inc(taken, 1)
                    nc.vector.tensor_copy(parts[:, nxt, i, 0:D], t2[:, r % 2, :]).then_inc(high, 1)
                    v.wait_ge(high, 2 * NB * k + (r + 1))
                    nc.vector.tensor_tensor(parts[:, nxt, i, D:2 * D], t2[:, r % 2, :], parts[:, nxt, i, 0:D],
                                            ALU.subtract).then_inc(ready, 1)
            v.wait_ge(ready, NB * (STEPS + 1))
            do(nc.vector.tensor_tensor(g0[:], parts[:, 0, :, 0:D], parts[:, 0, :, D:2 * D], ALU.add))
            do(nc.vector.tensor_tensor(g0[:], g0[:], bc_last(back[:], D), ALU.mult))
            do(nc.vector.tensor_tensor(g0[:], g0[:], m.x[:], ALU.add))
            sq = parts[:].rearrange("p a i f -> p (a i f)").bitcast(F32)[:, 0:NB * D]
            layer_norm(nc, v, do, m, m.x, g0, sq.rearrange("p (i f) -> p i f", f=D), 2)

        @b.tensor
        def _(pe):
            pe.sem_inc(taken, NBK)
            with pe.Fori(0, STEPS // 2) as k:
                for r in range(2 * NB):
                    pe.wait_ge(taken, 2 * NB * k + (r + 1))
                    before = (lambda s: pe.wait_ge(ready, 2 * NB * k + (r + s + 1))) if r % NB == 0 else None
                    count_product(nc, m, parts[:, r // NB], r % NB, r % NBK, before).then_inc(prod, 1)


def sage(nc, m, d, layer):
    with stage(nc, f"l1_{layer}") as (c, sem):
        sb = lambda n, s, t: c.enter_context(nc.sbuf_tensor(n + f"_{layer}", s, t))
        w0, w1 = sb("w0", [D, D], F32), sb("w1", [D, D], F32)
        w2a, w2b = sb("w2a", [D, D], F32), sb("w2b", [D, D], F32)
        b0, b1, b2 = sb("b0", [P, D], F32), sb("b1", [D, 1], F32), sb("b2", [P, D], F32)
        y = m.y
        nb = sb("nb", [P, NB, D], F32)
        parts = sb("nbparts", [P, NB, 2 * D], F16)
        early = carver(parts)
        xT, hsT = early("xT", [D, 2, GROUP * P], F32), early("hsT", [D, 2, GROUP * P], F32)
        agg, aggT = sb("agg", [P, 2, D], F32), sb("aggT", [D, 2, P], F32)
        gm, ga = sb("gm1", [P, 1], F32), sb("ga1", [P, 1], F32)
        un, scl = sb("un1", [P, 1], F32), sb("scl1", [P, 1], F32)
        wl, chain = sem("sage_weights"), sem("sage_chain")
        turned, xcp, nbd, hsd = sem("x_turned"), sem("xT_copied"), sem("nb_product"), sem("hs_product")
        nbc, hsc, outd, outc = sem("nb_copied"), sem("hs_copied"), sem("self_out"), sem("self_out_taken")
        mx, amx, ready = sem("nb_max"), sem("nb_max_all"), sem("nb_parts")
        prod, aggc, aggt, aggtc = sem("agg_product"), sem("agg_copied"), sem("agg_turned"), sem("aggT_copied")
        outb, outbc, half = sem("agg_out"), sem("agg_out_taken"), sem("agg_half")
        b = c.enter_context(nc.Block())
        src = m.x if layer == 0 else m.y

        @b.sync
        def _(sp):
            sp.dma_start(w0[:], d.W0[layer]).then_inc(wl, 16)
            sp.dma_start(w1[:], d.W1[layer]).then_inc(wl, 16)
            sp.dma_start(w2a[:], d.W2[layer, 0:D, :]).then_inc(wl, 16)
            sp.dma_start(w2b[:], d.W2[layer, D:2 * D, :]).then_inc(wl, 16)
            sp.dma_start(b0[:], d.b0[layer:layer + 1, :].to_broadcast([P, D])).then_inc(wl, 16)
            sp.dma_start(b2[:], d.b2[layer:layer + 1, :].to_broadcast([P, D])).then_inc(wl, 16)
            sp.dma_start(b1[:], d.b1[layer].rearrange("(f a) -> f a", a=1), allow_slow_non_contiguous=True).then_inc(wl, 16)
            sp.wait_ge(wl, 112)

        @b.gpsimd
        def _(g):
            g.wait_ge(mx, 1)
            nc.gpsimd.partition_all_reduce(ga[:], gm[:], P, RMAX).then_inc(amx, 1)

        @b.scalar
        def _(a):
            for g in range(NG + 1):
                if g < NG:
                    n = GROUPS[g][1] * P
                    a.wait_ge(turned, g + 1)
                    if g >= 2:
                        a.wait_ge(nbd, g - 1)
                    nc.scalar.activation(xT[:, g % 2, 0:n], m.ps[0:D, g % 2, 0:n], ACT.Copy).then_inc(xcp, 1)
                if g >= 1:
                    q, n = g - 1, GROUPS[g - 1][1] * P
                    if q == 0:
                        a.wait_ge(wl, 112)
                    a.wait_ge(hsd, q + 1)
                    if q >= 2:
                        a.wait_ge(outd, q - 1)
                    nc.scalar.activation(hsT[:, q % 2, 0:n], m.ps[0:D, 4 + q % 2, 0:n], ACT.Identity,
                                         bias=b1[:]).then_inc(hsc, 1)
            for i in range(NB):
                a.wait_ge(aggt, i + 1)
                if i >= 2:
                    a.wait_ge(outb, i - 1)
                nc.scalar.activation(aggT[:, i % 2, :], m.ps[0:D, 4 + i % 2, 0:P], ACT.Copy).then_inc(aggtc, 1)
            square_root(nc, a, m, 3 + layer, m.st2[:])
            if layer == 1:
                square_root(nc, a, m, 5, m.st2[:])

        @b.vector
        def _(v):
            do = Chain(v, chain)
            if layer == 0:
                for i in range(NB):
                    blk = m.at[:, i, i * P:(i + 1) * P]
                    nc.vector.tensor_tensor(blk, blk, m.ident16[:], ALU.subtract)
            v.wait_ge(wl, 112)
            for g in range(NG + 1):
                if g < NG:
                    a, n = GROUPS[g]
                    v.wait_ge(nbd, g + 1)
                    nc.vector.tensor_tensor(nb[:, a:a + n, :], blocks_of(m.ps[:, 2 + g % 2, 0:n * D]),
                                            bc_mid(b0[:], n), ALU.add).then_inc(nbc, 1)
                if g >= 1:
                    q, (a, n) = g - 1, GROUPS[g - 1]
                    v.wait_ge(outd, q + 1)
                    nc.vector.tensor_tensor(y[:, a:a + n, :], blocks_of(m.ps[:, 6 + q % 2, 0:n * D]),
                                            bc_mid(b2[:], n), ALU.add).then_inc(outc, 1)
            v.wait_ge(nbc, NG)
            v.wait_ge(outc, NG)
            nc.vector.tensor_reduce(gm[:], nb[:].rearrange("p i f -> p (i f)"), AX.X, ALU.max, apply_absolute_value=True).then_inc(mx, 1)
            v.wait_ge(amx, 1)
            scale_of(nc, do, m, ga[:], scl[:], un[:])
            do(nc.vector.tensor_scalar(nb[:], nb[:], scl[:], None, ALU.mult))
            do(nc.vector.tensor_copy(parts[:, :, 0:D], nb[:]))
            nc.vector.tensor_tensor(parts[:, :, D:2 * D], nb[:], parts[:, :, 0:D], ALU.subtract).then_inc(ready, 1)
            for i in range(NB + 2):
                if i < NB:
                    v.wait_ge(prod, i + 1)
                    if i >= 2:
                        v.wait_ge(aggt, i - 1)
                    nc.vector.tensor_scalar(agg[:, i % 2, :], m.ps[:, i % 4, 0:D], un[:], None,
                                            ALU.mult).then_inc(half, 1)
                    v.wait_ge(half, i + 1)
                    nc.vector.scalar_tensor_tensor(agg[:, i % 2, :], m.ps[:, i % 4, D:2 * D], un[:],
                                                   agg[:, i % 2, :], ALU.mult, ALU.add).then_inc(aggc, 1)
                if i >= 2:
                    q = i - 2
                    v.wait_ge(outb, q + 1)
                    nc.vector.tensor_tensor(y[:, q, :], y[:, q, :], m.ps[:, 6 + q % 2, 0:D], ALU.add).then_inc(outbc, 1)
            v.wait_ge(outbc, NB)
            do(nc.vector.tensor_reduce(m.st1[:], y[:], AX.X, ALU.add))
            do(nc.vector.tensor_scalar(m.st1[:], m.st1[:], 1.0 / D, None, ALU.mult))
            do(nc.vector.tensor_tensor(nb[:], y[:], bc_last(m.st1[:], D), ALU.subtract))
            do(nc.vector.tensor_tensor(nb[:], nb[:], nb[:], ALU.mult))
            do(nc.vector.tensor_reduce(m.st2[:], nb[:], AX.X, ALU.add))
            nc.vector.scalar_tensor_tensor(m.st2[:], m.st2[:], 1.0 / (D - 1), m.padcol[:], ALU.mult,
                                           ALU.add).then_inc(m.var_ready, 1)
            inverse_root(nc, v, do, m, 3 + layer, m.st2[:])
            do(nc.vector.tensor_tensor(y[:], y[:], bc_last(m.st2[:], D), ALU.mult))
            if layer == 1:
                do(nc.vector.tensor_tensor(y[:], y[:], m.x[:], ALU.add))
                layer_norm(nc, v, do, m, m.x, y, nb, 5)

        @b.tensor
        def _(pe):
            for g in range(NG + 2):
                if g < NG:
                    a, n = GROUPS[g]
                    if g >= 2:
                        pe.wait_ge(xcp, g - 1)
                    for j in range(n):
                        tr = nc.tensor.transpose(m.ps[0:D, g % 2, j * P:(j + 1) * P], src[:, a + j, :], m.ident[:])
                    tr.then_inc(turned, 1)
                if 1 <= g <= NG:
                    q, n = g - 1, GROUPS[g - 1][1]
                    if q == 0:
                        pe.wait_ge(wl, 112)
                    pe.wait_ge(xcp, q + 1)
                    if q >= 2:
                        pe.wait_ge(nbc, q - 1)
                        pe.wait_ge(hsc, q - 1)
                    nc.tensor.matmul(m.ps[0:D, 4 + q % 2, 0:n * P], w1[:], xT[:, q % 2, 0:n * P], start=True,
                                     stop=True).then_inc(hsd, 1)
                    for j in range(n):
                        mm = nc.tensor.matmul(m.ps[:, 2 + q % 2, j * D:(j + 1) * D], xT[:, q % 2, j * P:(j + 1) * P],
                                              w0[:], start=True, stop=True)
                    mm.then_inc(nbd, 1)
                if g >= 2:
                    q, n = g - 2, GROUPS[g - 2][1]
                    pe.wait_ge(hsc, q + 1)
                    if q >= 2:
                        pe.wait_ge(outc, q - 1)
                    for j in range(n):
                        mm = nc.tensor.matmul(m.ps[:, 6 + q % 2, j * D:(j + 1) * D], hsT[:, q % 2, j * P:(j + 1) * P],
                                              w2a[:], start=True, stop=True)
                    mm.then_inc(outd, 1)
            pe.wait_ge(ready, 1)
            for i in range(NB + 2):
                if i < NB:
                    if i >= 4:
                        pe.wait_ge(aggc, i - 3)
                    count_product(nc, m, parts, i, i % 4).then_inc(prod, 1)
                if 1 <= i <= NB:
                    q = i - 1
                    pe.wait_ge(aggc, q + 1)
                    if q >= 2:
                        pe.wait_ge(aggtc, q - 1)
                    nc.tensor.transpose(m.ps[0:D, 4 + q % 2, 0:P], agg[:, q % 2, :], m.ident[:]).then_inc(aggt, 1)
                if i >= 2:
                    q = i - 2
                    pe.wait_ge(aggtc, q + 1)
                    if q >= 2:
                        pe.wait_ge(outbc, q - 1)
                    nc.tensor.matmul(m.ps[:, 6 + q % 2, 0:D], aggT[:, q % 2, :], w2b[:], start=True,
                                     stop=True).then_inc(outb, 1)


def weighted_sum(nc, m, d):
    with stage(nc, "l2") as (c, sem):
        sb = lambda n, s, t: c.enter_context(nc.sbuf_tensor(n, s, t))
        R = 16
        tab = sb("tab", [P, BT, 4], I32)
        low, wt = sb("low", [P, BT], F32), sb("wt", [P, BT], F32)
        targets = sb("targets", [P, BT], I32)
        rows = sb("rows", [P, R, D], F32)
        onew = sb("onew", [P, 4, P], F32)
        sq = sb("sq2", [P, NB, D], F32)
        acc = sb("acc2", [P, NB * D], F32)
        tj, cmp, tji = sb("tj", [1, BT], F32), sb("cmp", [1, BT], F32), sb("tji", [1, BT], I32)
        io = sem("tile_iota")
        loaded, chain, xst = sem("table_loaded"), sem("l2_chain"), sem("x_stored")
        split = sem("targets_split")
        got = [sem(f"row_{j}_gathered") for j in range(R)]
        hot, prod, add = sem("weighted_onehots"), sem("l2_products"), sem("l2_added")
        b = c.enter_context(nc.Block())

        @b.sync
        def _(sp):
            sp.dma_start(tab[:], d.table.rearrange("(p t) c -> p t c", p=P)).then_inc(loaded, 16)
            sp.dma_start(d.xt.rearrange("(i p) f -> p i f", p=P), m.x[:]).then_inc(xst, 16)
            sp.wait_ge(xst, 16)

        @b.gpsimd
        def _(g):
            nc.gpsimd.iota(tji[:], [[1, BT]], 0, 0).then_inc(io, 1)
            g.wait_ge(split, 1)
            g.wait_ge(xst, 16)
            for t in range(BT):
                if t >= R:
                    g.wait_ge(prod, R + t - R + 1)
                nc.gpsimd.indirect_dma_start(rows[:, t % R, :], None, d.xt,
                                             bass.IndirectOffsetOnAxis(targets[:, t:t + 1], 0)).then_inc(got[t % R], 16)

        @b.vector
        def _(v):
            do = Chain(v, chain)
            do(nc.vector.memset(acc[:], 0.0))
            v.wait_ge(loaded, 16)
            nc.vector.tensor_copy(targets[:], tab[:, :, 0]).then_inc(split, 1)
            do(nc.vector.tensor_copy(low[:], tab[:, :, 1]))
            do(nc.vector.tensor_copy(wt[:], tab[:, :, 2].bitcast(F32)))
            v.wait_ge(io, 1)
            do(nc.vector.tensor_copy(tj[:], tji[:]))
            do(nc.vector.memset(cmp[:], -1.0))
            for i in range(NB):
                do(nc.vector.scalar_tensor_tensor(cmp[:], tj[:], m.first_tile[:, i:i + 1], cmp[:], ALU.is_ge, ALU.add))
            do(nc.vector.tensor_scalar(cmp[:], cmp[:], float(D), None, ALU.mult))
            do(nc.vector.tensor_copy(m.bucket[:], cmp[:]))
            regs = [v.alloc_register(f"bucket{j}") for j in range(R)]
            v.sem_inc(add, 8)
            with v.Fori(0, BT // R) as k:
                for j in range(0, R, 4):
                    v.load(regs[j:j + 4], m.bucket[0:1, bass.ds(R * k + j, 4)])
                at = [v.snap(r, min_val=0, max_val=(NB - 1) * D) for r in regs]
                for j in range(R + 1):
                    if j < R:
                        v.wait_ge(prod, R * k + (j + R - 3))
                        nc.vector.tensor_scalar(onew[:, j % 4, :], m.row[:, 0:P], low[:, bass.ds(R * k + j, 1)],
                                                wt[:, bass.ds(R * k + j, 1)], ALU.is_equal,
                                                ALU.mult).then_inc(hot, 1)
                    if j >= 1:
                        q = j - 1
                        v.wait_ge(prod, R * k + (q + R + 1))
                        v.wait_ge(add, R * k + (q + 8))
                        dst = acc[:, bass.ds(at[q], D)]
                        nc.vector.tensor_tensor(dst, dst, m.ps[:, q % 8, 0:D], ALU.add).then_inc(add, 1)
            v.wait_ge(add, BT + 8)
            s = acc[:].rearrange("p (i f) -> p i f", f=D)
            do(nc.vector.tensor_tensor(s, s, m.x[:], ALU.add))
            layer_norm(nc, v, do, m, m.x, s, sq, 6)

        @b.scalar
        def _(a):
            square_root(nc, a, m, 6, m.st2[:])

        @b.tensor
        def _(pe):
            pe.sem_inc(prod, R)
            with pe.Fori(0, BT // R) as k:
                for j in range(R):
                    pe.wait_ge(hot, R * k + (j + 1))
                    pe.wait_ge(got[j], 16 * k + 16)
                    pe.wait_ge(add, R * k + (j + 1))
                    nc.tensor.matmul(m.ps[:, j % 8, 0:D], onew[:, j % 4, :], rows[:, j, :], start=True,
                                     stop=True).then_inc(prod, 1)


def edge_masks(nc, m, d):
    with stage(nc, "masks") as (c, sem):
        sb = lambda n, s, t: c.enter_context(nc.sbuf_tensor(n, s, t))
        dsti = sb("dsti3", [P, T], I32)
        prev, dstf, prevf = sb("prev", [P, 1], I32), sb("dstf", [P, T], F32), sb("prevf", [P, 1], F32)
        cont, mcol = sb("cont", [P, 1], F32), sb("mcol", [P, 1], F32)
        mrep, rem = sb("mrep", [P, D], F32), sb("rem", [P, NB], F32)
        e, q, s = sb("e_end", [P, NB], F32), sb("q_end", [P, NB], F32), sb("q_start", [P, NB], F32)
        eld = sem("edges_loaded3")
        chain, z, ld = sem("mask_chain"), sem("prev_cleared"), sem("prev_loaded")
        rep, rowd = sem("carry_column"), sem("carry_row")
        qrep = sb("q_rep", [P, NB, P], F32)
        spread, ends, seld = sem("streams_spread"), sem("streams_in_rows"), sem("selector_made")
        b = c.enter_context(nc.Block())

        @b.sync
        def _(sp):
            sp.dma_start(dsti[:], d.dst_s).then_inc(eld, 16)
            sp.dma_start(m.srci[:], d.src_s).then_inc(eld, 16)
            sp.wait_ge(z, 1)
            sp.dma_start(prev[1:P, :], d.dst_s[0:P - 1, T - 1:T], allow_slow_non_contiguous=True).then_inc(ld, 16)
            sp.wait_ge(ld, 16)

        @b.vector
        def _(v):
            do = Chain(v, chain)
            nc.vector.memset(prev[:], -1).then_inc(z, 1)
            v.wait_ge(eld, 32)
            do(nc.vector.tensor_copy(dstf[:], dsti[:]))
            do(nc.vector.memset(m.brk[:], 0.0))
            do(nc.vector.tensor_tensor(m.brk[:, 1:T], dstf[:, 1:T], dstf[:, 0:T - 1], ALU.not_equal))
            do(nc.vector.tensor_scalar(m.brk[:], m.brk[:], -BIG, None, ALU.mult))
            v.wait_ge(ld, 16)
            do(nc.vector.tensor_copy(prevf[:], prev[:]))
            do(nc.vector.tensor_tensor(cont[:], dstf[:, 0:1], prevf[:], ALU.is_equal))
            do(nc.vector.tensor_tensor(mcol[:], dstf[:, 0:1], dstf[:, T - 1:T], ALU.is_equal))
            do(nc.vector.tensor_tensor(mcol[:], mcol[:], cont[:], ALU.mult))
            do(nc.vector.tensor_scalar(mcol[:], mcol[:], 1.0, BIG, ALU.subtract, ALU.mult))
            nc.vector.tensor_scalar(mrep[:], m.ones[:, 0:D], mcol[:], None, ALU.mult).then_inc(rep, 1)
            do(nc.vector.tensor_tensor(e[:], m.rowptr[:], m.deg[:], ALU.add))
            do(nc.vector.tensor_scalar(e[:], e[:], 1.0, 0.0, ALU.subtract, ALU.max))
            do(nc.vector.tensor_copy(m.endi[:], e[:]))

            def stream_of(out, x):
                do(nc.vector.tensor_scalar(out[:], x[:], 1.0 / T, 0.5 / T - 0.5, ALU.mult, ALU.add))
                do(nc.vector.tensor_copy(m.streami[:], out[:]))
                do(nc.vector.tensor_copy(out[:], m.streami[:]))
                do(nc.vector.scalar_tensor_tensor(rem[:], out[:], -float(T), x[:], ALU.mult, ALU.add))
                do(nc.vector.scalar_tensor_tensor(out[:], rem[:], float(T), out[:], ALU.is_ge, ALU.add))
                do(nc.vector.tensor_scalar(rem[:], rem[:], 0.0, None, ALU.is_lt))
                do(nc.vector.tensor_tensor(out[:], out[:], rem[:], ALU.subtract))
                do(nc.vector.tensor_copy(m.streami[:], out[:]))

            stream_of(s, m.rowptr)
            stream_of(q, e)
            nc.vector.tensor_copy(qrep[:], bc_last(q[:], P)).then_inc(spread, 1)
            do(nc.vector.tensor_tensor(m.nocarry[:], s[:], q[:], ALU.is_ge))
            do(nc.vector.tensor_scalar(m.nocarry[:], m.nocarry[:], -BIG, None, ALU.mult))
            do(nc.vector.tensor_scalar(m.some[:], m.deg[:], 0.0, None, ALU.is_gt))
            v.wait_ge(rowd, 1)
            do(nc.vector.tensor_copy(m.mrow[:], m.ps[0:D, 0, 0:P]))
            for g, (a, n) in enumerate(GROUPS):
                v.wait_ge(ends, g + 1)
                nc.vector.tensor_scalar(m.sel[:, a * P:(a + n) * P], m.ps[:, 1 + g, 0:n * P], m.col[:], None,
                                        ALU.is_equal).then_inc(seld, 1)
            v.wait_ge(seld, NG)

        @b.tensor
        def _(pe):
            pe.wait_ge(rep, 1)
            nc.tensor.matmul(m.ps[0:D, 0, 0:P], mrep[:], m.ident[:], start=True, stop=True).then_inc(rowd, 1)
            pe.wait_ge(spread, 1)
            for g, (a, n) in enumerate(GROUPS):
                for j in range(n):
                    mm = nc.tensor.matmul(m.ps[:, 1 + g, j * P:(j + 1) * P], qrep[:, a + j, :], m.ident[:],
                                          start=True, stop=True)
                mm.then_inc(ends, 1)


def edge_conv(nc, m, d, layer, out):
    with stage(nc, f"conv_{layer}") as (c, sem):
        sb = lambda n, s, t: c.enter_context(nc.sbuf_tensor(n + f"_c{layer}", s, t))
        wmr, we = sb("wmr", [D, 2 * D], F32), sb("we", [DE, D], F32)
        bias = sb("bias", [P, D], F32)
        xT = sb("xT", [D, NP], F32)
        ytab, root = sb("ytab", [P, NB, D], F32), sb("root", [P, NB, D], F32)
        ea = sb("ea", [DE, TURN, P], F32)
        rows = sb("rows", [P, TURN, D], F32)
        run = sb("run", [P, TURN, D], F32)
        carT, carr, lastT = sb("carT", [D, P], F32), sb("carr", [P, D], F32), sb("lastT", [D, P], F32)
        rg, cg = sb("rg", [P, NB, D], F32), sb("cg", [P, NB, D], F32)
        wl, chain, turned, xcp = sem("conv_weights"), sem("conv_chain"), sem("x_turned"), sem("xT_copied")
        yd, yc, yst, eal = sem("y_product"), sem("y_copied"), sem("y_stored"), [sem("ea_a"), sem("ea_b")]
        got = [sem(f"row_{j}_gathered") for j in range(TURN)]
        runz = sem("run_cleared")
        msg, ran, rst = sem("messages"), sem("running_max"), [sem("run_a"), sem("run_b")]
        lt, sc, ct, cc = sem("last_turned"), sem("carries"), sem("carry_turned"), sem("carry_copied")
        rgd = [sem(f"ends_gathered_{g}") for g in range(NB // ENDS)]
        cgd, res, ost = sem("carries_selected"), sem("result"), sem("out_stored")
        rd, rc = sem("root_product"), sem("root_copied")
        b = c.enter_context(nc.Block())
        cur = m.x if layer == 0 else m.y
        TN = T // TURN
        spans = ((0, HALF[0]), (HALF[0], HALF[1]))
        NBK = 6

        @b.sync
        def _(sp):
            sp.dma_start(wmr[:, 0:D], d.Wmsg[layer]).then_inc(wl, 16)
            sp.dma_start(wmr[:, D:2 * D], d.Wroot[layer]).then_inc(wl, 16)
            sp.dma_start(we[:], d.Wedge[layer]).then_inc(wl, 16)
            sp.dma_start(bias[:], d.bias[layer].rearrange("(a f) -> a f", a=1).to_broadcast([P, D])).then_inc(wl, 16)
            for g, (a, n) in enumerate(GROUPS):
                sp.wait_ge(yc, g + 1)
                sp.dma_start(d.yt.rearrange("(i p) f -> p i f", p=P)[:, a:a + n, :], ytab[:, a:a + n, :]).then_inc(yst, 16)
            with sp.Fori(0, TN) as k:
                for h, (a, n) in enumerate(spans):
                    sp.wait_ge(msg, TURN * k + a + n)
                    sp.dma_start(ea[:, a:a + n, :], d.eaT[:, bass.ds(k * TURN + a, n), :]).then_inc(eal[h], 16)
            sp.wait_ge(yst, 16 * NG)
            if layer == 1:
                sp.wait_ge(res, 1)
                sp.dma_start(out.rearrange("(i p) f -> p i f", p=P), m.x[:]).then_inc(ost, 16)
                sp.wait_ge(ost, 16)

        @b.gpsimd
        def _(g):
            g.wait_ge(yst, 16 * NG)
            for t in range(T):
                if t >= TURN:
                    g.wait_ge(msg, TURN + t - TURN + 1)
                nc.gpsimd.indirect_dma_start(rows[:, t % TURN, :], None, d.yt,
                                             bass.IndirectOffsetOnAxis(m.srci[:, t:t + 1], 0)).then_inc(got[t % TURN], 16)
            for r in rst:
                g.wait_ge(r, 16 * TN + 16)
            for i in range(NB):
                nc.gpsimd.indirect_dma_start(rg[:, i, :], None, d.run,
                                             bass.IndirectOffsetOnAxis(m.endi[:, i:i + 1], 0)).then_inc(rgd[i // ENDS], 16)
            for r in rgd:
                g.wait_ge(r, 16 * ENDS)

        @b.scalar
        def _(a_):
            for g, (a, n) in enumerate(GROUPS):
                a_.wait_ge(turned, g + 1)
                nc.scalar.activation(xT[:, a * P:(a + n) * P], m.ps[0:D, g % 2, 0:n * P], ACT.Copy).then_inc(xcp, 1)
            rdram = d.run.rearrange("(p t) f -> p t f", t=T)
            a_.wait_ge(runz, 1)
            for h, (a, n) in enumerate(spans):
                a_.dma_start(rdram[:, a:a + n, :], run[:, a:a + n, :]).then_inc(rst[h], 16)
            with a_.Fori(0, TN) as k:
                for h, (a, n) in enumerate(spans):
                    a_.wait_ge(ran, TURN * k + (a + n + TURN))
                    a_.wait_ge(rst[h], 16 * k + 16)
                    a_.dma_start(rdram[:, bass.ds(k * TURN + a, n), :], run[:, a:a + n, :]).then_inc(rst[h], 16)
            for r in rst:
                a_.wait_ge(r, 16 * TN + 16)
            if layer == 1:
                square_root(nc, a_, m, 7, m.st2[:])

        @b.vector
        def _(v):
            do = Chain(v, chain)
            v.wait_ge(wl, 64)
            for g, (a, n) in enumerate(GROUPS):
                v.wait_ge(yd, g + 1)
                nc.vector.tensor_copy(ytab[:, a:a + n, :], blocks_of(m.ps[:, 2 + g % 2, 0:n * D])).then_inc(yc, 1)
            for g, (a, n) in enumerate(GROUPS):
                v.wait_ge(rd, g + 1)
                nc.vector.tensor_tensor(root[:, a:a + n, :], blocks_of(m.ps[:, 4 + g % 2, 0:n * D]), bc_mid(bias[:], n),
                                        ALU.add).then_inc(rc, 1)
            nc.vector.memset(run[:], -BIG).then_inc(runz, 1)
            v.wait_ge(runz, 1)
            v.sem_inc(ran, TURN)
            with v.Fori(0, TN) as k:
                for h, (a, n) in enumerate(spans):
                    for j in range(a, a + n):
                        v.wait_ge(msg, TURN * k + (j + 1 + TURN))
                        if j == a:
                            v.wait_ge(rst[h], 16 * k + 16)
                        nc.vector.scalar_tensor_tensor(run[:, j, :], run[:, (j - 1) % TURN, :],
                                                       m.brk[:, bass.ds(k * TURN + j, 1)],
                                                       m.ps[:, j % NBK, 0:D], ALU.add, ALU.max).then_inc(ran, 1)
                        v.wait_ge(ran, TURN * k + (j + 1 + TURN))
            v.wait_ge(lt, 1)
            do(nc.vector.tensor_copy(lastT[:], m.ps[0:D, 6, 0:P]))
            do(nc.vector.memset(carT[:, 0:1], -BIG))
            nc.vector.tensor_tensor_scan(carT[:, 1:P], m.mrow[:, 0:P - 1], lastT[:, 0:P - 1], -BIG,
                                         ALU.add, ALU.max).then_inc(sc, 1)
            v.wait_ge(ct, 1)
            nc.vector.tensor_copy(carr[:], m.ps[:, 7, 0:D]).then_inc(cc, 1)
            for g in range(NB // ENDS):
                blk = slice(g * ENDS, (g + 1) * ENDS)
                v.wait_ge(cgd, g + 1)
                do(nc.vector.tensor_tensor(cg[:, blk, :], blocks_of(m.ps[:, g, 0:ENDS * D]),
                                           bc_last(m.nocarry[:, blk], D), ALU.add))
            for g in range(NB // ENDS):
                blk = slice(g * ENDS, (g + 1) * ENDS)
                v.wait_ge(rgd[g], 16 * ENDS)
                do(nc.vector.tensor_tensor(rg[:, blk, :], rg[:, blk, :], cg[:, blk, :], ALU.max))
                do(nc.vector.tensor_tensor(rg[:, blk, :], rg[:, blk, :], bc_last(m.some[:, blk], D), ALU.mult))
                do(nc.vector.tensor_tensor(rg[:, blk, :], rg[:, blk, :], root[:, blk, :], ALU.add))
                do(nc.vector.scalar_tensor_tensor(m.y[:, blk, :], rg[:, blk, :], 0.01, rg[:, blk, :], ALU.mult,
                                                  ALU.max))
                if layer == 1:
                    do(nc.vector.tensor_tensor(m.y[:, blk, :], m.y[:, blk, :], m.x[:, blk, :], ALU.add))
                    centre(nc, do, m, m.y, rg, blk)
            if layer == 1:
                scale_by_deviation(nc, v, do, m, m.x, m.y, 7)
                v.sem_inc(res, 1)

        @b.tensor
        def _(pe):
            for g in range(NG + 1):
                if g < NG:
                    a, n = GROUPS[g]
                    if g >= 2:
                        pe.wait_ge(xcp, g - 1)
                    for j in range(n):
                        tr = nc.tensor.transpose(m.ps[0:D, g % 2, j * P:(j + 1) * P], cur[:, a + j, :], m.ident[:])
                    tr.then_inc(turned, 1)
                if g >= 1:
                    q, (a, n) = g - 1, GROUPS[g - 1]
                    if q == 0:
                        pe.wait_ge(wl, 64)
                    pe.wait_ge(xcp, q + 1)
                    if q >= 2:
                        pe.wait_ge(yc, q - 1)
                    for j in range(n):
                        mm = nc.tensor.matmul(m.ps[:, 2 + q % 2, j * D:(j + 1) * D], xT[:, (a + j) * P:(a + j + 1) * P],
                                              wmr[:, 0:D], start=True, stop=True)
                    mm.then_inc(yd, 1)
            for g, (a, n) in enumerate(GROUPS):
                if g >= 2:
                    pe.wait_ge(rc, g - 1)
                for j in range(n):
                    mm = nc.tensor.matmul(m.ps[:, 4 + g % 2, j * D:(j + 1) * D], xT[:, (a + j) * P:(a + j + 1) * P],
                                          wmr[:, D:2 * D], start=True, stop=True)
                mm.then_inc(rd, 1)
            pe.wait_ge(yc, NG)
            pe.wait_ge(rc, NG)
            pe.sem_inc(msg, TURN)
            with pe.Fori(0, TN) as k:
                for h, (a, n) in enumerate(spans):
                    pe.wait_ge(eal[h], 16 * k + 16)
                    for j in range(a, a + n):
                        pe.wait_ge(got[j], 16 * k + 16)
                        pe.wait_ge(ran, TURN * k + (j + TURN - 4))
                        nc.tensor.matmul(m.ps[:, j % NBK, 0:D], ea[:, j, :], we[:], start=True, stop=False)
                        nc.tensor.matmul(m.ps[:, j % NBK, 0:D], m.ident[:], rows[:, j, :], start=False,
                                         stop=True).then_inc(msg, 1)
            pe.wait_ge(ran, T + TURN)
            nc.tensor.transpose(m.ps[0:D, 6, 0:P], run[:, TURN - 1, :], m.ident[:]).then_inc(lt, 1)
            pe.wait_ge(sc, 1)
            nc.tensor.transpose(m.ps[:, 7, 0:D], carT[:], m.ident[0:D, 0:D]).then_inc(ct, 1)
            pe.wait_ge(cc, 1)
            for g in range(NB // ENDS):
                for j in range(ENDS):
                    i = g * ENDS + j
                    mm = nc.tensor.matmul(m.ps[:, g, j * D:(j + 1) * D], m.sel[:, i * P:(i + 1) * P], carr[:],
                                          start=True, stop=True)
                mm.then_inc(cgd, 1)


def program(nc, x, src_s, dst_s, w_s, src_rows, dst_rows, eaT, W0, b0, W1, b1, W2, b2,
            Wm1, We1, Wr1, c1, Wm2, We2, Wr2, c2, out):
    dram = lambda n, s, t: nc.dram_tensor(n, s, t).ap()
    d = Names()
    d.x, d.src_s, d.dst_s, d.w_s, d.src_rows, d.dst_rows, d.eaT = x, src_s, dst_s, w_s, src_rows, dst_rows, eaT
    d.W0, d.b0, d.W1, d.b1, d.W2, d.b2 = W0, b0, W1, b1, W2, b2
    d.Wmsg, d.Wedge, d.Wroot, d.bias = [Wm1, Wm2], [We1, We2], [Wr1, Wr2], [c1, c2]
    d.ptr, d.off = dram("ptr", [16 * NB], F32), dram("off", [SG * P], I32)
    d.table, d.rec = dram("table", [P * BT, 4], I32), dram("records", [P, T, 4], I32)
    d.xt, d.yt = dram("x_table", [NP, D], F32), dram("y_table", [NP, D], F32)
    d.run = dram("run_max", [EP, D], F32)
    with ExitStack() as c:
        sb = lambda n, s, t: c.enter_context(nc.sbuf_tensor(n, s, t))
        m = Names()
        m.ps = c.enter_context(nc.psum_tensor("ps", [P, 8, 512], F32))
        m.x = sb("x_sb", [P, NB, D], F32)
        m.row, m.row16, m.col = sb("row", [P, 256], F32), sb("row16", [P, 256], F16), sb("col", [P, 1], F32)
        m.ident, m.ident16 = sb("ident", [P, P], F32), sb("ident16", [P, P], F16)
        m.upper, m.neglow16 = sb("upper", [P, P], F32), sb("neglow16", [P, P], F16)
        m.ones, m.ones16 = sb("ones", [P, P], F32), sb("ones16", [P, P], F16)
        m.deg, m.dinv, m.rowptr = sb("deg", [P, NB], F32), sb("dinv", [P, NB], F32), sb("rowptr", [P, NB], F32)
        m.padcol = sb("padcol", [P, NB], F32)
        m.sd, m.nt = sb("sd", [P, NB], F32), sb("nt", [P, NB], F32)
        m.var_ready, m.root_done = c.enter_context(nc.semaphore("variances")), c.enter_context(nc.semaphore("roots"))
        m.st1, m.st2 = sb("st1", [P, NB], F32), sb("st2", [P, NB], F32)
        m.ki, m.kf, m.kg = sb("ki", [P, 1], I32), sb("kf", [P, 1], F32), sb("kg", [P, 1], F32)
        m.first_tile, m.bucket = sb("first_tile", [1, NB], F32), sb("bucket", [1, BT], I32)
        with ExitStack() as with_at:
            m.at = with_at.enter_context(nc.sbuf_tensor("at", [P, NB, NP], F16))
            with ExitStack() as k:
                m.keyT = k.enter_context(nc.sbuf_tensor("keyT", [P, SG * P], F32))
                m.lowT = k.enter_context(nc.sbuf_tensor("lowT", [P, SG * P], F32))
                m.off = k.enter_context(nc.sbuf_tensor("off_sb", [1, SG * P], I32))
                prepare(nc, m, d)
                bucket_ranks(nc, m, d)
                build_counts(nc, m, d)
            appnp(nc, m, d)
            m.y = with_at.enter_context(nc.sbuf_tensor("y_sb", [P, NB, D], F32))
            sage(nc, m, d, 0)
            sage(nc, m, d, 1)
        m.y = sb("y2_sb", [P, NB, D], F32)
        m.srci = sb("srci_sb", [P, T], I32)
        m.brk = sb("brk", [P, T], F32)
        m.mrow = sb("mrow", [D, P], F32)
        m.endi, m.streami = sb("endi", [P, NB], I32), sb("streami", [P, NB], I32)
        m.sel = sb("stream_selector", [P, NP], F32)
        m.nocarry, m.some = sb("nocarry", [P, NB], F32), sb("some", [P, NB], F32)
        weighted_sum(nc, m, d)
        edge_masks(nc, m, d)
        edge_conv(nc, m, d, 0, out)
        edge_conv(nc, m, d, 1, out)


def kernel(x, src, dst, edge_attr_32, edge_weight, L1_gnn_W0, L1_gnn_b0, L1_gnn_W1, L1_gnn_b1, L1_gnn_W2,
           L1_gnn_b2, L3_gnn_W1_msg, L3_gnn_W1_edge, L3_gnn_W1_root, L3_gnn_b1, L3_gnn_W2_msg,
           L3_gnn_W2_edge, L3_gnn_W2_root, L3_gnn_b2):
    import numpy as np
    import concourse.bacc as bacc
    from concourse.bass_utils import run_bass_kernel_spmd

    def padded(a, rows, value=0):
        a = np.asarray(a)
        out = np.full((rows,) + a.shape[1:], value, a.dtype)
        out[:a.shape[0]] = a
        return out

    s, t = padded(src, EP + P, NP - 1), padded(dst, EP + P, NP - 1)
    ea = padded(edge_attr_32, EP).reshape(P, T, DE)
    arrays = {
        "x": padded(x, NP), "src_s": s[:EP].reshape(P, T), "dst_s": t[:EP].reshape(P, T),
        "w_s": padded(edge_weight, EP).reshape(P, T),
        "src_rows": s.reshape(T + 1, P), "dst_rows": t.reshape(T + 1, P),
        "eaT": np.ascontiguousarray(ea.transpose(2, 1, 0)),
        "W0": L1_gnn_W0, "b0": L1_gnn_b0, "W1": L1_gnn_W1, "b1": L1_gnn_b1, "W2": L1_gnn_W2, "b2": L1_gnn_b2,
        "Wm1": L3_gnn_W1_msg, "We1": L3_gnn_W1_edge, "Wr1": L3_gnn_W1_root, "c1": L3_gnn_b1,
        "Wm2": L3_gnn_W2_msg, "We2": L3_gnn_W2_edge, "Wr2": L3_gnn_W2_root, "c2": L3_gnn_b2,
    }
    nc = bacc.Bacc("TRN2", target_bir_lowering=False, num_devices=1)
    feeds, args = {}, []
    for name, a in arrays.items():
        a = np.ascontiguousarray(a)
        feeds["in_" + name] = a
        args.append(nc.dram_tensor("in_" + name, a.shape, mybir.dt.from_np(a.dtype), kind="ExternalInput").ap())
    args.append(nc.dram_tensor("out", (NP, D), F32, kind="ExternalOutput").ap())
    program(nc, *args)
    got = run_bass_kernel_spmd(nc, [feeds], core_ids=[0])
    return got.results[0]["out"][:N]
```

```python
from contextlib import ExitStack, contextmanager

import concourse.bass as bass
from concourse import mybir

F32 = mybir.dt.float32
F16 = mybir.dt.float16
I32 = mybir.dt.int32
ALU = mybir.AluOpType
ACT = mybir.ActivationFunctionType
AX = mybir.AxisListType
RMAX = bass.bass_isa.ReduceOp.max

P = 128
N, D, E, DE = 3125, 96, 50000, 32
NB = -(-N // P)
NP = NB * P
T = -(-E // P)
EP = T * P
W = 8
NW = -(-N // W)
SLOTS = -(-(T + NW) // 16) * 16
SG = -(-(SLOTS + 8) // P)
BT = -(-(T + NB) // 16) * 16
TG = -(-BT // P)
KEYS = NB * W
KEPT, RANKED, EARLY = 4, 8, 15
STEPS, ALPHA = 16, 0.1
GROUP = 4
GROUPS = [(a, min(GROUP, NB - a)) for a in range(0, NB, GROUP)]
NG = len(GROUPS)
ENDS = 5
HALF = (9, 8)
TURN = sum(HALF)
assert T % TURN == 0
EPS = 1e-5
BIG = 1.0e30


@contextmanager
def stage(nc, tag):
    used = []

    def sem(name):
        used.append(nc.alloc_semaphore(f"{name}_{tag}"))
        return used[-1]

    with ExitStack() as c:
        yield c, sem
    nc.clear_and_free_semaphores(used)
    nc.all_engine_barrier()


class Names:
    pass


class Chain:

    def __init__(self, eng, sem):
        self.eng, self.sem, self.n = eng, sem, 0

    def __call__(self, ins):
        self.n += 1
        ins.then_inc(self.sem, 1)
        self.eng.wait_ge(self.sem, self.n)


def carver(at):
    flat, at_byte = at.rearrange("p i n -> p (i n)"), [0]

    def take(name, shape, dtype):
        count = 1
        for n in shape[1:]:
            count *= n
        size = 2 if dtype == F16 else 4
        start = at_byte[0] // 2
        at_byte[0] += -(-count * size // 64) * 64
        assert at_byte[0] <= 2 * flat.shape[1]
        part = flat[0:shape[0], start:start + count * size // 2]
        part = part if dtype == F16 else part.bitcast(dtype)
        return part.rearrange("p (a b) -> p a b", b=shape[2]) if len(shape) == 3 else part

    return take


def bc_mid(ap, n):
    return ap.unsqueeze(1).to_broadcast([ap.shape[0], n, ap.shape[1]])


def blocks_of(ap):
    return ap.rearrange("p (i f) -> p i f", f=D)


def bc_last(ap, n):
    return ap.unsqueeze(2).to_broadcast([ap.shape[0], ap.shape[1], n])


def square_root(nc, act, m, n, x):
    act.wait_ge(m.var_ready, n)
    nc.scalar.activation(m.sd[:], x, ACT.Sqrt).then_inc(m.root_done, 1)


def inverse_root(nc, v, do, m, n, x):
    v.wait_ge(m.root_done, n)
    do(nc.vector.reciprocal(m.sd[:], m.sd[:]))
    do(nc.vector.tensor_tensor(m.nt[:], m.sd[:], m.sd[:], ALU.mult))
    do(nc.vector.tensor_tensor(m.nt[:], m.nt[:], x, ALU.mult))
    do(nc.vector.tensor_scalar(m.nt[:], m.nt[:], -0.5, 1.5, ALU.mult, ALU.add))
    do(nc.vector.tensor_tensor(x, m.sd[:], m.nt[:], ALU.mult))


def layer_norm(nc, v, do, m, out, t, sq, n):
    centre(nc, do, m, t, sq, slice(0, NB))
    scale_by_deviation(nc, v, do, m, out, t, n)


def centre(nc, do, m, t, sq, blk):
    do(nc.vector.tensor_reduce(m.st1[:, blk], t[:, blk, :], AX.X, ALU.add))
    do(nc.vector.tensor_scalar(m.st1[:, blk], m.st1[:, blk], 1.0 / D, None, ALU.mult))
    do(nc.vector.tensor_tensor(t[:, blk, :], t[:, blk, :], bc_last(m.st1[:, blk], D), ALU.subtract))
    do(nc.vector.tensor_tensor(sq[:, blk, :], t[:, blk, :], t[:, blk, :], ALU.mult))
    do(nc.vector.tensor_reduce(m.st2[:, blk], sq[:, blk, :], AX.X, ALU.add))


def scale_by_deviation(nc, v, do, m, out, t, n):
    nc.vector.tensor_scalar(m.st2[:], m.st2[:], 1.0 / D, EPS, ALU.mult, ALU.add).then_inc(m.var_ready, 1)
    inverse_root(nc, v, do, m, n, m.st2[:])
    do(nc.vector.tensor_tensor(out[:], t[:], bc_last(m.st2[:], D), ALU.mult))


def scale_of(nc, do, m, big, scale, unscale):
    k = m.ki
    do(nc.vector.tensor_scalar(k[:, 0:1], big.bitcast(I32), 23, None, ALU.logical_shift_right))
    do(nc.vector.tensor_copy(m.kf[:], k[:, 0:1]))
    do(nc.vector.tensor_scalar(m.kf[:], m.kf[:], 40.0, None, ALU.max))
    do(nc.vector.tensor_scalar(m.kg[:], m.kf[:], -1.0, 254.0 + 13.0, ALU.mult, ALU.add))
    do(nc.vector.tensor_copy(k[:, 0:1], m.kg[:]))
    do(nc.vector.tensor_scalar(scale.bitcast(I32), k[:, 0:1], 23, None, ALU.logical_shift_left))
    do(nc.vector.tensor_scalar(m.kg[:], m.kf[:], 13.0, None, ALU.subtract))
    do(nc.vector.tensor_copy(k[:, 0:1], m.kg[:]))
    do(nc.vector.tensor_scalar(unscale.bitcast(I32), k[:, 0:1], 23, None, ALU.logical_shift_left))


def prepare(nc, m, d):
    with stage(nc, "prepare") as (c, sem):
        sb = carver(m.at[:, KEPT:EARLY, :])
        dsti = sb("dsti", [P, T], I32)
        rowi = sb("rowi", [P, 256], I32)
        coli = sb("coli", [P, 1], I32)
        lo16, hi16 = sb("lo16", [P, T], F16), sb("hi16", [P, T], F16)
        inti = sb("inti", [P, T], I32)
        onehi = sb("onehi", [P, T * NB], F16)
        onelo = sb("onelo", [P, TURN, P], F16)
        zero16 = sb("zero16", [P, P], F16)
        totincl = sb("totincl", [P, NB], F32)
        srow = sb("srow", [P, 16 * NB], F32)
        sint = sb("sint", [P, 16 * NB], I32)
        first, ceil = sb("first", [P, NW], F32), sb("ceil", [P, NW], F32)
        firsti = sb("firsti", [P, NW + 1], I32)
        cnt, pos, dlt = sb("cnt", [P, NW], F32), sb("pos", [P, NW], F32), sb("dlt", [P, NW], F32)
        junk = sb("junk", [P, NW], F32)
        jcol, bsum, tsum = sb("jcol", [P, SG], F32), sb("bsum", [P, SG], F32), sb("tsum", [P, SG], F32)
        jcoli = sb("jcoli", [P, SG], I32)
        srchi16 = sb("src_hi", [P, T], F16)
        places = sb("places", [P, HALF[1], P], F16)
        spread, srcs, clear = sem("places_spread"), sem("sources_loaded"), sem("space_cleared")
        b8 = sb("b8", [P, SG], F32)
        b8i, ti = sb("b8i", [P, SG], I32), sb("ti", [P, SG], I32)
        dg, sg = sb("dg", [P, SG, P], I32), sb("sg", [P, SG, P], I32)
        rel, ok = sb("rel", [P, SG, P], F32), sb("ok", [P, SG, P], F32)
        hi8, lof = sb("hi8", [P, SG, P], F32), sb("lof", [P, SG, P], F32)
        edges, nodes = sem("edges_loaded"), sem("x_loaded")
        iotas, consts, chain = sem("iotas"), sem("constants"), sem("vector_chain")
        lows, free, lowr = sem("low_onehots"), sem("low_buffer_free"), sem("places_found")
        zeroed, counted = sem("psum_zeroed"), sem("degrees_counted")
        degs, prefixed, ptrs = sem("degrees"), sem("prefixes"), sem("row_pointers")
        stored, read = sem("pointers_stored"), sem("pointers_read")
        slots, rows, offs = sem("slot_rows"), sem("slot_edges"), sem("offsets_stored")
        offr, keys, turned = sem("offsets_read"), sem("slot_keys"), sem("keys_turned")
        b = c.enter_context(nc.Block())

        @b.sync
        def _(sp):
            sp.dma_start(dsti[:], d.dst_s).then_inc(edges, 16)
            sp.dma_start(m.src_early[:], d.src_s).then_inc(srcs, 16)
            sp.dma_start(m.x[:], d.x.rearrange("(i p) f -> p i f", p=P)).then_inc(nodes, 16)
            sp.wait_ge(ptrs, 1)
            sp.dma_start(d.ptr.rearrange("(i q) -> q i", q=16), m.rowptr[0:P:8, :], allow_slow_non_contiguous=True).then_inc(stored, 16)
            sp.wait_ge(stored, 16)
            sp.dma_start(srow[:], d.ptr.rearrange("(a n) -> a n", a=1).to_broadcast([P, 16 * NB])).then_inc(read, 16)
            sp.wait_ge(slots, 1)
            sp.dma_start(d.off.rearrange("(g p) -> p g", p=P), b8i[:], allow_slow_non_contiguous=True).then_inc(offs, 16)
            sp.wait_ge(offs, 16)
            sp.dma_start(m.off[:], d.off.rearrange("(a n) -> a n", a=1)).then_inc(offr, 16)
            sp.wait_ge(nodes, 16)
            sp.wait_ge(offr, 16)

        @b.gpsimd
        def _(g):
            nc.gpsimd.iota(rowi[:], [[1, 256]], 0, 0).then_inc(iotas, 1)
            nc.gpsimd.iota(coli[:], [[0, 1]], 0, 1).then_inc(iotas, 1)
            nc.gpsimd.iota(jcoli[:], [[P, SG]], 0, 1).then_inc(iotas, 1)
            nc.gpsimd.memset(m.at[:, EARLY:NB, :], 0.0).then_inc(clear, 1)
            g.wait_ge(clear, 1)
            g.wait_ge(slots, 1)
            for k in range(SG):
                nc.gpsimd.indirect_dma_start(dg[:, k, :], None, d.dst_rows,
                                             bass.IndirectOffsetOnAxis(ti[:, k:k + 1], 0)).then_inc(rows, 16)
                nc.gpsimd.indirect_dma_start(sg[:, k, :], None, d.src_rows,
                                             bass.IndirectOffsetOnAxis(ti[:, k:k + 1], 0)).then_inc(rows, 16)
            g.wait_ge(rows, 32 * SG)

        @b.vector
        def _(v):
            do = Chain(v, chain)
            v.wait_ge(iotas, 3)
            do(nc.vector.tensor_copy(m.row[:], rowi[:]))
            do(nc.vector.tensor_copy(m.row16[:], rowi[:]))
            do(nc.vector.tensor_copy(m.col[:], coli[:]))
            do(nc.vector.tensor_copy(jcol[:], jcoli[:]))
            do(nc.vector.tensor_scalar(m.ident[:], m.row[:, 0:P], m.col[:], None, ALU.is_equal))
            do(nc.vector.tensor_scalar(m.ident16[:], m.row[:, 0:P], m.col[:], None, ALU.is_equal))
            do(nc.vector.tensor_scalar(m.upper[:], m.row[:, 0:P], m.col[:], None, ALU.is_gt))
            do(nc.vector.tensor_scalar(m.neglow16[:], m.row[:, 0:P], m.col[:], -1.0, ALU.is_le, ALU.mult))
            do(nc.vector.memset(m.ones[:], 1.0))
            do(nc.vector.memset(m.ones16[:], 1.0))
            nc.vector.memset(zero16[:], 0.0).then_inc(consts, 1)
            do(nc.vector.memset(m.padcol[:], 0.0))
            do(nc.vector.tensor_scalar(m.padcol[:, NB - 1:NB], m.col[:], float(N - (NB - 1) * P), None, ALU.is_ge))
            v.wait_ge(edges, 16)
            do(nc.vector.tensor_scalar(inti[:], dsti[:], 7, None, ALU.logical_shift_right))
            do(nc.vector.tensor_copy(hi16[:], inti[:]))
            do(nc.vector.tensor_scalar(inti[:], dsti[:], P - 1, None, ALU.bitwise_and))
            do(nc.vector.tensor_copy(lo16[:], inti[:]))
            do(nc.vector.tensor_tensor(onehi[:].rearrange("p (t i) -> p t i", i=NB), bc_last(hi16[:], NB),
                                       bc_mid(m.row16[:, 0:NB], T), ALU.is_equal))
            v.sem_inc(lowr, 1)
            for k in range(T // TURN):
                for h, (a, n) in enumerate(((0, HALF[0]), (HALF[0], HALF[1]))):
                    v.wait_ge(free, 2 * k + h + 1)
                    if h == 0:
                        places_of = bc_last(lo16[:, k * TURN:k * TURN + n], P)
                    else:
                        v.wait_ge(spread, k + 1)
                        places_of = places[:]
                    nc.vector.tensor_tensor(onelo[:, a:a + n, :], places_of, bc_mid(m.row16[:, 0:P], n),
                                            ALU.is_equal).then_inc(lows, 1)
            v.wait_ge(counted, 1)
            do(nc.vector.tensor_copy(m.deg[:], m.ps[:, 0, 0:NB]))
            nc.vector.tensor_scalar(m.dinv[:], m.deg[:], 1.0, None, ALU.add).then_inc(m.var_ready, 1)
            inverse_root(nc, v, do, m, 1, m.dinv[:])
            v.sem_inc(degs, 1)
            v.wait_ge(prefixed, 1)
            do(nc.vector.tensor_tensor_scan(totincl[:], m.ones[:, 0:NB], m.ps[:, 2, 0:NB], 0.0, ALU.mult, ALU.add))
            do(nc.vector.tensor_tensor(totincl[:], totincl[:], m.ps[:, 2, 0:NB], ALU.subtract))
            nc.vector.tensor_tensor(m.rowptr[:], totincl[:], m.ps[:, 1, 0:NB], ALU.add).then_inc(ptrs, 1)
            v.wait_ge(read, 16)
            do(nc.vector.tensor_copy(sint[:], srow[:]))
            do(nc.vector.tensor_scalar(firsti[:, 0:NW], sint[:, 0:NW], 7, None, ALU.logical_shift_right))
            do(nc.vector.tensor_copy(first[:], firsti[:, 0:NW]))
            do(nc.vector.tensor_scalar(srow[:], srow[:], float(P - 1), None, ALU.add))
            do(nc.vector.tensor_copy(sint[:], srow[:]))
            do(nc.vector.tensor_scalar(firsti[:, 0:NW], sint[:, 1:NW + 1], 7, None, ALU.logical_shift_right))
            do(nc.vector.tensor_copy(ceil[:], firsti[:, 0:NW]))
            do(nc.vector.tensor_tensor(cnt[:], ceil[:], first[:], ALU.subtract))
            do(nc.vector.tensor_scalar(cnt[:], cnt[:], 1.0, None, ALU.max))
            do(nc.vector.memset(junk[:], 1.0))
            do(nc.vector.tensor_tensor_scan(pos[:], junk[:], cnt[:], 0.0, ALU.mult, ALU.add))
            do(nc.vector.tensor_tensor(pos[:], pos[:], cnt[:], ALU.subtract))
            do(nc.vector.tensor_tensor(first[:], first[:], pos[:], ALU.subtract))
            do(nc.vector.tensor_copy(dlt[:], first[:]))
            do(nc.vector.tensor_tensor(dlt[:, 1:NW], first[:, 1:NW], first[:, 0:NW - 1], ALU.subtract))
            for k in range(SG):
                do(nc.vector.tensor_scalar(junk[:], pos[:], jcol[:, k:k + 1], 0.0, ALU.is_le, ALU.add,
                                           accum_out=bsum[:, k:k + 1]))
                do(nc.vector.scalar_tensor_tensor(junk[:], pos[:], jcol[:, k:k + 1], dlt[:], ALU.is_le, ALU.mult,
                                                  accum_out=tsum[:, k:k + 1]))
            do(nc.vector.tensor_tensor(tsum[:], tsum[:], jcol[:], ALU.add))
            do(nc.vector.tensor_scalar(tsum[:], tsum[:], float(T), None, ALU.min))
            do(nc.vector.tensor_scalar(b8[:], bsum[:], float(W), -float(W), ALU.mult, ALU.add))
            do(nc.vector.tensor_copy(b8i[:], b8[:]))
            nc.vector.tensor_copy(ti[:], tsum[:]).then_inc(slots, 1)
            v.wait_ge(srcs, 16)
            do(nc.vector.tensor_scalar(m.srchi[:], m.src_early[:], 7, None, ALU.logical_shift_right))
            do(nc.vector.tensor_copy(srchi16[:], m.srchi[:]))
            for i in range(NB):
                ins = nc.vector.tensor_scalar(m.src_blocks[:, i, :], srchi16[:], float(i), 0.0, ALU.is_equal, ALU.add,
                                              accum_out=m.row_counts[:, i:i + 1])
            do(ins)
            v.wait_ge(rows, 32 * SG)
            do(nc.vector.tensor_copy(rel[:], dg[:]))
            do(nc.vector.tensor_tensor(rel[:], rel[:], bc_last(b8[:], P), ALU.subtract))
            do(nc.vector.tensor_scalar(ok[:], rel[:], 0.0, None, ALU.is_ge))
            do(nc.vector.scalar_tensor_tensor(ok[:], rel[:], float(W), ok[:], ALU.is_lt, ALU.mult))
            do(nc.vector.tensor_scalar(dg[:], sg[:], 7, 3, ALU.logical_shift_right, ALU.logical_shift_left))
            do(nc.vector.tensor_copy(hi8[:], dg[:]))
            do(nc.vector.scalar_tensor_tensor(rel[:], rel[:], 1.0, hi8[:], ALU.add, ALU.add))
            do(nc.vector.tensor_tensor(rel[:], rel[:], ok[:], ALU.mult))
            do(nc.vector.tensor_scalar(rel[:], rel[:], -1.0, None, ALU.add))
            do(nc.vector.tensor_scalar(dg[:], sg[:], P - 1, None, ALU.bitwise_and))
            nc.vector.tensor_copy(lof[:], dg[:]).then_inc(keys, 1)
            v.wait_ge(turned, 1)
            do(nc.vector.tensor_copy(m.keyT[:], m.ps[:, 4:6, :].rearrange("p a b -> p (a b)")[:, 0:SG * P]))
            do(nc.vector.tensor_copy(m.lowT[:], m.ps[:, 6:8, :].rearrange("p a b -> p (a b)")[:, 0:SG * P]))

        @b.scalar
        def _(a):
            a.wait_ge(lowr, 1)
            for k in range(T // TURN):
                if k >= 1:
                    a.wait_ge(lows, 2 * k)
                nc.scalar.activation(places[:], bc_last(lo16[:, k * TURN + HALF[0]:(k + 1) * TURN], P),
                                     ACT.Copy).then_inc(spread, 1)
            square_root(nc, a, m, 1, m.dinv[:])

        @b.tensor
        def _(pe):
            pe.wait_ge(consts, 1)
            nc.tensor.matmul(m.ps[:, 0, 0:NB], zero16[:], zero16[:, 0:NB], start=True, stop=False,
                             skip_group_check=True).then_inc(zeroed, 1)
            pe.wait_ge(zeroed, 1)
            pe.sem_inc(free, 2)
            for k in range(T // TURN):
                for h, (a, n) in enumerate(((0, HALF[0]), (HALF[0], HALF[1]))):
                    pe.wait_ge(lows, 2 * k + h + 1)
                    for j in range(a, a + n):
                        mm = nc.tensor.matmul(m.ps[:, 0, 0:NB], onelo[:, j, :],
                                              onehi[:, (k * TURN + j) * NB:(k * TURN + j + 1) * NB],
                                              start=False, stop=False, skip_group_check=True)
                    mm.then_inc(free, 1)
            pe.wait_ge(free, 2 + 2 * (T // TURN))
            pe.sem_inc(counted, 1)
            pe.wait_ge(degs, 1)
            nc.tensor.matmul(m.ps[:, 1, 0:NB], m.upper[:], m.deg[:], start=True, stop=True)
            nc.tensor.matmul(m.ps[:, 2, 0:NB], m.ones[:], m.deg[:], start=True, stop=True).then_inc(prefixed, 1)
            pe.wait_ge(keys, 1)
            for k in range(SG):
                nc.tensor.transpose(m.ps[:, 4 + k // 4, (k % 4) * P:(k % 4 + 1) * P], rel[:, k, :], m.ident[:])
                mm = nc.tensor.transpose(m.ps[:, 6 + k // 4, (k % 4) * P:(k % 4 + 1) * P], lof[:, k, :], m.ident[:])
            mm.then_inc(turned, 1)


def build_counts(nc, m, d):
    with stage(nc, "build") as (c, sem):
        sb = lambda n, s, t: c.enter_context(nc.sbuf_tensor(n, s, t))
        RING, LEAD, PER, PAIRS = 8, 4, 16, 4
        CUT = RANKED * 5 // 8
        onekey = sb("onekey", [P, RING, KEYS], F16)
        oneplace = sb("oneplace", [P, RING, P], F16)
        counts = sb("counts", [P, PAIRS, 2, KEYS], F16)
        cleared = sem("counts_cleared")
        onehot, product = sem("onehots"), sem("slot_products")
        copied, added = sem("pairs_copied"), sem("slots_added")
        b = c.enter_context(nc.Block())

        @b.gpsimd
        def _(g):
            nc.gpsimd.memset(m.at[:, CUT:RANKED, :], 0.0).then_inc(cleared, 1)

        @b.scalar
        def _(a):
            for n in range(SLOTS // 2):
                a.wait_ge(product, 2 * n + 2)
                if n >= PAIRS:
                    a.wait_ge(added, 2 * (n - PAIRS) + 2)
                nc.scalar.activation(counts[:, n % PAIRS, :, :],
                                     m.ps[:, n % 8, :].rearrange("p (a k) -> p a k", a=2)[:, :, 0:KEYS],
                                     ACT.Copy).then_inc(copied, 1)

        @b.vector
        def _(v):
            nc.vector.memset(m.at[:, 0:CUT, :], 0.0).then_inc(cleared, 1)

            def onehots(s):
                if s >= RING:
                    v.wait_ge(product, s - RING + 1)
                nc.vector.tensor_scalar(onekey[:, s % RING, :], m.row16[:, 0:KEYS], m.keyT[:, s:s + 1], None,
                                        ALU.is_equal)
                nc.vector.tensor_scalar(oneplace[:, s % RING, :], m.row16[:, 0:P], m.lowT[:, s:s + 1], None,
                                        ALU.is_equal).then_inc(onehot, 1)

            for s in range(LEAD):
                onehots(s)
            v.wait_ge(cleared, 2)
            regs = [v.alloc_register(f"window{j}") for j in range(PER)]
            for s in range(SLOTS):
                if s % PER == 0:
                    v.load(regs, m.off[0:1, s:s + PER])
                if s + LEAD < SLOTS:
                    onehots(s + LEAD)
                window = m.at[:, :, bass.ds(v.snap(regs[s % PER], min_val=0, max_val=(NW - 1) * W), W)]
                v.wait_ge(copied, s // 2 + 1)
                if s >= 1:
                    v.wait_ge(added, s)
                nc.vector.tensor_tensor(window, window,
                                        counts[:, s // 2 % PAIRS, s % 2, :].rearrange("p (i w) -> p i w", w=W),
                                        ALU.add).then_inc(added, 1)

        @b.tensor
        def _(pe):
            for s in range(SLOTS):
                pe.wait_ge(onehot, s + 1)
                if s >= 16 and s % 2 == 0:
                    pe.wait_ge(copied, s // 2 - 8 + 1)
                nc.tensor.matmul(m.ps[:, s // 2 % 8, 256 * (s % 2):256 * (s % 2) + KEYS], oneplace[:, s % RING, :],
                                 onekey[:, s % RING, :], start=True, stop=True).then_inc(product, 1)


def bucket_ranks(nc, m, d):
    with stage(nc, "ranks") as (c, sem):
        sb = carver(m.at[:, KEPT:RANKED, :])
        inti, hii, onehi, cnt, srci = sb("inti2", [P, T], I32), m.srchi, m.src_blocks, m.row_counts, m.src_early
        dsti = sb("dsti2", [P, T], I32)
        w, rec = sb("w", [P, T], F32), sb("rec", [P, T, 4], I32)
        mask = sb("mask", [P, 2, T], I32)
        run, acc, tmp = sb("run", [P, 2, T], F32), sb("acc", [P, T], F32), sb("tmp", [P, T], F32)
        one = sb("one_row", [P, T], F32)
        tiles, base = sb("tiles", [P, NB], F32), sb("base", [P, NB], F32)
        cnti = sb("cnti", [P, NB], I32)
        rank = sb("rank", [P, T], I32)
        zeros = sb("zeros", [P, BT * 4 // 16], I32)
        chain, summed, clear = sem("rank_chain"), sem("count_sums"), sem("space_cleared")
        cleared, tabz = sem("zeros_made"), sem("table_cleared")
        ld, made, stored = sem("edges_loaded"), sem("records_made"), sem("records_stored")
        b = c.enter_context(nc.Block())

        @b.gpsimd
        def _(g):
            nc.gpsimd.memset(m.at[:, RANKED:EARLY, :], 0.0).then_inc(clear, 1)
            g.wait_ge(clear, 1)

        @b.sync
        def _(sp):
            sp.dma_start(dsti[:], d.dst_s).then_inc(ld, 16)
            sp.dma_start(w[:], d.w_s).then_inc(ld, 16)
            sp.wait_ge(cleared, 1)
            for q in range(16):
                n = BT * 4 // 16
                sp.dma_start(d.table.rearrange("(p t) c -> p (t c)", p=P)[:, q * n:(q + 1) * n], zeros[:]).then_inc(tabz, 16)
            sp.wait_ge(made, 1)
            sp.dma_start(d.rec, rec[:]).then_inc(stored, 16)
            sp.wait_ge(tabz, 256)
            sp.wait_ge(stored, 16)

        @b.vector
        def _(v):
            do = Chain(v, chain)
            nc.vector.memset(zeros[:], 0).then_inc(cleared, 1)
            do(nc.vector.memset(one[:], 1.0))
            v.wait_ge(ld, 32)
            do(nc.vector.tensor_scalar(inti[:], srci[:], P - 1, None, ALU.bitwise_and))
            nc.vector.tensor_copy(rec[:, :, 0:1], dsti[:].unsqueeze(2))
            nc.vector.tensor_copy(rec[:, :, 1:2], inti[:].unsqueeze(2))
            do(nc.vector.tensor_copy(rec[:, :, 2:3], w[:].bitcast(I32).unsqueeze(2)))
            v.wait_ge(summed, 1)
            do(nc.vector.tensor_scalar(tiles[:], m.ps[:, 1, 0:NB], float(P - 1), None, ALU.add))
            do(nc.vector.tensor_copy(cnti[:], tiles[:]))
            do(nc.vector.tensor_scalar(cnti[:], cnti[:], 7, None, ALU.logical_shift_right))
            do(nc.vector.tensor_copy(tiles[:], cnti[:]))
            do(nc.vector.tensor_tensor_scan(base[:], one[:, 0:NB], tiles[:], 0.0, ALU.mult, ALU.add))
            do(nc.vector.tensor_tensor(base[:], base[:], tiles[:], ALU.subtract))
            do(nc.vector.tensor_copy(m.first_tile[:], base[:]))
            do(nc.vector.tensor_scalar(base[:], base[:], float(P), -1.0, ALU.mult, ALU.add))
            do(nc.vector.tensor_tensor(base[:], base[:], m.ps[:, 0, 0:NB], ALU.add))
            for i in range(NB + 1):
                if i < NB:
                    nc.vector.tensor_scalar(mask[:, i % 2, :], hii[:], float(i), None, ALU.is_equal)
                if i >= 1:
                    do(nc.vector.copy_predicated(acc[:], mask[:, (i - 1) % 2, :], run[:, (i - 1) % 2, :]))
                if i < NB:
                    do(nc.vector.tensor_tensor_scan(run[:, i % 2, :], one[:], onehi[:, i, :], base[:, i:i + 1],
                                                    ALU.mult, ALU.add))
            do(nc.vector.tensor_copy(rank[:], acc[:]))
            do(nc.vector.tensor_scalar(inti[:], rank[:], 7, None, ALU.logical_shift_right))
            do(nc.vector.tensor_scalar(hii[:], rank[:], P - 1, None, ALU.bitwise_and))
            do(nc.vector.tensor_copy(tmp[:], inti[:]))
            do(nc.vector.tensor_copy(acc[:], hii[:]))
            do(nc.vector.scalar_tensor_tensor(acc[:], acc[:], float(BT), tmp[:], ALU.mult, ALU.add))
            nc.vector.tensor_copy(rec[:, :, 3:4], acc[:].unsqueeze(2)).then_inc(made, 1)

        @b.tensor
        def _(pe):
            nc.tensor.matmul(m.ps[:, 0, 0:NB], m.upper[:], cnt[:], start=True, stop=True)
            nc.tensor.matmul(m.ps[:, 1, 0:NB], m.ones[:], cnt[:], start=True, stop=True).then_inc(summed, 1)


def count_product(nc, m, parts, blk, bank, before=None):
    for s in range(NB):
        if before:
            before(s)
        mm = nc.tensor.matmul(m.ps[:, bank, 0:2 * D], m.at[:, s, blk * P:(blk + 1) * P], parts[:, s, :],
                              start=(s == 0), stop=(s == NB - 1))
    return mm


def appnp(nc, m, d):
    with stage(nc, "l0") as (c, sem):
        sb = lambda n, s, t: c.enter_context(nc.sbuf_tensor(n, s, t))
        parts = sb("parts", [P, 2, NB, 2 * D], F16)
        g0 = sb("g0", [P, NB, D], F32)
        coef = sb("coef", [P, NB], F32)
        t1 = sb("t1", [P, 2, D], F32)
        t2 = sb("t2", [P, 2, D], F32)
        gm, ga = sb("gm", [P, 1], F32), sb("ga", [P, 1], F32)
        back = sb("back", [P, NB], F32)
        un, scl = sb("un0", [P, 1], F32), sb("scl0", [P, 1], F32)
        recs = sb("recs", [P, 2, HALF[0], 4], I32)
        chain, mx, amx, ready = sem("l0_chain"), sem("g_max"), sem("g_max_all"), sem("g_parts")
        prod, taken, high = sem("l0_products"), sem("l0_product_taken"), sem("high_part")
        tmp1, turns = sem("l0_partial"), sem("turns")
        staged, scat = [sem("records_a"), sem("records_b")], [sem("scattered_a"), sem("scattered_b")]
        b = c.enter_context(nc.Block())
        NBK = 5

        @b.gpsimd
        def _(g):
            g.wait_ge(mx, 1)
            nc.gpsimd.partition_all_reduce(ga[:], gm[:], P, RMAX).then_inc(amx, 1)
            with g.Fori(0, T // TURN) as k:
                for h, n in enumerate(HALF):
                    g.wait_ge(staged[h], 16 * k + 16)
                    g.sem_inc(turns, 1)
                    for j in range(n):
                        nc.gpsimd.indirect_dma_start(d.table, bass.IndirectOffsetOnAxis(recs[:, h, j, 3:4], 0),
                                                     recs[:, h, j, :], None).then_inc(scat[h], 16)
            for h, n in enumerate(HALF):
                g.wait_ge(scat[h], 16 * n * (T // TURN))

        @b.scalar
        def _(a):
            square_root(nc, a, m, 2, m.st2[:])

        @b.sync
        def _(sp):
            for h, n in enumerate(HALF):
                sp.dma_start(recs[:, h, 0:n, :], d.rec[:, h * HALF[0]:h * HALF[0] + n, :]).then_inc(staged[h], 16)
            with sp.Fori(1, T // TURN) as k:
                for h, n in enumerate(HALF):
                    sp.wait_ge(scat[h], 16 * n * k)
                    sp.dma_start(recs[:, h, 0:n, :], d.rec[:, bass.ds(k * TURN + h * HALF[0], n), :]).then_inc(staged[h], 16)

        @b.vector
        def _(v):
            do = Chain(v, chain)
            do(nc.vector.tensor_tensor(g0[:], m.x[:], bc_last(m.dinv[:], D), ALU.mult))
            nc.vector.tensor_reduce(gm[:], g0[:].rearrange("p i f -> p (i f)"), AX.X, ALU.max, apply_absolute_value=True).then_inc(mx, 1)
            for i in range(NB):
                blk = m.at[:, i, i * P:(i + 1) * P]
                nc.vector.tensor_tensor(blk, blk, m.ident16[:], ALU.add)
            do(nc.vector.tensor_tensor(coef[:], m.dinv[:], m.dinv[:], ALU.mult))
            do(nc.vector.tensor_scalar(coef[:], coef[:], 1.0 - ALPHA, None, ALU.mult))
            v.wait_ge(amx, 1)
            scale_of(nc, do, m, ga[:], scl[:], un[:])
            do(nc.vector.tensor_scalar(g0[:], g0[:], scl[:], None, ALU.mult))
            do(nc.vector.tensor_copy(parts[:, 0, :, 0:D], g0[:]))
            do(nc.vector.tensor_tensor(parts[:, 0, :, D:2 * D], g0[:], parts[:, 0, :, 0:D], ALU.subtract))
            v.sem_inc(ready, NB)
            do(nc.vector.tensor_scalar(g0[:], g0[:], ALPHA, None, ALU.mult))
            do(nc.vector.tensor_scalar(back[:], m.deg[:], 1.0, None, ALU.add))
            do(nc.vector.tensor_tensor(back[:], back[:], m.dinv[:], ALU.mult))
            do(nc.vector.tensor_scalar(back[:], back[:], un[:], None, ALU.mult))
            with v.Fori(0, STEPS // 2) as k:
                for r in range(2 * NB):
                    i, nxt = r % NB, 1 - r // NB
                    v.wait_ge(prod, 2 * NB * k + (r + 1))
                    nc.vector.scalar_tensor_tensor(t1[:, r % 2, :], m.ps[:, r % NBK, 0:D], coef[:, i:i + 1],
                                                   g0[:, i, :], ALU.mult, ALU.add).then_inc(tmp1, 1)
                    v.wait_ge(tmp1, 4 * NB * k + (2 * r + 1))
                    nc.vector.scalar_tensor_tensor(t2[:, r % 2, :], m.ps[:, r % NBK, D:2 * D], coef[:, i:i + 1],
                                                   t1[:, r % 2, :], ALU.mult, ALU.add).then_inc(tmp1, 1)
                    v.wait_ge(tmp1, 4 * NB * k + (2 * r + 2))
                    v.sem_inc(taken, 1)
                    nc.vector.tensor_copy(parts[:, nxt, i, 0:D], t2[:, r % 2, :]).then_inc(high, 1)
                    v.wait_ge(high, 2 * NB * k + (r + 1))
                    nc.vector.tensor_tensor(parts[:, nxt, i, D:2 * D], t2[:, r % 2, :], parts[:, nxt, i, 0:D],
                                            ALU.subtract).then_inc(ready, 1)
            v.wait_ge(ready, NB * (STEPS + 1))
            do(nc.vector.tensor_tensor(g0[:], parts[:, 0, :, 0:D], parts[:, 0, :, D:2 * D], ALU.add))
            do(nc.vector.tensor_tensor(g0[:], g0[:], bc_last(back[:], D), ALU.mult))
            do(nc.vector.tensor_tensor(g0[:], g0[:], m.x[:], ALU.add))
            sq = parts[:].rearrange("p a i f -> p (a i f)").bitcast(F32)[:, 0:NB * D]
            layer_norm(nc, v, do, m, m.x, g0, sq.rearrange("p (i f) -> p i f", f=D), 2)

        @b.tensor
        def _(pe):
            pe.sem_inc(taken, NBK)
            with pe.Fori(0, STEPS // 2) as k:
                for r in range(2 * NB):
                    pe.wait_ge(taken, 2 * NB * k + (r + 1))
                    before = (lambda s: pe.wait_ge(ready, 2 * NB * k + (r + s + 1))) if r % NB == 0 else None
                    count_product(nc, m, parts[:, r // NB], r % NB, r % NBK, before).then_inc(prod, 1)


def sage(nc, m, d, layer):
    with stage(nc, f"l1_{layer}") as (c, sem):
        sb = lambda n, s, t: c.enter_context(nc.sbuf_tensor(n + f"_{layer}", s, t))
        w0, w1 = sb("w0", [D, D], F32), sb("w1", [D, D], F32)
        w2a, w2b = sb("w2a", [D, D], F32), sb("w2b", [D, D], F32)
        b0, b1, b2 = sb("b0", [P, D], F32), sb("b1", [D, 1], F32), sb("b2", [P, D], F32)
        y = m.y
        nb = sb("nb", [P, NB, D], F32)
        parts = sb("nbparts", [P, NB, 2 * D], F16)
        early = carver(parts[:])
        xT, hsT = early("xT", [D, 2, GROUP * P], F32), early("hsT", [D, 2, GROUP * P], F32)
        agg, aggT = sb("agg", [P, 2, D], F32), sb("aggT", [D, 2, P], F32)
        gm, ga = sb("gm1", [P, 1], F32), sb("ga1", [P, 1], F32)
        un, scl = sb("un1", [P, 1], F32), sb("scl1", [P, 1], F32)
        wl, chain = sem("sage_weights"), sem("sage_chain")
        turned, xcp, nbd, hsd = sem("x_turned"), sem("xT_copied"), sem("nb_product"), sem("hs_product")
        nbc, hsc, outd, outc = sem("nb_copied"), sem("hs_copied"), sem("self_out"), sem("self_out_taken")
        mx, amx, ready = sem("nb_max"), sem("nb_max_all"), sem("nb_parts")
        prod, aggc, aggt, aggtc = sem("agg_product"), sem("agg_copied"), sem("agg_turned"), sem("aggT_copied")
        outb, outbc, half = sem("agg_out"), sem("agg_out_taken"), sem("agg_half")
        b = c.enter_context(nc.Block())
        src = m.x if layer == 0 else m.y

        @b.sync
        def _(sp):
            sp.dma_start(w0[:], d.W0[layer]).then_inc(wl, 16)
            sp.dma_start(w1[:], d.W1[layer]).then_inc(wl, 16)
            sp.dma_start(w2a[:], d.W2[layer, 0:D, :]).then_inc(wl, 16)
            sp.dma_start(w2b[:], d.W2[layer, D:2 * D, :]).then_inc(wl, 16)
            sp.dma_start(b0[:], d.b0[layer:layer + 1, :].to_broadcast([P, D])).then_inc(wl, 16)
            sp.dma_start(b2[:], d.b2[layer:layer + 1, :].to_broadcast([P, D])).then_inc(wl, 16)
            sp.dma_start(b1[:], d.b1[layer].rearrange("(f a) -> f a", a=1), allow_slow_non_contiguous=True).then_inc(wl, 16)
            sp.wait_ge(wl, 112)

        @b.gpsimd
        def _(g):
            g.wait_ge(mx, 1)
            nc.gpsimd.partition_all_reduce(ga[:], gm[:], P, RMAX).then_inc(amx, 1)

        @b.scalar
        def _(a):
            for g in range(NG + 1):
                if g < NG:
                    n = GROUPS[g][1] * P
                    a.wait_ge(turned, g + 1)
                    if g >= 2:
                        a.wait_ge(nbd, g - 1)
                    nc.scalar.activation(xT[:, g % 2, 0:n], m.ps[0:D, g % 2, 0:n], ACT.Copy).then_inc(xcp, 1)
                if g >= 1:
                    q, n = g - 1, GROUPS[g - 1][1] * P
                    if q == 0:
                        a.wait_ge(wl, 112)
                    a.wait_ge(hsd, q + 1)
                    if q >= 2:
                        a.wait_ge(outd, q - 1)
                    nc.scalar.activation(hsT[:, q % 2, 0:n], m.ps[0:D, 4 + q % 2, 0:n], ACT.Identity,
                                         bias=b1[:]).then_inc(hsc, 1)
            for i in range(NB):
                a.wait_ge(aggt, i + 1)
                if i >= 2:
                    a.wait_ge(outb, i - 1)
                nc.scalar.activation(aggT[:, i % 2, :], m.ps[0:D, 4 + i % 2, 0:P], ACT.Copy).then_inc(aggtc, 1)
            square_root(nc, a, m, 3 + layer, m.st2[:])
            if layer == 1:
                square_root(nc, a, m, 5, m.st2[:])

        @b.vector
        def _(v):
            do = Chain(v, chain)
            if layer == 0:
                for i in range(NB):
                    blk = m.at[:, i, i * P:(i + 1) * P]
                    nc.vector.tensor_tensor(blk, blk, m.ident16[:], ALU.subtract)
            v.wait_ge(wl, 112)
            for g in range(NG + 1):
                if g < NG:
                    a, n = GROUPS[g]
                    v.wait_ge(nbd, g + 1)
                    nc.vector.tensor_tensor(nb[:, a:a + n, :], blocks_of(m.ps[:, 2 + g % 2, 0:n * D]),
                                            bc_mid(b0[:], n), ALU.add).then_inc(nbc, 1)
                if g >= 1:
                    q, (a, n) = g - 1, GROUPS[g - 1]
                    v.wait_ge(outd, q + 1)
                    nc.vector.tensor_tensor(y[:, a:a + n, :], blocks_of(m.ps[:, 6 + q % 2, 0:n * D]),
                                            bc_mid(b2[:], n), ALU.add).then_inc(outc, 1)
            v.wait_ge(nbc, NG)
            v.wait_ge(outc, NG)
            nc.vector.tensor_reduce(gm[:], nb[:].rearrange("p i f -> p (i f)"), AX.X, ALU.max, apply_absolute_value=True).then_inc(mx, 1)
            v.wait_ge(amx, 1)
            scale_of(nc, do, m, ga[:], scl[:], un[:])
            do(nc.vector.tensor_scalar(nb[:], nb[:], scl[:], None, ALU.mult))
            do(nc.vector.tensor_copy(parts[:, :, 0:D], nb[:]))
            nc.vector.tensor_tensor(parts[:, :, D:2 * D], nb[:], parts[:, :, 0:D], ALU.subtract).then_inc(ready, 1)
            for i in range(NB + 2):
                if i < NB:
                    v.wait_ge(prod, i + 1)
                    if i >= 2:
                        v.wait_ge(aggt, i - 1)
                    nc.vector.tensor_scalar(agg[:, i % 2, :], m.ps[:, i % 4, 0:D], un[:], None,
                                            ALU.mult).then_inc(half, 1)
                    v.wait_ge(half, i + 1)
                    nc.vector.scalar_tensor_tensor(agg[:, i % 2, :], m.ps[:, i % 4, D:2 * D], un[:],
                                                   agg[:, i % 2, :], ALU.mult, ALU.add).then_inc(aggc, 1)
                if i >= 2:
                    q = i - 2
                    v.wait_ge(outb, q + 1)
                    nc.vector.tensor_tensor(y[:, q, :], y[:, q, :], m.ps[:, 6 + q % 2, 0:D], ALU.add).then_inc(outbc, 1)
            v.wait_ge(outbc, NB)
            do(nc.vector.tensor_reduce(m.st1[:], y[:], AX.X, ALU.add))
            do(nc.vector.tensor_scalar(m.st1[:], m.st1[:], 1.0 / D, None, ALU.mult))
            do(nc.vector.tensor_tensor(nb[:], y[:], bc_last(m.st1[:], D), ALU.subtract))
            do(nc.vector.tensor_tensor(nb[:], nb[:], nb[:], ALU.mult))
            do(nc.vector.tensor_reduce(m.st2[:], nb[:], AX.X, ALU.add))
            nc.vector.scalar_tensor_tensor(m.st2[:], m.st2[:], 1.0 / (D - 1), m.padcol[:], ALU.mult,
                                           ALU.add).then_inc(m.var_ready, 1)
            inverse_root(nc, v, do, m, 3 + layer, m.st2[:])
            do(nc.vector.tensor_tensor(y[:], y[:], bc_last(m.st2[:], D), ALU.mult))
            if layer == 1:
                do(nc.vector.tensor_tensor(y[:], y[:], m.x[:], ALU.add))
                layer_norm(nc, v, do, m, m.x, y, nb, 5)

        @b.tensor
        def _(pe):
            for g in range(NG + 2):
                if g < NG:
                    a, n = GROUPS[g]
                    if g >= 2:
                        pe.wait_ge(xcp, g - 1)
                    for j in range(n):
                        tr = nc.tensor.transpose(m.ps[0:D, g % 2, j * P:(j + 1) * P], src[:, a + j, :], m.ident[:])
                    tr.then_inc(turned, 1)
                if 1 <= g <= NG:
                    q, n = g - 1, GROUPS[g - 1][1]
                    if q == 0:
                        pe.wait_ge(wl, 112)
                    pe.wait_ge(xcp, q + 1)
                    if q >= 2:
                        pe.wait_ge(nbc, q - 1)
                        pe.wait_ge(hsc, q - 1)
                    nc.tensor.matmul(m.ps[0:D, 4 + q % 2, 0:n * P], w1[:], xT[:, q % 2, 0:n * P], start=True,
                                     stop=True).then_inc(hsd, 1)
                    for j in range(n):
                        mm = nc.tensor.matmul(m.ps[:, 2 + q % 2, j * D:(j + 1) * D], xT[:, q % 2, j * P:(j + 1) * P],
                                              w0[:], start=True, stop=True)
                    mm.then_inc(nbd, 1)
                if g >= 2:
                    q, n = g - 2, GROUPS[g - 2][1]
                    pe.wait_ge(hsc, q + 1)
                    if q >= 2:
                        pe.wait_ge(outc, q - 1)
                    for j in range(n):
                        mm = nc.tensor.matmul(m.ps[:, 6 + q % 2, j * D:(j + 1) * D], hsT[:, q % 2, j * P:(j + 1) * P],
                                              w2a[:], start=True, stop=True)
                    mm.then_inc(outd, 1)
            pe.wait_ge(ready, 1)
            for i in range(NB + 2):
                if i < NB:
                    if i >= 4:
                        pe.wait_ge(aggc, i - 3)
                    count_product(nc, m, parts, i, i % 4).then_inc(prod, 1)
                if 1 <= i <= NB:
                    q = i - 1
                    pe.wait_ge(aggc, q + 1)
                    if q >= 2:
                        pe.wait_ge(aggtc, q - 1)
                    nc.tensor.transpose(m.ps[0:D, 4 + q % 2, 0:P], agg[:, q % 2, :], m.ident[:]).then_inc(aggt, 1)
                if i >= 2:
                    q = i - 2
                    pe.wait_ge(aggtc, q + 1)
                    if q >= 2:
                        pe.wait_ge(outbc, q - 1)
                    nc.tensor.matmul(m.ps[:, 6 + q % 2, 0:D], aggT[:, q % 2, :], w2b[:], start=True,
                                     stop=True).then_inc(outb, 1)


def weighted_sum(nc, m, d):
    with stage(nc, "l2") as (c, sem):
        sb = lambda n, s, t: c.enter_context(nc.sbuf_tensor(n, s, t))
        R = 16
        tab = sb("tab", [P, BT, 4], I32)
        low, wt = sb("low", [P, BT], F32), sb("wt", [P, BT], F32)
        targets = sb("targets", [P, BT], I32)
        ti, tf = sb("target_parts_i", [P, 2, BT], I32), sb("target_parts", [P, 2, BT], F32)
        rows = sb("rows", [P, R, D], F32)
        onew = sb("onew", [P, 4, P], F32)
        sq = sb("sq2", [P, NB, D], F32)
        acc = sb("acc2", [P, NB * D], F32)
        tcol, below = sb("tile_column", [P, TG], F32), sb("below", [P, TG, NB], F32)
        tblock = sb("tile_block", [P, TG], F32)
        tiled, trow = sem("tile_blocks"), sem("tile_blocks_in_row")
        dsti = sb("dsti3", [P, T], I32)
        prev, dstf, prevf = sb("prev", [P, 1], I32), sb("dstf", [P, T], F32), sb("prevf", [P, 1], F32)
        cont, mcol = sb("cont", [P, 1], F32), sb("mcol", [P, 1], F32)
        mrep, rem = sb("mrep", [P, D], F32), sb("rem", [P, NB], F32)
        e_end, q_end, q_start = sb("e_end", [P, NB], F32), sb("q_end", [P, NB], F32), sb("q_start", [P, NB], F32)
        eld = sem("edges_loaded3")
        z, ld, wl = sem("prev_cleared"), sem("prev_loaded"), sem("conv_weights")
        rep, rowd = sem("carry_column"), sem("carry_row")
        loaded, chain, xst = sem("table_loaded"), sem("l2_chain"), sem("x_stored")
        split = sem("targets_split")
        got = [sem(f"row_{j}_gathered") for j in range(R)]
        hot, prod, add = sem("weighted_onehots"), sem("l2_products"), sem("l2_added")
        b = c.enter_context(nc.Block())

        @b.sync
        def _(sp):
            sp.dma_start(tab[:], d.table.rearrange("(p t) c -> p t c", p=P)).then_inc(loaded, 16)
            sp.dma_start(dsti[:], d.dst_s).then_inc(eld, 16)
            sp.wait_ge(z, 1)
            sp.dma_start(prev[1:P, :], d.dst_s[0:P - 1, T - 1:T], allow_slow_non_contiguous=True).then_inc(ld, 16)
            sp.dma_start(d.xt.rearrange("(p i) f -> p i f", p=P), m.x[:]).then_inc(xst, 16)
            sp.wait_ge(xst, 16)

        @b.gpsimd
        def _(g):
            g.wait_ge(split, 1)
            g.wait_ge(xst, 16)
            for t in range(BT):
                if t >= R:
                    g.wait_ge(prod, R + t - R + 1)
                nc.gpsimd.indirect_dma_start(rows[:, t % R, :], None, d.xt,
                                             bass.IndirectOffsetOnAxis(targets[:, t:t + 1], 0)).then_inc(got[t % R], 16)

        @b.vector
        def _(v):
            do = Chain(v, chain)
            nc.vector.memset(prev[:], -1).then_inc(z, 1)
            do(nc.vector.memset(acc[:], 0.0))
            v.wait_ge(loaded, 16)
            nc.vector.tensor_scalar(ti[:, 0, :], tab[:, :, 0], 7, None, ALU.logical_shift_right)
            do(nc.vector.tensor_scalar(ti[:, 1, :], tab[:, :, 0], P - 1, None, ALU.bitwise_and))
            do(nc.vector.tensor_copy(tf[:], ti[:]))
            do(nc.vector.scalar_tensor_tensor(tf[:, 0, :], tf[:, 1, :], float(NB), tf[:, 0, :], ALU.mult, ALU.add))
            nc.vector.tensor_copy(targets[:], tf[:, 0, :]).then_inc(split, 1)
            do(nc.vector.tensor_copy(low[:], tab[:, :, 1]))
            do(nc.vector.tensor_copy(wt[:], tab[:, :, 2].bitcast(F32)))
            for k in range(TG):
                nc.vector.tensor_scalar(tcol[:, k:k + 1], m.col[:], float(k * P), None, ALU.add)
            do(nc.vector.memset(below[:], 0.0))
            for k in range(TG):
                ins = nc.vector.tensor_scalar(below[:, k, :], m.first_tile[:], tcol[:, k:k + 1], 0.0, ALU.is_le, ALU.add,
                                              accum_out=tblock[:, k:k + 1])
            do(ins)
            nc.vector.tensor_scalar(tblock[:], tblock[:], float(D), -float(D), ALU.mult, ALU.add).then_inc(tiled, 1)
            v.wait_ge(eld, 16)
            do(nc.vector.tensor_copy(dstf[:], dsti[:]))
            do(nc.vector.memset(m.brk[:], 0.0))
            do(nc.vector.tensor_tensor(m.brk[:, 1:T], dstf[:, 1:T], dstf[:, 0:T - 1], ALU.not_equal))
            do(nc.vector.tensor_scalar(m.brk[:], m.brk[:], -BIG, None, ALU.mult))
            v.wait_ge(ld, 16)
            do(nc.vector.tensor_copy(prevf[:], prev[:]))
            do(nc.vector.tensor_tensor(cont[:], dstf[:, 0:1], prevf[:], ALU.is_equal))
            do(nc.vector.tensor_tensor(mcol[:], dstf[:, 0:1], dstf[:, T - 1:T], ALU.is_equal))
            do(nc.vector.tensor_tensor(mcol[:], mcol[:], cont[:], ALU.mult))
            do(nc.vector.tensor_scalar(mcol[:], mcol[:], 1.0, BIG, ALU.subtract, ALU.mult))
            nc.vector.tensor_scalar(mrep[:], m.ones[:, 0:D], mcol[:], None, ALU.mult).then_inc(rep, 1)
            do(nc.vector.tensor_tensor(e_end[:], m.rowptr[:], m.deg[:], ALU.add))
            do(nc.vector.tensor_scalar(e_end[:], e_end[:], 1.0, 0.0, ALU.subtract, ALU.max))
            do(nc.vector.tensor_copy(m.endi[:], e_end[:]))

            def stream_of(out, x):
                do(nc.vector.tensor_scalar(out[:], x[:], 1.0 / T, 0.5 / T - 0.5, ALU.mult, ALU.add))
                do(nc.vector.tensor_copy(m.streami[:], out[:]))
                do(nc.vector.tensor_copy(out[:], m.streami[:]))
                do(nc.vector.scalar_tensor_tensor(rem[:], out[:], -float(T), x[:], ALU.mult, ALU.add))
                do(nc.vector.scalar_tensor_tensor(out[:], rem[:], float(T), out[:], ALU.is_ge, ALU.add))
                do(nc.vector.tensor_scalar(rem[:], rem[:], 0.0, None, ALU.is_lt))
                do(nc.vector.tensor_tensor(out[:], out[:], rem[:], ALU.subtract))
                do(nc.vector.tensor_copy(m.streami[:], out[:]))

            stream_of(q_start, m.rowptr)
            stream_of(q_end, e_end)
            do(nc.vector.tensor_copy(m.last_stream[:], q_end[:]))
            do(nc.vector.tensor_tensor(m.nocarry[:], q_start[:], q_end[:], ALU.is_ge))
            do(nc.vector.tensor_scalar(m.nocarry[:], m.nocarry[:], -BIG, None, ALU.mult))
            do(nc.vector.tensor_scalar(m.some[:], m.deg[:], 0.0, None, ALU.is_gt))
            v.wait_ge(rowd, 1)
            do(nc.vector.tensor_copy(m.mrow[:], m.ps[0:D, 1, 0:P]))
            v.wait_ge(trow, 1)
            do(nc.vector.tensor_copy(m.bucket[:], m.ps[0:1, 0, 0:BT]))
            regs = [v.alloc_register(f"bucket{j}") for j in range(R)]
            v.sem_inc(add, 8)
            with v.Fori(0, BT // R) as k:
                for j in range(0, R, 4):
                    v.load(regs[j:j + 4], m.bucket[0:1, bass.ds(R * k + j, 4)])
                at = [v.snap(r, min_val=0, max_val=(NB - 1) * D) for r in regs]
                for j in range(R + 1):
                    if j < R:
                        v.wait_ge(prod, R * k + (j + R - 3))
                        nc.vector.tensor_scalar(onew[:, j % 4, :], m.row[:, 0:P], low[:, bass.ds(R * k + j, 1)],
                                                wt[:, bass.ds(R * k + j, 1)], ALU.is_equal,
                                                ALU.mult).then_inc(hot, 1)
                    if j >= 1:
                        q = j - 1
                        v.wait_ge(prod, R * k + (q + R + 1))
                        v.wait_ge(add, R * k + (q + 8))
                        dst = acc[:, bass.ds(at[q], D)]
                        nc.vector.tensor_tensor(dst, dst, m.ps[:, q % 8, 0:D], ALU.add).then_inc(add, 1)
            v.wait_ge(add, BT + 8)
            s = acc[:].rearrange("p (i f) -> p i f", f=D)
            do(nc.vector.tensor_tensor(s, s, m.x[:], ALU.add))
            layer_norm(nc, v, do, m, m.x, s, sq, 6)

        @b.scalar
        def _(a):
            a.wait_ge(ld, 16)
            a.dma_start(m.srci[:], d.src_s).then_inc(wl, 16)
            for k in range(2):
                a.dma_start(m.wmr[:, k, 0:D], d.Wmsg[k]).then_inc(wl, 16)
                a.dma_start(m.wmr[:, k, D:2 * D], d.Wroot[k]).then_inc(wl, 16)
                a.dma_start(m.we[:, k, :], d.Wedge[k]).then_inc(wl, 16)
                a.dma_start(m.bias[:, k, :], d.bias[k].rearrange("(a f) -> a f", a=1).to_broadcast([P, D])).then_inc(wl, 16)
            a.wait_ge(wl, 144)
            square_root(nc, a, m, 6, m.st2[:])

        @b.tensor
        def _(pe):
            pe.wait_ge(tiled, 1)
            for k in range(TG):
                mm = nc.tensor.matmul(m.ps[0:1, 0, k * P:(k + 1) * P], tblock[:, k:k + 1], m.ident[:], start=True,
                                      stop=True)
            mm.then_inc(trow, 1)
            pe.wait_ge(rep, 1)
            nc.tensor.matmul(m.ps[0:D, 1, 0:P], mrep[:], m.ident[:], start=True, stop=True).then_inc(rowd, 1)
            pe.sem_inc(prod, R)
            with pe.Fori(0, BT // R) as k:
                for j in range(R):
                    pe.wait_ge(hot, R * k + (j + 1))
                    pe.wait_ge(got[j], 16 * k + 16)
                    pe.wait_ge(add, R * k + (j + 1))
                    nc.tensor.matmul(m.ps[:, j % 8, 0:D], onew[:, j % 4, :], rows[:, j, :], start=True,
                                     stop=True).then_inc(prod, 1)


class TableSems:

    def __init__(self, sem):
        self.turned, self.xcp = sem("x_turned"), sem("xT_copied")
        self.yd, self.yc = sem("y_product"), sem("y_copied")


def table_products(nc, pe, m, q, x, w, base, ready=None):
    for g in range(NG + 1):
        if g < NG:
            a, n = GROUPS[g]
            if ready:
                ready(a + n - 1)
            if g >= 2:
                pe.wait_ge(q.xcp, base + g - 1)
            for j in range(n):
                tr = nc.tensor.transpose(m.ps[0:D, 5 + g % 2, j * P:(j + 1) * P], x[:, a + j, :], m.ident[:])
            tr.then_inc(q.turned, 1)
        if g >= 1:
            p, (a, n) = g - 1, GROUPS[g - 1]
            pe.wait_ge(q.xcp, base + p + 1)
            if p >= 2:
                pe.wait_ge(q.yc, base + p - 1)
            for j in range(n):
                mm = nc.tensor.matmul(m.ps[:, p % 2, j * D:(j + 1) * D], m.xT[:, (a + j) * P:(a + j + 1) * P], w,
                                      start=True, stop=True)
            mm.then_inc(q.yd, 1)


def table_turned(nc, a_, m, q, base):
    for g, (a, n) in enumerate(GROUPS):
        a_.wait_ge(q.turned, base + g + 1)
        nc.scalar.activation(m.xT[:, a * P:(a + n) * P], m.ps[0:D, 5 + g % 2, 0:n * P], ACT.Copy).then_inc(q.xcp, 1)


def table_copy(nc, v, m, q, base, g):
    a, n = GROUPS[g]
    v.wait_ge(q.yd, base + g + 1)
    nc.vector.tensor_copy(m.ytab[:, a:a + n, :], blocks_of(m.ps[:, g % 2, 0:n * D])).then_inc(q.yc, 1)


def table_store(sp, m, d, q, yst, base):
    for g, (a, n) in enumerate(GROUPS):
        sp.wait_ge(q.yc, base + g + 1)
        sp.dma_start(d.yt.rearrange("(i p) f -> p i f", p=P)[:, a:a + n, :], m.ytab[:, a:a + n, :]).then_inc(yst, 16)


def edge_conv(nc, m, d, layer, out):
    with stage(nc, f"conv_{layer}") as (c, sem):
        sb = lambda n, s, t: c.enter_context(nc.sbuf_tensor(n + f"_c{layer}", s, t))
        root = sb("root", [P, NB, D], F32)
        ea = sb("ea", [DE, TURN, P], F32)
        rows = sb("rows", [P, TURN, D], F32)
        run = sb("run", [P, TURN, D], F32)
        carT, carr, lastT = sb("carT", [D, P], F32), sb("carr", [P, D], F32), sb("lastT", [D, P], F32)
        rg, cg = sb("rg", [P, NB, D], F32), sb("cg", [P, NB, D], F32)
        q, chain, ydone = TableSems(sem), sem("conv_chain"), sem("ends_done")
        yst, eal = sem("y_stored"), [sem("ea_a"), sem("ea_b")]
        got = [sem(f"row_{j}_gathered") for j in range(TURN)]
        runz = sem("run_cleared")
        msg, ran, rst = sem("messages"), sem("running_max"), [sem("run_a"), sem("run_b")]
        lt, sc, ct, cc = sem("last_turned"), sem("carries"), sem("carry_turned"), sem("carry_copied")
        rgd = [sem(f"ends_gathered_{g}") for g in range(NB // ENDS)]
        cgd, res, ost = sem("carries_selected"), sem("result"), sem("out_stored")
        rd, rc = sem("root_product"), sem("root_copied")
        if layer == 0:
            qrep = sb("stream_rep", [P, NB, P], F32)
            spread, ends, seld = sem("streams_spread"), sem("streams_in_rows"), sem("selector_made")
        b = c.enter_context(nc.Block())
        TN = T // TURN
        spans = ((0, HALF[0]), (HALF[0], HALF[1]))
        NBK = 6

        @b.sync
        def _(sp):
            if layer == 0:
                table_store(sp, m, d, q, yst, 0)
            with sp.Fori(0, TN) as k:
                for h, (a, n) in enumerate(spans):
                    sp.wait_ge(msg, TURN * k + a + n)
                    sp.dma_start(ea[:, a:a + n, :], d.eaT[:, bass.ds(k * TURN + a, n), :]).then_inc(eal[h], 16)
            if layer == 0:
                table_store(sp, m, d, q, yst, NG)
                sp.wait_ge(yst, 32 * NG)
            if layer == 1:
                sp.wait_ge(res, 1)
                sp.dma_start(out.rearrange("(i p) f -> p i f", p=P), m.x[:]).then_inc(ost, 16)
                sp.wait_ge(ost, 16)

        @b.gpsimd
        def _(g):
            if layer == 0:
                g.wait_ge(yst, 16 * NG)
            for t in range(T):
                if t >= TURN:
                    g.wait_ge(msg, TURN + t - TURN + 1)
                nc.gpsimd.indirect_dma_start(rows[:, t % TURN, :], None, d.yt,
                                             bass.IndirectOffsetOnAxis(m.srci[:, t:t + 1], 0)).then_inc(got[t % TURN], 16)
            for r in rst:
                g.wait_ge(r, 16 * TN + 16)
            for i in range(NB):
                nc.gpsimd.indirect_dma_start(rg[:, i, :], None, d.run,
                                             bass.IndirectOffsetOnAxis(m.endi[:, i:i + 1], 0)).then_inc(rgd[i // ENDS], 16)
            for r in rgd:
                g.wait_ge(r, 16 * ENDS)

        @b.scalar
        def _(a_):
            if layer == 0:
                table_turned(nc, a_, m, q, 0)
                nc.scalar.activation(qrep[:], bc_last(m.last_stream[:], P), ACT.Copy).then_inc(spread, 1)
            rdram = d.run.rearrange("(p t) f -> p t f", t=T)
            a_.wait_ge(runz, 1)
            for h, (a, n) in enumerate(spans):
                a_.dma_start(rdram[:, a:a + n, :], run[:, a:a + n, :]).then_inc(rst[h], 16)
            with a_.Fori(0, TN) as k:
                for h, (a, n) in enumerate(spans):
                    a_.wait_ge(ran, TURN * k + (a + n + TURN))
                    a_.wait_ge(rst[h], 16 * k + 16)
                    a_.dma_start(rdram[:, bass.ds(k * TURN + a, n), :], run[:, a:a + n, :]).then_inc(rst[h], 16)
            for r in rst:
                a_.wait_ge(r, 16 * TN + 16)
            if layer == 0:
                table_turned(nc, a_, m, q, NG)
            if layer == 1:
                square_root(nc, a_, m, 7, m.st2[:])

        @b.vector
        def _(v):
            do = Chain(v, chain)
            if layer == 0:
                for g in range(NG):
                    table_copy(nc, v, m, q, 0, g)
            nc.vector.memset(run[:], -BIG).then_inc(runz, 1)
            for g, (a, n) in enumerate(GROUPS):
                v.wait_ge(rd, g + 1)
                nc.vector.tensor_tensor(root[:, a:a + n, :], blocks_of(m.ps[:, 2 + g % 2, 0:n * D]),
                                        bc_mid(m.bias[:, layer, :], n), ALU.add).then_inc(rc, 1)
            if layer == 0:
                for g, (a, n) in enumerate(GROUPS):
                    v.wait_ge(ends, g + 1)
                    nc.vector.tensor_scalar(m.sel[:, a * P:(a + n) * P], m.ps[:, 4 + g % 4, 0:n * P], m.col[:], None,
                                            ALU.is_equal).then_inc(seld, 1)
            v.wait_ge(runz, 1)
            v.sem_inc(ran, TURN)
            with v.Fori(0, TN) as k:
                for h, (a, n) in enumerate(spans):
                    for j in range(a, a + n):
                        v.wait_ge(msg, TURN * k + (j + 1 + TURN))
                        if j == a:
                            v.wait_ge(rst[h], 16 * k + 16)
                        nc.vector.scalar_tensor_tensor(run[:, j, :], run[:, (j - 1) % TURN, :],
                                                       m.brk[:, bass.ds(k * TURN + j, 1)],
                                                       m.ps[:, j % NBK, 0:D], ALU.add, ALU.max).then_inc(ran, 1)
                        v.wait_ge(ran, TURN * k + (j + 1 + TURN))
            v.wait_ge(lt, 1)
            do(nc.vector.tensor_copy(lastT[:], m.ps[0:D, 6, 0:P]))
            do(nc.vector.memset(carT[:, 0:1], -BIG))
            nc.vector.tensor_tensor_scan(carT[:, 1:P], m.mrow[:, 0:P - 1], lastT[:, 0:P - 1], -BIG,
                                         ALU.add, ALU.max).then_inc(sc, 1)
            v.wait_ge(ct, 1)
            nc.vector.tensor_copy(carr[:], m.ps[:, 7, 0:D]).then_inc(cc, 1)
            for g in range(NB // ENDS):
                blk = slice(g * ENDS, (g + 1) * ENDS)
                v.wait_ge(cgd, g + 1)
                do(nc.vector.tensor_tensor(cg[:, blk, :], blocks_of(m.ps[:, g, 0:ENDS * D]),
                                           bc_last(m.nocarry[:, blk], D), ALU.add))
            copied = 0
            if layer == 0:
                v.wait_ge(yst, 16 * NG)
            for g in range(NB // ENDS):
                blk = slice(g * ENDS, (g + 1) * ENDS)
                v.wait_ge(rgd[g], 16 * ENDS)
                do(nc.vector.tensor_tensor(rg[:, blk, :], rg[:, blk, :], cg[:, blk, :], ALU.max))
                do(nc.vector.tensor_tensor(rg[:, blk, :], rg[:, blk, :], bc_last(m.some[:, blk], D), ALU.mult))
                do(nc.vector.tensor_tensor(rg[:, blk, :], rg[:, blk, :], root[:, blk, :], ALU.add))
                do(nc.vector.scalar_tensor_tensor(m.y[:, blk, :], rg[:, blk, :], 0.01, rg[:, blk, :], ALU.mult,
                                                  ALU.max))
                if layer == 0:
                    v.sem_inc(ydone, 1)
                    while sum(GROUPS[copied]) <= g * ENDS:
                        table_copy(nc, v, m, q, NG, copied)
                        copied += 1
                if layer == 1:
                    do(nc.vector.tensor_tensor(m.y[:, blk, :], m.y[:, blk, :], m.x[:, blk, :], ALU.add))
                    centre(nc, do, m, m.y, rg, blk)
            if layer == 0:
                for g in range(copied, NG):
                    table_copy(nc, v, m, q, NG, g)
            if layer == 1:
                scale_by_deviation(nc, v, do, m, m.x, m.y, 7)
                v.sem_inc(res, 1)

        @b.tensor
        def _(pe):
            if layer == 0:
                table_products(nc, pe, m, q, m.x, m.wmr[:, 0, 0:D], 0)
            for g, (a, n) in enumerate(GROUPS):
                if g >= 2:
                    pe.wait_ge(rc, g - 1)
                for j in range(n):
                    mm = nc.tensor.matmul(m.ps[:, 2 + g % 2, j * D:(j + 1) * D], m.xT[:, (a + j) * P:(a + j + 1) * P],
                                          m.wmr[:, layer, D:2 * D], start=True, stop=True)
                mm.then_inc(rd, 1)
            if layer == 0:
                pe.wait_ge(q.yc, NG)
                pe.wait_ge(spread, 1)
                for g, (a, n) in enumerate(GROUPS):
                    if g >= 4:
                        pe.wait_ge(seld, g - 3)
                    for j in range(n):
                        mm = nc.tensor.matmul(m.ps[:, 4 + g % 4, j * P:(j + 1) * P], qrep[:, a + j, :], m.ident[:],
                                              start=True, stop=True)
                    mm.then_inc(ends, 1)
                pe.wait_ge(seld, NG)
            pe.wait_ge(rc, NG)
            pe.sem_inc(msg, TURN)
            with pe.Fori(0, TN) as k:
                for h, (a, n) in enumerate(spans):
                    pe.wait_ge(eal[h], 16 * k + 16)
                    for j in range(a, a + n):
                        pe.wait_ge(got[j], 16 * k + 16)
                        pe.wait_ge(ran, TURN * k + (j + TURN - 4))
                        nc.tensor.matmul(m.ps[:, j % NBK, 0:D], ea[:, j, :], m.we[:, layer, :], start=True, stop=False)
                        nc.tensor.matmul(m.ps[:, j % NBK, 0:D], m.ident[:], rows[:, j, :], start=False,
                                         stop=True).then_inc(msg, 1)
            pe.wait_ge(ran, T + TURN)
            nc.tensor.transpose(m.ps[0:D, 6, 0:P], run[:, TURN - 1, :], m.ident[:]).then_inc(lt, 1)
            pe.wait_ge(sc, 1)
            nc.tensor.transpose(m.ps[:, 7, 0:D], carT[:], m.ident[0:D, 0:D]).then_inc(ct, 1)
            pe.wait_ge(cc, 1)
            for g in range(NB // ENDS):
                for j in range(ENDS):
                    i = g * ENDS + j
                    mm = nc.tensor.matmul(m.ps[:, g, j * D:(j + 1) * D], m.sel[:, i * P:(i + 1) * P], carr[:],
                                          start=True, stop=True)
                mm.then_inc(cgd, 1)
            if layer == 0:
                table_products(nc, pe, m, q, m.y, m.wmr[:, 1, 0:D], NG,
                               lambda i: pe.wait_ge(ydone, i // ENDS + 1))


def program(nc, x, src_s, dst_s, w_s, src_rows, dst_rows, eaT, W0, b0, W1, b1, W2, b2,
            Wm1, We1, Wr1, c1, Wm2, We2, Wr2, c2, out):
    dram = lambda n, s, t: nc.dram_tensor(n, s, t).ap()
    d = Names()
    d.x, d.src_s, d.dst_s, d.w_s, d.src_rows, d.dst_rows, d.eaT = x, src_s, dst_s, w_s, src_rows, dst_rows, eaT
    d.W0, d.b0, d.W1, d.b1, d.W2, d.b2 = W0, b0, W1, b1, W2, b2
    d.Wmsg, d.Wedge, d.Wroot, d.bias = [Wm1, Wm2], [We1, We2], [Wr1, Wr2], [c1, c2]
    d.ptr, d.off = dram("ptr", [16 * NB], F32), dram("off", [SG * P], I32)
    d.table, d.rec = dram("table", [P * BT, 4], I32), dram("records", [P, T, 4], I32)
    d.xt, d.yt = dram("x_table", [NP, D], F32), dram("y_table", [NP, D], F32)
    d.run = dram("run_max", [EP, D], F32)
    with ExitStack() as c:
        sb = lambda n, s, t: c.enter_context(nc.sbuf_tensor(n, s, t))
        m = Names()
        m.ps = c.enter_context(nc.psum_tensor("ps", [P, 8, 512], F32))
        m.x = sb("x_sb", [P, NB, D], F32)
        m.row, m.row16, m.col = sb("row", [P, 256], F32), sb("row16", [P, 256], F16), sb("col", [P, 1], F32)
        m.ident, m.ident16 = sb("ident", [P, P], F32), sb("ident16", [P, P], F16)
        m.upper, m.neglow16 = sb("upper", [P, P], F32), sb("neglow16", [P, P], F16)
        m.ones, m.ones16 = sb("ones", [P, P], F32), sb("ones16", [P, P], F16)
        m.deg, m.dinv, m.rowptr = sb("deg", [P, NB], F32), sb("dinv", [P, NB], F32), sb("rowptr", [P, NB], F32)
        m.padcol = sb("padcol", [P, NB], F32)
        m.sd, m.nt = sb("sd", [P, NB], F32), sb("nt", [P, NB], F32)
        m.var_ready, m.root_done = c.enter_context(nc.semaphore("variances")), c.enter_context(nc.semaphore("roots"))
        m.st1, m.st2 = sb("st1", [P, NB], F32), sb("st2", [P, NB], F32)
        m.ki, m.kf, m.kg = sb("ki", [P, 1], I32), sb("kf", [P, 1], F32), sb("kg", [P, 1], F32)
        m.first_tile, m.bucket = sb("first_tile", [P, NB], F32), sb("bucket", [1, BT], I32)
        with ExitStack() as with_at:
            m.at = with_at.enter_context(nc.sbuf_tensor("at", [P, NB, NP], F16))
            with ExitStack() as k:
                m.keyT = k.enter_context(nc.sbuf_tensor("keyT", [P, SG * P], F32))
                m.lowT = k.enter_context(nc.sbuf_tensor("lowT", [P, SG * P], F32))
                m.off = k.enter_context(nc.sbuf_tensor("off_sb", [1, SG * P], I32))
                kept = carver(m.at[:, 0:KEPT, :])
                m.src_early, m.srchi = kept("src", [P, T], I32), kept("src_hi_i", [P, T], I32)
                m.src_blocks, m.row_counts = kept("src_blocks", [P, NB, T], F16), kept("row_counts", [P, NB], F32)
                prepare(nc, m, d)
                bucket_ranks(nc, m, d)
                build_counts(nc, m, d)
            appnp(nc, m, d)
            m.y = with_at.enter_context(nc.sbuf_tensor("y_sb", [P, NB, D], F32))
            sage(nc, m, d, 0)
            sage(nc, m, d, 1)
        m.y = sb("y2_sb", [P, NB, D], F32)
        m.srci = sb("srci_sb", [P, T], I32)
        m.brk = sb("brk", [P, T], F32)
        m.mrow = sb("mrow", [D, P], F32)
        m.endi, m.streami = sb("endi", [P, NB], I32), sb("streami", [P, NB], I32)
        m.sel = sb("stream_selector", [P, NP], F32)
        m.xT, m.ytab = sb("xT_sb", [D, NP], F32), sb("ytab", [P, NB, D], F32)
        m.wmr, m.we = sb("w_msg_root", [D, 2, 2 * D], F32), sb("w_edge", [DE, 2, D], F32)
        m.bias = sb("conv_bias", [P, 2, D], F32)
        m.last_stream = sb("last_stream", [P, NB], F32)
        m.nocarry, m.some = sb("nocarry", [P, NB], F32), sb("some", [P, NB], F32)
        weighted_sum(nc, m, d)
        edge_conv(nc, m, d, 0, out)
        edge_conv(nc, m, d, 1, out)


def kernel(x, src, dst, edge_attr_32, edge_weight, L1_gnn_W0, L1_gnn_b0, L1_gnn_W1, L1_gnn_b1, L1_gnn_W2,
           L1_gnn_b2, L3_gnn_W1_msg, L3_gnn_W1_edge, L3_gnn_W1_root, L3_gnn_b1, L3_gnn_W2_msg,
           L3_gnn_W2_edge, L3_gnn_W2_root, L3_gnn_b2):
    import numpy as np
    import concourse.bacc as bacc
    from concourse.bass_utils import run_bass_kernel_spmd

    def padded(a, rows, value=0):
        a = np.asarray(a)
        out = np.full((rows,) + a.shape[1:], value, a.dtype)
        out[:a.shape[0]] = a
        return out

    s, t = padded(src, EP + P, NP - 1), padded(dst, EP + P, NP - 1)
    ea = padded(edge_attr_32, EP).reshape(P, T, DE)
    arrays = {
        "x": padded(x, NP), "src_s": s[:EP].reshape(P, T), "dst_s": t[:EP].reshape(P, T),
        "w_s": padded(edge_weight, EP).reshape(P, T),
        "src_rows": s.reshape(T + 1, P), "dst_rows": t.reshape(T + 1, P),
        "eaT": np.ascontiguousarray(ea.transpose(2, 1, 0)),
        "W0": L1_gnn_W0, "b0": L1_gnn_b0, "W1": L1_gnn_W1, "b1": L1_gnn_b1, "W2": L1_gnn_W2, "b2": L1_gnn_b2,
        "Wm1": L3_gnn_W1_msg, "We1": L3_gnn_W1_edge, "Wr1": L3_gnn_W1_root, "c1": L3_gnn_b1,
        "Wm2": L3_gnn_W2_msg, "We2": L3_gnn_W2_edge, "Wr2": L3_gnn_W2_root, "c2": L3_gnn_b2,
    }
    nc = bacc.Bacc("TRN2", target_bir_lowering=False, num_devices=1)
    feeds, args = {}, []
    for name, a in arrays.items():
        a = np.ascontiguousarray(a)
        feeds["in_" + name] = a
        args.append(nc.dram_tensor("in_" + name, a.shape, mybir.dt.from_np(a.dtype), kind="ExternalInput").ap())
    args.append(nc.dram_tensor("out", (NP, D), F32, kind="ExternalOutput").ap())
    program(nc, *args)
    got = run_bass_kernel_spmd(nc, [feeds], core_ids=[0])
    return got.results[0]["out"][:N]
```
